# Optimizing a Trainium2 kernel written in Bass

```python
import numpy as np
import jax
import jax.numpy as jnp

def _softmax(x, axis=-1):
    return jax.nn.softmax(x, axis=axis)

def _gelu(x):
    return jax.nn.gelu(x, approximate=True)

def _silu(x):
    return jax.nn.silu(x)

def _sigmoid(x):
    return jax.nn.sigmoid(x)

def _layernorm(x, axis=-1, eps=1e-05):
    m = jnp.mean(x, axis=axis, keepdims=True)
    v = jnp.var(x, axis=axis, keepdims=True)
    return (x - m) / jnp.sqrt(v + eps)

def _scatter_add(tgt, idx, src, axis=0):
    return tgt.at[idx].add(src)

def _segment_sum(src, seg, n):
    return jax.ops.segment_sum(src, seg, n)
kernel_name = 'mk_xattn_ffn_d2_seqx_r8_e0d516'

def setup_inputs(seed: int=0):
    np.random.seed(seed)
    _w = jnp.asarray

    def _rec_inputs():
        import jax
        import jax.numpy as jnp
        _rk = jax.random.key(seed)
        x = 0.000341 + 1 * jax.random.normal(jax.random.fold_in(_rk, 1), (16, 128, 256), jnp.float32)
        _lenS = 128 - jax.random.randint(jax.random.fold_in(_rk, 7), (16,), 0, max(1, 128 // 4) + 1, jnp.int32)
        _lenS2 = 128 - jax.random.randint(jax.random.fold_in(_rk, 8), (16,), 0, max(1, 128 // 4) + 1, jnp.int32)
        _ctx_2048P = jax.random.normal(jax.random.fold_in(_rk, 11), (16, 16, 256), jnp.float32)
        _ctx_2048c = jax.random.dirichlet(jax.random.fold_in(_rk, 511), 0.3 * jnp.ones((16,), jnp.float32), (16, 128))
        _ctx_2048t = jnp.einsum('bsk,bkd->bsd', _ctx_2048c, _ctx_2048P)
        _ctx_2048t = _ctx_2048t * jax.lax.rsqrt(jnp.mean(jnp.square(_ctx_2048t)) + 1e-12) * 0.953939
        ctx_2048 = -1.47943e-05 + 1.00017 * (_ctx_2048t + 0.3 * jax.random.normal(jax.random.fold_in(_rk, 611), (16, 128, 256), jnp.float32))
        return (x, ctx_2048)
    x, ctx_2048 = _rec_inputs()

    def _L0_xattn_setup():
        import jax, jax.numpy as jnp
        import numpy as np

        def _wkv(time_decay, time_first, k, v):
            w = -jnp.exp(time_decay)
            u = time_first
            B, T, C = k.shape
            aa = jnp.zeros((B, C), dtype=k.dtype)
            bb = jnp.zeros((B, C), dtype=k.dtype)
            pp = jnp.full((B, C), -1e+38, dtype=k.dtype)

            def step(carry, kv_t):
                aa, bb, pp = carry
                kt, vt = kv_t
                ww = u + kt
                q = jnp.maximum(pp, ww)
                e1 = jnp.exp(pp - q)
                e2 = jnp.exp(ww - q)
                y_t = (e1 * aa + e2 * vt) / (e1 * bb + e2)
                ww2 = pp + w
                q2 = jnp.maximum(ww2, kt)
                e1b = jnp.exp(ww2 - q2)
                e2b = jnp.exp(kt - q2)
                new_carry = (e1b * aa + e2b * vt, e1b * bb + e2b, q2)
                return (new_carry, y_t)
            ks = jnp.transpose(k, (1, 0, 2))
            vs = jnp.transpose(v, (1, 0, 2))
            _, ys = jax.lax.scan(step, (aa, bb, pp), (ks, vs))
            return jnp.transpose(ys, (1, 0, 2))
        key = jax.random.key(seed)
        k1, k2, k3, k4 = jax.random.split(key, 4)
        B, T, C = (8, 128, 256)
        return {'batch_size': B, 'seq_len': T, 'embedding_dim': C, 'time_decay': jax.random.normal(k1, (C,), dtype=jnp.float32), 'time_first': jax.random.normal(k2, (C,), dtype=jnp.float32), 'k': jax.random.normal(k3, (B, T, C), dtype=jnp.float32), 'v': jax.random.normal(k4, (B, T, C), dtype=jnp.float32)}
    _L0_xattn_all = _L0_xattn_setup()
    _L0_xattn_in = {k: v for k, v in _L0_xattn_all.items() if k in ('time_decay', 'time_first')}
    del _L0_xattn_all

    def _L0_ffn_setup():
        import jax, jax.numpy as jnp
        import numpy as np
        B, T, D = (2, 128, 256)
        H, K, DK = (4, 8, 64)
        E = 2048
        NK = 128
        key = jax.random.key(seed)
        k1, k2, k3, k4, k5 = jax.random.split(key, 5)
        x = jax.random.normal(k1, (B, T, D), dtype=jnp.float32)
        Wq = jax.random.normal(k2, (D, 2 * H * DK), dtype=jnp.float32) * 0.02
        keys = jax.random.normal(k3, (H, NK, 2, DK), dtype=jnp.float32) * 0.02
        e_down = jax.random.normal(k4, (E, D), dtype=jnp.float32) * 0.01
        e_up = jax.random.normal(k5, (E, D), dtype=jnp.float32) * 0.01
        return {'x': x, 'Wq': Wq, 'keys': keys, 'e_down': e_down, 'e_up': e_up}
    _L0_ffn_all = _L0_ffn_setup()
    _L0_ffn_in = {k: v for k, v in _L0_ffn_all.items() if k in ('Wq', 'keys', 'e_down', 'e_up')}
    del _L0_ffn_all

    def _L1_xattn_setup():
        import jax, jax.numpy as jnp
        import numpy as np
        D_MODEL = 256
        NUM_HEADS = 16
        HEAD_DIM = D_MODEL // NUM_HEADS

        def _fq_sym(x, axis):
            s = jnp.max(jnp.abs(x), axis=axis, keepdims=True) / 127.0
            s = jnp.maximum(s, 1e-08)
            q = jnp.clip(jnp.round(x / s), -127.0, 127.0) * s
            return x + jax.lax.stop_gradient(q - x)

        def _fq_unsigned(x, axis):
            s = jnp.max(x, axis=axis, keepdims=True) / 255.0
            s = jnp.maximum(s, 1e-08)
            q = jnp.clip(jnp.round(x / s), 0.0, 255.0) * s
            return x + jax.lax.stop_gradient(q - x)
        key = jax.random.key(seed)
        ks = jax.random.split(key, 8)
        B, N, M, C = (2, 256, 64, D_MODEL)
        return {'x': jax.random.normal(ks[0], (B, N, C), jnp.float32), 'cond': jax.random.normal(ks[1], (B, M, C), jnp.float32), 'Wq': jax.random.normal(ks[2], (C, C), jnp.float32) * 0.02, 'bq': jnp.zeros((C,), jnp.float32), 'Wkv': jax.random.normal(ks[3], (C, 2 * C), jnp.float32) * 0.02, 'bkv': jnp.zeros((2 * C,), jnp.float32), 'Wp': jax.random.normal(ks[4], (C, C), jnp.float32) * 0.02, 'bp': jnp.zeros((C,), jnp.float32)}
    _L1_xattn_all = _L1_xattn_setup()
    _L1_xattn_in = {k: v for k, v in _L1_xattn_all.items() if k in ('Wq', 'bq', 'Wkv', 'bkv', 'Wp', 'bp')}
    del _L1_xattn_all

    def _L1_ffn_setup():
        import jax, jax.numpy as jnp
        import numpy as np
        TOP_K = 4
        key = jax.random.key(seed)
        ks = jax.random.split(key, 8)
        B, S, H = (1, 128, 256)
        E, I = (60, 176)
        I_SH = 704
        s = 0.02
        return {'hidden_states': jax.random.normal(ks[0], (B, S, H), jnp.float32), 'gate_w': jax.random.normal(ks[1], (E, H), jnp.float32) * s, 'shared_gate_w': jax.random.normal(ks[2], (1, H), jnp.float32) * s, 'w13': jax.random.normal(ks[3], (E, 2 * I, H), jnp.float32) * s, 'w2': jax.random.normal(ks[4], (E, H, I), jnp.float32) * s, 'se_gate_up_w': jax.random.normal(ks[5], (2 * I_SH, H), jnp.float32) * s, 'se_down_w': jax.random.normal(ks[6], (H, I_SH), jnp.float32) * s}
    _L1_ffn_all = _L1_ffn_setup()
    _L1_ffn_in = {k: v for k, v in _L1_ffn_all.items() if k in ('gate_w', 'shared_gate_w', 'w13', 'w2', 'se_gate_up_w', 'se_down_w')}
    del _L1_ffn_all
    return {'x': x, 'ctx_2048': ctx_2048, 'L0_xattn_time_decay': _L0_xattn_in['time_decay'], 'L0_xattn_time_first': _L0_xattn_in['time_first'], 'L0_ffn_Wq': _L0_ffn_in['Wq'], 'L0_ffn_keys': _L0_ffn_in['keys'], 'L0_ffn_e_down': _L0_ffn_in['e_down'], 'L0_ffn_e_up': _L0_ffn_in['e_up'], 'L1_xattn_Wq': _L1_xattn_in['Wq'], 'L1_xattn_bq': _L1_xattn_in['bq'], 'L1_xattn_Wkv': _L1_xattn_in['Wkv'], 'L1_xattn_bkv': _L1_xattn_in['bkv'], 'L1_xattn_Wp': _L1_xattn_in['Wp'], 'L1_xattn_bp': _L1_xattn_in['bp'], 'L1_ffn_gate_w': _L1_ffn_in['gate_w'], 'L1_ffn_shared_gate_w': _L1_ffn_in['shared_gate_w'], 'L1_ffn_w13': _L1_ffn_in['w13'], 'L1_ffn_w2': _L1_ffn_in['w2'], 'L1_ffn_se_gate_up_w': _L1_ffn_in['se_gate_up_w'], 'L1_ffn_se_down_w': _L1_ffn_in['se_down_w']}

def reference(x, ctx_2048, L0_xattn_time_decay, L0_xattn_time_first, L0_ffn_Wq, L0_ffn_keys, L0_ffn_e_down, L0_ffn_e_up, L1_xattn_Wq, L1_xattn_bq, L1_xattn_Wkv, L1_xattn_bkv, L1_xattn_Wp, L1_xattn_bp, L1_ffn_gate_w, L1_ffn_shared_gate_w, L1_ffn_w13, L1_ffn_w2, L1_ffn_se_gate_up_w, L1_ffn_se_down_w):
    import jax
    import jax.numpy as jnp

    def _L0_xattn_ref(batch_size, seq_len, embedding_dim, time_decay, time_first, k, v):
        import jax, jax.numpy as jnp
        import numpy as np

        def _wkv(time_decay, time_first, k, v):
            w = -jnp.exp(time_decay)
            u = time_first
            B, T, C = k.shape
            aa = jnp.zeros((B, C), dtype=k.dtype)
            bb = jnp.zeros((B, C), dtype=k.dtype)
            pp = jnp.full((B, C), -1e+38, dtype=k.dtype)

            def step(carry, kv_t):
                aa, bb, pp = carry
                kt, vt = kv_t
                ww = u + kt
                q = jnp.maximum(pp, ww)
                e1 = jnp.exp(pp - q)
                e2 = jnp.exp(ww - q)
                y_t = (e1 * aa + e2 * vt) / (e1 * bb + e2)
                ww2 = pp + w
                q2 = jnp.maximum(ww2, kt)
                e1b = jnp.exp(ww2 - q2)
                e2b = jnp.exp(kt - q2)
                new_carry = (e1b * aa + e2b * vt, e1b * bb + e2b, q2)
                return (new_carry, y_t)
            ks = jnp.transpose(k, (1, 0, 2))
            vs = jnp.transpose(v, (1, 0, 2))
            _, ys = jax.lax.scan(step, (aa, bb, pp), (ks, vs))
            return jnp.transpose(ys, (1, 0, 2))
        assert seq_len <= 128
        return _wkv(time_decay, time_first, k, v)

    def _L0_ffn_ref(x, Wq, keys, e_down, e_up):
        import jax, jax.numpy as jnp
        import numpy as np
        B, T, D = (2, 128, 256)
        H, K, DK = (4, 8, 64)
        E = 2048
        NK = 128
        b, t, d = x.shape
        q = (x @ Wq).reshape(b, t, H, 2, DK)
        q1, q2 = (q[..., 0, :], q[..., 1, :])
        sim1 = jnp.einsum('bthd,hkd->bthk', q1, keys[:, :, 0, :])
        sim2 = jnp.einsum('bthd,hkd->bthk', q2, keys[:, :, 1, :])
        s1, i1 = jax.lax.top_k(sim1, K)
        s2, i2 = jax.lax.top_k(sim2, K)
        all_scores = (s1[..., :, None] + s2[..., None, :]).reshape(b, t, H, K * K)
        all_indices = (i1[..., :, None] * NK + i2[..., None, :]).reshape(b, t, H, K * K)
        final_scores, pk_idx = jax.lax.top_k(all_scores, K)
        final_indices = jnp.take_along_axis(all_indices, pk_idx, axis=-1)
        w_down = e_down[final_indices]
        w_up = e_up[final_indices]
        hidden = jnp.einsum('btd,bthkd->bthk', x, w_down)
        hidden = jax.nn.silu(hidden)
        hidden = hidden * jax.nn.relu(final_scores)
        out = jnp.einsum('bthk,bthkd->btd', hidden, w_up)
        return out

    def _L1_xattn_ref(x, cond, Wq, bq, Wkv, bkv, Wp, bp):
        import jax, jax.numpy as jnp
        import numpy as np
        D_MODEL = 256
        NUM_HEADS = 16
        HEAD_DIM = D_MODEL // NUM_HEADS

        def _fq_sym(x, axis):
            s = jnp.max(jnp.abs(x), axis=axis, keepdims=True) / 127.0
            s = jnp.maximum(s, 1e-08)
            q = jnp.clip(jnp.round(x / s), -127.0, 127.0) * s
            return x + jax.lax.stop_gradient(q - x)

        def _fq_unsigned(x, axis):
            s = jnp.max(x, axis=axis, keepdims=True) / 255.0
            s = jnp.maximum(s, 1e-08)
            q = jnp.clip(jnp.round(x / s), 0.0, 255.0) * s
            return x + jax.lax.stop_gradient(q - x)
        B, N, C = x.shape
        H, hd = (NUM_HEADS, HEAD_DIM)
        q = (x @ Wq + bq).reshape(1, B * N, H, hd)
        kv = (cond @ Wkv + bkv).reshape(1, -1, 2, H, hd)
        k, v = (kv[:, :, 0], kv[:, :, 1])
        scale = 1.0 / np.sqrt(hd).astype(np.float32)
        q = jnp.transpose(q * scale, (0, 2, 1, 3))
        k = jnp.transpose(k, (0, 2, 1, 3))
        v = jnp.transpose(v, (0, 2, 1, 3))
        q = _fq_sym(q, axis=-1)
        k = _fq_sym(k, axis=-1)
        v = _fq_sym(v, axis=2)
        attn = jnp.einsum('bhqd,bhkd->bhqk', q, k)
        attn = jax.nn.softmax(attn.astype(jnp.float32), axis=-1)
        attn = _fq_unsigned(attn, axis=-1)
        out = jnp.einsum('bhqk,bhkd->bhqd', attn, v)
        out = jnp.transpose(out, (0, 2, 1, 3)).reshape(B, N, C)
        return out @ Wp + bp

    def _L1_ffn_ref(hidden_states, gate_w, shared_gate_w, w13, w2, se_gate_up_w, se_down_w):
        import jax, jax.numpy as jnp
        import numpy as np
        TOP_K = 4
        orig_shape = hidden_states.shape
        E, H = gate_w.shape
        I = w2.shape[2]
        x = hidden_states.reshape(-1, H)
        M = x.shape[0]
        gu = x @ se_gate_up_w.T
        I_sh = se_down_w.shape[1]
        shared = jax.nn.silu(gu[:, :I_sh]) * gu[:, I_sh:] @ se_down_w.T
        shared = shared * jax.nn.sigmoid(x @ shared_gate_w.T)
        logits = x @ gate_w.T
        probs = jax.nn.softmax(logits.astype(jnp.float32), axis=-1)
        weights, sel = jax.lax.top_k(probs, TOP_K)
        cw = jnp.zeros((M, E), jnp.float32).at[jnp.arange(M)[:, None], sel].add(weights)

        def step(acc, ews):
            w13_e, w2_e, cw_e = ews
            gu_e = x @ w13_e.T
            h = jax.nn.silu(gu_e[:, :I]) * gu_e[:, I:]
            return (acc + cw_e[:, None] * (h @ w2_e.T), None)
        sparse, _ = jax.lax.scan(step, jnp.zeros((M, H), jnp.float32), (w13, w2, cw.T))
        return (shared + sparse).reshape(orig_shape)
    x = x + _L0_xattn_ref(16, 128, 256, L0_xattn_time_decay, L0_xattn_time_first, _layernorm(x, axis=-1), ctx_2048)
    x = x + _L0_ffn_ref(_layernorm(x, axis=-1), L0_ffn_Wq, L0_ffn_keys, L0_ffn_e_down, L0_ffn_e_up)
    x = x + _L1_xattn_ref(_layernorm(x, axis=-1), ctx_2048, L1_xattn_Wq, L1_xattn_bq, L1_xattn_Wkv, L1_xattn_bkv, L1_xattn_Wp, L1_xattn_bp)
    x = x + _L1_ffn_ref(_layernorm(x, axis=-1), L1_ffn_gate_w, L1_ffn_shared_gate_w, L1_ffn_w13, L1_ffn_w2, L1_ffn_se_gate_up_w, L1_ffn_se_down_w)
    return x

_drawn_inputs = setup_inputs


def setup_inputs(seed=0):
    import zlib

    import numpy as np

    out = dict(_drawn_inputs(seed))
    spreads = {'L1_xattn_bq': (0.0, 2.0), 'L1_xattn_bkv': (0.0, 2.0), 'L1_xattn_bp': (0.0, 0.8)}
    factors = {'L0_ffn_Wq': 8.0,
     'L0_ffn_keys': 8.0,
     'L0_ffn_e_down': 8.0,
     'L0_ffn_e_up': 8.0,
     'L1_xattn_Wq': 8.0,
     'L1_xattn_Wkv': 5.461,
     'L1_ffn_gate_w': 8.0,
     'L1_ffn_shared_gate_w': 21.647,
     'L1_ffn_w13': 8.0,
     'L1_ffn_w2': 8.0,
     'L1_ffn_se_gate_up_w': 5.168,
     'L1_ffn_se_down_w': 5.153}
    for name, (base, spread) in spreads.items():
        noise = np.random.default_rng([zlib.crc32(name.encode()), seed]).standard_normal(out[name].shape)
        drawn = base * np.exp(spread * noise) if base else spread * noise
        out[name] = jnp.asarray(drawn.astype(out[name].dtype))
    for name, factor in factors.items():
        out[name] = (out[name] * factor).astype(out[name].dtype)
    return out
```

```python
import concourse.bass as bass
from concourse import mybir
from contextlib import ExitStack

F32 = mybir.dt.float32
BF16 = mybir.dt.bfloat16
U32 = mybir.dt.uint32
ALU = mybir.AluOpType
ACT = mybir.ActivationFunctionType
AX = mybir.AxisListType

P = 128
BATCH, SEQ, DIM = 16, 128, 256
TILES = BATCH * SEQ // P
TOKENS = TILES * P
CH = DIM // P
EPS = 1e-5
ROUND = 12582912.0
BLK = 512
BLKS = TOKENS // BLK

PK_HEADS, PK_KEYS, PK_TOP, PK_DK = 4, 128, 8, 64
PK_EXPERTS = 2048
PK_ROWS = PK_EXPERTS // P

HEADS, HD = 16, 16
LN255 = 5.541263545158426

MOE, INTER, SH_INTER, MOE_TOP = 60, 176, 704, 4
SHARED = SH_INTER // INTER
EXPERTS = MOE + SHARED
REST = INTER - P
UPCOLS = 2 * P + 64 + REST


def counter(engine, semaphore):
    count = [0]

    def link(instruction):
        instruction.then_inc(semaphore, 1)
        count[0] += 1
        engine.wait_ge(semaphore, count[0])

    return link


def norm_statistics(nc, dve, link, resid, stats, mv, work, var_ready, std_ready):
    for i in range(TILES):
        last = nc.vector.bn_stats(stats[:, i, :], resid[:, i, :])
    link(last)
    for i in range(TILES):
        last = nc.vector.bn_aggr(mv[:, i, :], stats[:, i, :])
    link(last)
    nc.vector.tensor_scalar(work[:, 0, :], mv[:, :, 1], EPS, None, ALU.add).then_inc(var_ready, 1)
    dve.wait_ge(std_ready, 1)
    link(nc.vector.reciprocal(work[:, 2, :], work[:, 1, :]))
    link(nc.vector.tensor_tensor(work[:, 3, :], work[:, 2, :], work[:, 2, :], ALU.mult))
    link(nc.vector.tensor_tensor(work[:, 3, :], work[:, 3, :], work[:, 0, :], ALU.mult))
    link(nc.vector.tensor_scalar(work[:, 3, :], work[:, 3, :], -0.5, 1.5, ALU.mult, ALU.add))
    link(nc.vector.tensor_tensor(work[:, 2, :], work[:, 2, :], work[:, 3, :], ALU.mult))


def norm_std(nc, act, work, var_ready, std_ready):
    act.wait_ge(var_ready, 1)
    nc.scalar.activation(work[:, 1, :], work[:, 0, :], ACT.Sqrt).then_inc(std_ready, 1)


def norm_tile(nc, dve, i, resid, xn, mv, work, normed, transposed):
    if i >= 4:
        dve.wait_ge(transposed, i - 3)
    nc.vector.tensor_scalar(xn[:, i % 4, :], resid[:, i, :], mv[:, i, 0:1], work[:, 2, i:i + 1],
                            ALU.subtract, ALU.mult).then_inc(normed, 1)


def transpose_tile(nc, pe, i, xn, psT, ident, normed, transposed, evacuated):
    pe.wait_ge(normed, i + 1)
    if i >= 2:
        pe.wait_ge(evacuated, i - 1)
    for c in range(CH):
        last = nc.tensor.transpose(psT[:, i % 2, c * P:(c + 1) * P], xn[:, i % 4, c * P:(c + 1) * P], ident[:, :])
    last.then_inc(transposed, 1)


def stage_recurrence(nc, ctx, sem, sb, ps, g):
    resid, ctxT, ident = g["resid"], g["ctxT"], g["ident"]
    stats, mv, work, xn = g["stats"], g["mv"], g["work"], g["xn"]
    par = sb("wkv_par", [P, 8, CH])
    ek = sb("ek", [P, CH, TOKENS])
    ev = sb("ev", [P, CH, TOKENS])
    decay = sb("decay", [P, TOKENS])
    acc_v = sb("acc_v", [P, TOKENS])
    acc_k = sb("acc_k", [P, TOKENS])
    cur_v = sb("cur_v", [P, TOKENS])
    cur_k = sb("cur_k", [P, TOKENS])
    yT = sb("yT", [P, CH, TOKENS])
    psT = ps("a_psT", [P, 2, BLK])
    psY = ps("a_psY", [P, 2, BLK])
    var_ready, std_ready, normed = sem("a_var"), sem("a_std"), sem("a_normed")
    transposed, evacuated = sem("a_transposed"), sem("a_evacuated")
    chain, achain = sem("a_chain"), sem("a_achain")
    m_ready, par_ready, decay_ready, cur_ready = sem("a_m"), sem("a_par"), sem("a_decay"), sem("a_cur")
    ev_ready, scans_done, num_done = sem("a_ev"), sem("a_scans"), sem("a_num")
    y_ready, y_back, pool_ms = sem("a_y"), sem("a_yback"), sem("a_pool")
    y_added, par_in = sem("a_yadded"), sem("a_parin")

    with nc.Block() as block:
        @block.sync
        def _(sp):
            sp.dma_start(resid[:, :, :], g["x"].rearrange("(i p) d -> p i d", p=P)).then_inc(g["x_in"], 16)
            sp.dma_start(par[:, 0, :], g["td"]).then_inc(par_in, 16)
            sp.dma_start(par[:, 1, :], g["tf"]).then_inc(par_in, 16)
            sp.dma_start(ctxT[:, :, :], g["ctxT_d"].rearrange("(c p) t -> p c t", p=P)).then_inc(g["ctx_in"], 16)

        @block.gpsimd
        def _(pool):
            nc.gpsimd.memset(ident[:, :], 0.0).then_inc(pool_ms, 1)
            pool.wait_ge(pool_ms, 1)
            nc.gpsimd.affine_select(out=ident[:, :], in_=ident[:, :], compare_op=ALU.not_equal, fill=1.0,
                                    base=0, pattern=[[-1, P]], channel_multiplier=1).then_inc(g["ident_ready"], 1)
            pool.wait_ge(par_ready, 1)
            for c in range(CH):
                if c:
                    pool.wait_ge(scans_done, 2 * c)
                nc.gpsimd.memset(decay[:, :], 1.0).then_inc(pool_ms, 1)
                pool.wait_ge(pool_ms, 3 * c + 2)
                nc.gpsimd.tensor_scalar(decay[:, :], decay[:, :], par[:, 5, c:c + 1], None, ALU.mult).then_inc(pool_ms, 1)
                pool.wait_ge(pool_ms, 3 * c + 3)
                nc.gpsimd.memset(decay[:, :].rearrange("p (b t) -> p b t", t=SEQ)[:, :, 0], 0.0).then_inc(pool_ms, 1)
                pool.wait_ge(pool_ms, 3 * c + 4)
                pool.sem_inc(decay_ready, 1)
                pool.wait_ge(ev_ready, c + 1)
                if c:
                    pool.wait_ge(num_done, c)
                nc.gpsimd.tensor_scalar(cur_v[:, :], ev[:, c, :], par[:, 7, c:c + 1], None, ALU.mult)
                nc.gpsimd.tensor_scalar(cur_k[:, :], ek[:, c, :], par[:, 7, c:c + 1], None, ALU.mult).then_inc(cur_ready, 1)

        @block.scalar
        def _(act):
            norm_std(nc, act, work, var_ready, std_ready)
            act.wait_ge(par_in, 32)
            nc.scalar.activation(par[:, 4, :], par[:, 0, :], ACT.Exp).then_inc(achain, 1)
            act.wait_ge(achain, 1)
            nc.scalar.activation(par[:, 5, :], par[:, 4, :], ACT.Exp, scale=-1.0)
            act.wait_ge(m_ready, 1)
            nc.scalar.activation(par[:, 6, :], par[:, 2, :], ACT.Exp, scale=-1.0)
            nc.scalar.activation(par[:, 7, :], par[:, 3, :], ACT.Exp).then_inc(par_ready, 1)
            for i in range(TILES):
                act.wait_ge(transposed, i + 1)
                nc.scalar.activation(ek[:, :, i * P:(i + 1) * P],
                                     psT[:, i % 2, 0:DIM].rearrange("p (c t) -> p c t", c=CH),
                                     ACT.Exp).then_inc(evacuated, 1)

        @block.vector
        def _(dve):
            link = counter(dve, chain)
            dve.wait_ge(par_in, 32)
            link(nc.vector.tensor_scalar(par[:, 2, :], par[:, 1, :], 0.0, None, ALU.max))
            nc.vector.tensor_tensor(par[:, 3, :], par[:, 1, :], par[:, 2, :], ALU.subtract).then_inc(m_ready, 1)
            dve.wait_ge(g["x_in"], 16)
            norm_statistics(nc, dve, link, resid, stats, mv, work, var_ready, std_ready)
            for i in range(TILES):
                norm_tile(nc, dve, i, resid, xn, mv, work, normed, transposed)
            dve.wait_ge(g["ctx_in"], 16)
            dve.wait_ge(evacuated, TILES)
            for c in range(CH):
                nc.vector.tensor_tensor(ev[:, c, :], ek[:, c, :], ctxT[:, c, :], ALU.mult).then_inc(ev_ready, 1)
            for c in range(CH):
                dve.wait_ge(ev_ready, c + 1)
                dve.wait_ge(decay_ready, c + 1)
                nc.vector.tensor_tensor_scan(acc_v[:, :], decay[:, :], ev[:, c, :], 0.0, ALU.mult, ALU.add).then_inc(scans_done, 1)
                nc.vector.tensor_tensor_scan(acc_k[:, :], decay[:, :], ek[:, c, :], 0.0, ALU.mult, ALU.add).then_inc(scans_done, 1)
                dve.wait_ge(scans_done, 2 * c + 2)
                dve.wait_ge(cur_ready, c + 1)
                for cur, acc in ((cur_v, acc_v), (cur_k, acc_k)):
                    later = cur[:, :].rearrange("p (b t) -> p b t", t=SEQ)[:, :, 1:SEQ]
                    earlier = acc[:, :].rearrange("p (b t) -> p b t", t=SEQ)[:, :, 0:SEQ - 1]
                    last = nc.vector.scalar_tensor_tensor(later, earlier, par[:, 6, c:c + 1], later, ALU.mult, ALU.add)
                link(last)
                link(nc.vector.reciprocal(cur_k[:, :], cur_k[:, :]))
                link(nc.vector.tensor_tensor(yT[:, c, :], cur_v[:, :], cur_k[:, :], ALU.mult))
                nc.vector.tensor_copy(yT[:, c, :].rearrange("p (b t) -> p b t", t=SEQ)[:, :, 0],
                                      ctxT[:, c, :].rearrange("p (b t) -> p b t", t=SEQ)[:, :, 0]).then_inc(num_done, 1)
            for i in range(TILES):
                dve.wait_ge(y_back, i + 1)
                nc.vector.tensor_tensor(resid[:, i, :], psY[:, i % 2, 0:DIM], resid[:, i, :], ALU.add).then_inc(y_added, 1)

        @block.tensor
        def _(pe):
            pe.wait_ge(g["ident_ready"], 1)
            for i in range(TILES):
                transpose_tile(nc, pe, i, xn, psT, ident, normed, transposed, evacuated)
            pe.wait_ge(num_done, CH)
            for i in range(TILES):
                if i >= 2:
                    pe.wait_ge(y_added, i - 1)
                for c in range(CH):
                    last = nc.tensor.transpose(psY[:, i % 2, c * P:(c + 1) * P], yT[:, c, i * P:(i + 1) * P], ident[:, :])
                last.then_inc(y_back, 1)


def stage_product_keys(nc, ctx, sem, sb, ps, g):
    resid, ident, xn = g["resid"], g["ident"], g["xn"]
    stats, mv, work = g["stats"], g["mv"], g["work"]
    G8 = 2 * PK_HEADS
    PICKS = PK_HEADS * PK_TOP
    TPG = P // PICKS
    GROUPS = TOKENS // TPG
    GPT = P // TPG
    HALF = GPT // 2
    xnT = g["xnT"]
    nsel = TILES * PK_HEADS
    downT = sb("pk_downT", [P, CH, PK_EXPERTS])
    up = sb("pk_up", [P, PK_ROWS, DIM])
    iota128 = sb("pk_iota128", [P, P])
    rowtab = sb("pk_rowtab", [P, PK_ROWS, TPG])
    packed = sb("pk_packed", [P, 3, TILES, PICKS])
    choice = ctx.enter_context(ExitStack())

    def first(name, shape, dtype=F32):
        return choice.enter_context(nc.sbuf_tensor(name, shape, dtype))

    wqT = first("pk_wqT", [PK_DK, G8, DIM])
    keysT = first("pk_keysT", [PK_DK, G8, PK_KEYS])
    mix = first("pk_mix", [P, CH, G8 * PK_KEYS])
    top_v = first("pk_top_v", [P, 2, G8, PK_TOP])
    top_i = first("pk_top_i", [P, TILES, G8, PK_TOP], U32)
    sums = first("pk_sums", [P, PK_HEADS, PK_TOP, PK_TOP])
    best = first("pk_best", [P, TILES, PK_HEADS, PK_TOP])
    best_i = first("pk_best_i", [P, TILES, PK_HEADS, PK_TOP], U32)
    iota8 = first("pk_iota8", [P, PK_TOP])
    top_f = first("pk_top_f", [P, nsel, 2, PK_TOP])
    pos_u = first("pk_pos_u", [P, 2, nsel * PK_TOP], U32)
    pos_f = first("pk_pos_f", [P, 2, nsel, PK_TOP])
    picked = first("pk_picked", [P, 2, nsel * PK_TOP])
    onehot = first("pk_onehot", [P, nsel // 2 * PK_TOP * PK_TOP])
    scratch = nc.dram_tensor("pk_scratch", (3, TOKENS, PICKS), F32, kind="Internal").ap()

    s = {n: sem("b_" + n) for n in (
        "var std normed transposed evacuated chain w_in wide_in mix_ready mix_copied scored scores_used "
        "packed_ready packed_out rows_in rows_tr groups_ready iotas col_ready row_ready spread down_done act_ready hid_ready "
        "hid_used out_done added pool_chain act_used").split()}
    sc = ctx.enter_context(ExitStack())
    psT = sc.enter_context(nc.psum_tensor("b_psT", [P, 2, BLK], F32))
    psS = sc.enter_context(nc.psum_tensor("b_psS", [P, 2, G8 * PK_KEYS], F32))
    with nc.Block() as block:
        @block.sync
        def _(sp):
            sp.dma_start(wqT[:, :, :], g["pk_wqT_d"].rearrange("(q p) c -> p q c", p=PK_DK)).then_inc(s["w_in"], 16)
            sp.dma_start(keysT[:, :, :], g["pk_keysT_d"].rearrange("(q p) k -> p q k", p=PK_DK)).then_inc(s["w_in"], 16)
            sp.dma_start(downT[:, :, :], g["pk_downT_d"].rearrange("(c p) e -> p c e", p=P)).then_inc(s["wide_in"], 16)
            sp.dma_start(up[:, :, :], g["pk_up_d"].rearrange("(r p) c -> p r c", p=P)).then_inc(s["wide_in"], 16)

        @block.gpsimd
        def _(pool):
            for table, pattern in ((iota8, [[1, PK_TOP]]), (iota128, [[1, P]])):
                nc.gpsimd.iota(table[:, :], pattern, base=0, channel_multiplier=0,
                               allow_small_or_imprecise_dtypes=True).then_inc(s["iotas"], 1)
            nc.gpsimd.iota(rowtab[:, :, :], [[1, PK_ROWS], [0, TPG]], base=0, channel_multiplier=0,
                           allow_small_or_imprecise_dtypes=True).then_inc(s["pool_chain"], 1)
            pool.wait_ge(s["pool_chain"], 1)
            nc.gpsimd.affine_select(out=rowtab[:, :, :], in_=rowtab[:, :, :], compare_op=ALU.is_ge, fill=-1.0,
                                    base=0, pattern=[[0, PK_ROWS], [-PICKS, TPG]], channel_multiplier=1).then_inc(s["pool_chain"], 1)
            pool.wait_ge(s["pool_chain"], 2)
            nc.gpsimd.affine_select(out=rowtab[:, :, :], in_=rowtab[:, :, :], compare_op=ALU.is_ge, fill=-1.0,
                                    base=PICKS - 1, pattern=[[0, PK_ROWS], [PICKS, TPG]], channel_multiplier=-1).then_inc(s["iotas"], 1)

        @block.scalar
        def _(act):
            norm_std(nc, act, work, s["var"], s["std"])
            act.wait_ge(s["mix_ready"], 1)
            for c in range(CH):
                last = nc.scalar.activation(mix[:, c, :], psS[:, c, :], ACT.Copy)
            last.then_inc(s["mix_copied"], 1)
            for i in range(TILES):
                act.wait_ge(s["transposed"], i + 1)
                nc.scalar.activation(xnT[:, :, i * P:(i + 1) * P],
                                     psT[:, i % 2, 0:DIM].rearrange("p (c t) -> p c t", c=CH),
                                     ACT.Copy).then_inc(s["evacuated"], 1)

        @block.vector
        def _(dve):
            link = counter(dve, s["chain"])
            norm_statistics(nc, dve, link, resid, stats, mv, work, s["var"], s["std"])
            for i in range(2):
                norm_tile(nc, dve, i, resid, xn, mv, work, s["normed"], s["transposed"])
            for i in range(TILES):
                if i + 2 < TILES:
                    norm_tile(nc, dve, i + 2, resid, xn, mv, work, s["normed"], s["transposed"])
                dve.wait_ge(s["scored"], i + 1)
                part = psS[:, i % 2, :].rearrange("p (g k) -> p g k", g=G8)
                tv = top_v[:, i % 2, :, :]
                for q in range(G8):
                    last = nc.vector.max(tv[:, q, :], part[:, q, :])
                link(last)
                for q in range(G8):
                    last = nc.vector.max_index(top_i[:, i, q, :], tv[:, q, :], part[:, q, :])
                last.then_inc(s["scores_used"], 1)
                pair = tv.rearrange("p (h z) k -> p h z k", z=2)
                link(nc.vector.tensor_tensor(sums[:, :, :, :],
                                             pair[:, :, 0, :].unsqueeze(3).to_broadcast([P, PK_HEADS, PK_TOP, PK_TOP]),
                                             pair[:, :, 1, :].unsqueeze(2).to_broadcast([P, PK_HEADS, PK_TOP, PK_TOP]), ALU.add))
                flat = sums[:, :, :, :].rearrange("p h a b -> p h (a b)")
                for h in range(PK_HEADS):
                    last = nc.vector.max(best[:, i, h, :], flat[:, h, :])
                link(last)
                for h in range(PK_HEADS):
                    last = nc.vector.max_index(best_i[:, i, h, :], best[:, i, h, :], flat[:, h, :])
                link(last)
            bi = best_i[:, :, :, :].rearrange("p i h k -> p (i h k)")
            link(nc.vector.tensor_scalar(pos_u[:, 0, :], bi, 3, None, ALU.logical_shift_right))
            link(nc.vector.tensor_scalar(pos_u[:, 1, :], bi, PK_TOP - 1, None, ALU.bitwise_and))
            link(nc.vector.tensor_copy(pos_f[:, :, :, :].rearrange("p z n k -> p (z n k)"), pos_u[:, :, :].rearrange("p z n -> p (z n)")))
            link(nc.vector.tensor_copy(top_f[:, :, :, :].rearrange("p n z k -> p (n z k)"),
                                       top_i[:, :, :, :].rearrange("p i g k -> p (i g k)")))
            dve.wait_ge(s["iotas"], 3)
            hot = onehot[:, :].rearrange("p (n k a) -> p n k a", k=PK_TOP, a=PK_TOP)
            for z in range(2):
                for q in range(nsel // 32):
                    n0 = 32 * q
                    shape = [P, 32, PK_TOP, PK_TOP]
                    flat3 = [P, 32 * PK_TOP, PK_TOP]
                    hotf = hot.rearrange("p n k a -> p (n k) a")
                    link(nc.vector.tensor_tensor(hotf, pos_f[:, z, n0:n0 + 32, :].rearrange("p n k -> p (n k)").unsqueeze(2).to_broadcast(flat3),
                                                 iota8[:, :].unsqueeze(1).to_broadcast(flat3), ALU.is_equal))
                    link(nc.vector.tensor_tensor(hot, hot, top_f[:, n0:n0 + 32, z, :].unsqueeze(2).to_broadcast(shape), ALU.mult))
                    link(nc.vector.reduce_sum(picked[:, z, n0 * PK_TOP:(n0 + 32) * PK_TOP].unsqueeze(2), hotf, AX.X))
            link(nc.vector.scalar_tensor_tensor(picked[:, 0, :], picked[:, 0, :], float(PK_KEYS), picked[:, 1, :], ALU.mult, ALU.add))
            link(nc.vector.tensor_scalar(pos_u[:, 0, :], picked[:, 0, :], float(PK_EXPERTS - 1), None, ALU.min))
            link(nc.vector.tensor_scalar(pos_u[:, 1, :], pos_u[:, 0, :], 7, None, ALU.logical_shift_right))
            link(nc.vector.tensor_copy(packed[:, 0, :, :].rearrange("p i k -> p (i k)"), pos_u[:, 1, :]))
            link(nc.vector.tensor_scalar(pos_u[:, 1, :], pos_u[:, 0, :], P - 1, None, ALU.bitwise_and))
            link(nc.vector.tensor_copy(packed[:, 1, :, :].rearrange("p i k -> p (i k)"), pos_u[:, 1, :]))
            nc.vector.tensor_scalar(packed[:, 2, :, :].rearrange("p i k -> p (i k)"),
                                    best[:, :, :, :].rearrange("p i h k -> p (i h k)"), 0.0, None, ALU.max).then_inc(s["packed_ready"], 1)

        @block.tensor
        def _(pe):
            pe.wait_ge(s["w_in"], 32)
            for c in range(CH):
                for q in range(G8):
                    last = nc.tensor.matmul(psS[:, c, q * PK_KEYS:(q + 1) * PK_KEYS], wqT[:, q, c * P:(c + 1) * P],
                                            keysT[:, q, :], start=True, stop=True)
            last.then_inc(s["mix_ready"], 1)
            for i in range(TILES + 1):
                if i < TILES:
                    transpose_tile(nc, pe, i, xn, psT, ident, s["normed"], s["transposed"], s["evacuated"])
                if i == 0:
                    pe.wait_ge(s["mix_copied"], 1)
                    continue
                j = i - 1
                pe.wait_ge(s["evacuated"], j + 1)
                if j >= 2:
                    pe.wait_ge(s["scores_used"], j - 1)
                for n in range(2):
                    for c in range(CH):
                        last = nc.tensor.matmul(psS[:, j % 2, n * BLK:(n + 1) * BLK], xnT[:, c, j * P:(j + 1) * P],
                                                mix[:, c, n * BLK:(n + 1) * BLK], start=(c == 0), stop=(c == CH - 1))
                last.then_inc(s["scored"], 1)

    choice.close()
    rows = sb("pk_rows", [P, 3, GROUPS // P, P])
    groups = sb("pk_groups", [P, 3, GROUPS])
    colhot = sb("pk_colhot", [P, 2, HALF, P])
    rowhot = sb("pk_rowhot", [P, 2, HALF, PK_ROWS * TPG])
    act_d = sb("pk_act", [P, PK_ROWS, BLK])
    hid = sb("pk_hid", [P, PK_ROWS, P])
    sc.close()
    sc = ctx.enter_context(ExitStack())
    psR = sc.enter_context(nc.psum_tensor("b_psR", [P, BLK], F32))
    psD = sc.enter_context(nc.psum_tensor("b_psD", [P, 2, BLK], F32))
    psG = sc.enter_context(nc.psum_tensor("b_psG", [P, GPT, PK_ROWS, TPG], F32))
    psO = sc.enter_context(nc.psum_tensor("b_psO", [P, BLK], F32))
    with nc.Block() as block:
        @block.sync
        def _(sp):
            sp.wait_ge(s["packed_ready"], 1)
            for v in range(3):
                sp.dma_start(scratch[v].rearrange("(i p) k -> p i k", p=P), packed[:, v, :, :]).then_inc(s["packed_out"], 16)
            sp.wait_ge(s["packed_out"], 48)
            for v in range(3):
                sp.dma_start(rows[:, v, :, :],
                             scratch[v].rearrange("(j p t) k -> p j (t k)", p=P, t=TPG)).then_inc(s["rows_in"], 16)

        @block.vector
        def _(dve):
            link = counter(dve, s["hid_used"])
            for v in range(3):
                dve.wait_ge(s["rows_tr"], v + 1)
                nc.vector.tensor_copy(groups[:, v, :], psR[:, :]).then_inc(s["groups_ready"], 1)
            dve.wait_ge(s["groups_ready"], 3)

            def hot_tables(i):
                for q in range(2):
                    n = 2 * i + q
                    if n >= 2:
                        dve.wait_ge(s["spread"], n - 1)
                    g0 = i * GPT + q * HALF
                    shape = [P, HALF, PK_ROWS * TPG]
                    tab = rowtab[:, :, :].rearrange("p r t -> p (r t)").unsqueeze(1).to_broadcast(shape)
                    link(nc.vector.tensor_tensor(rowhot[:, q, :, :], tab,
                                                 groups[:, 0, g0:g0 + HALF].unsqueeze(2).to_broadcast(shape), ALU.is_equal))
                    nc.vector.tensor_tensor(rowhot[:, q, :, :], rowhot[:, q, :, :],
                                            groups[:, 2, g0:g0 + HALF].unsqueeze(2).to_broadcast(shape), ALU.mult).then_inc(s["row_ready"], 1)

            hot_tables(0)
            for i in range(TILES):
                if i + 1 < TILES:
                    hot_tables(i + 1)
                blk = i * P // BLK
                dve.wait_ge(s["act_ready"], (blk + 1) * PK_ROWS)
                dve.wait_ge(s["spread"], 2 * i + 2)
                if i:
                    dve.wait_ge(s["out_done"], i)
                off = i * P % BLK
                for r in range(PK_ROWS):
                    last = nc.vector.tensor_tensor(hid[:, r, :].rearrange("p (g t) -> p g t", t=TPG), psG[:, :, r, :],
                                                   act_d[:, r, off:off + P].rearrange("p (g t) -> p g t", t=TPG), ALU.mult)
                last.then_inc(s["hid_ready"], 1)
                dve.wait_ge(s["out_done"], i + 1)
                nc.vector.tensor_tensor(resid[:, i, :], psO[:, 0:DIM], resid[:, i, :], ALU.add).then_inc(s["added"], 1)

        @block.gpsimd
        def _(pool):
            pool.wait_ge(s["groups_ready"], 3)
            for n in range(2 * TILES):
                if n >= 2:
                    pool.wait_ge(s["spread"], n - 1)
                g0 = n * HALF
                for k in range(HALF):
                    last = nc.gpsimd.tensor_scalar(colhot[:, n % 2, k, :], iota128[:, :], groups[:, 1, g0 + k:g0 + k + 1], None,
                                                   ALU.is_equal)
                last.then_inc(s["col_ready"], 1)

        @block.scalar
        def _(act):
            for n in range(BLKS * PK_ROWS):
                blk, r = n // PK_ROWS, n % PK_ROWS
                act.wait_ge(s["down_done"], n + 1)
                if r == 0 and blk:
                    act.wait_ge(s["hid_ready"], blk * BLK // P)
                nc.scalar.activation(act_d[:, r, :], psD[:, n % 2, :], ACT.Silu).then_inc(s["act_ready"], 1)

        @block.tensor
        def _(pe):
            pe.wait_ge(s["rows_in"], 48)
            for v in range(3):
                if v:
                    pe.wait_ge(s["groups_ready"], v)
                for j in range(GROUPS // P):
                    last = nc.tensor.transpose(psR[:, j * P:(j + 1) * P], rows[:, v, j, :], ident[:, :])
                last.then_inc(s["rows_tr"], 1)
            pe.wait_ge(s["wide_in"], 32)
            for i in range(TILES):
                blk = i * P // BLK
                if i * P % BLK == 0:
                    for r in range(PK_ROWS):
                        n = blk * PK_ROWS + r
                        if n >= 2:
                            pe.wait_ge(s["act_ready"], n - 1)
                        for c in range(CH):
                            last = nc.tensor.matmul(psD[:, n % 2, :], downT[:, c, r * P:(r + 1) * P],
                                                    xnT[:, c, blk * BLK:(blk + 1) * BLK], start=(c == 0), stop=(c == CH - 1))
                        last.then_inc(s["down_done"], 1)
                if i:
                    pe.wait_ge(s["hid_ready"], i)
                for q in range(2):
                    pe.wait_ge(s["col_ready"], 2 * i + q + 1)
                    pe.wait_ge(s["row_ready"], 2 * i + q + 1)
                    for k in range(HALF):
                        last = nc.tensor.matmul(psG[:, q * HALF + k, :, :].rearrange("p r t -> p (r t)"), colhot[:, q, k, :],
                                                rowhot[:, q, k, :], start=True, stop=True)
                    last.then_inc(s["spread"], 1)
                pe.wait_ge(s["hid_ready"], i + 1)
                if i:
                    pe.wait_ge(s["added"], i)
                for r in range(PK_ROWS):
                    last = nc.tensor.matmul(psO[:, 0:DIM], hid[:, r, :], up[:, r, :], start=(r == 0), stop=(r == PK_ROWS - 1))
                last.then_inc(s["out_done"], 1)
    sc.close()


def stage_attention(nc, ctx, sem, sb, ps, g):
    resid, ctxT, xnT, ident, xn = g["resid"], g["ctxT"], g["xnT"], g["ident"], g["xn"]
    stats, mv, work = g["stats"], g["mv"], g["work"]
    PAIRS = HEADS // 2
    K3 = 3 * HD
    PADDED = 64
    identb = sb("c_identb", [P, P], BF16)
    qT = sb("c_qT", [P, PAIRS, TOKENS], BF16)
    kT = sb("c_kT", [P, PAIRS, TOKENS], BF16)
    values = sb("c_values", [P, TILES, DIM], BF16)
    heads_out = sb("c_heads_out", [P, TILES, DIM])
    wp = sb("c_wp", [P, CH, DIM])
    bp = sb("c_bp", [P, DIM])
    v_scale = sb("c_v_scale", [P, CH, 3])
    q_scale = sb("c_q_scale", [P, HEADS, TILES])
    scratch = ctx.enter_context(ExitStack())

    def first(name, shape, dtype=F32):
        return scratch.enter_context(nc.sbuf_tensor(name, shape, dtype))

    wq = first("c_wq", [P, CH, DIM])
    wkv = first("c_wkv", [P, CH, 2 * DIM])
    bq = first("c_bq", [P, 2 * DIM])
    bv = first("c_bv", [P, CH])
    vT = first("c_vT", [P, CH, TOKENS])
    v_int = first("c_v_int", [P, CH, TOKENS], BF16)
    qk = first("c_qk", [P, 2, 2, HEADS, HD])
    amax = first("c_amax", [P, 2, 3, 2, HEADS])
    khat = first("c_khat", [P, 3, HEADS, HD])
    qrows = first("c_qrows", [P, 2, HEADS, PADDED], BF16)
    krows = first("c_krows", [P, 2, HEADS, PADDED], BF16)

    s = {n: sem("c_" + n) for n in (
        "var std normed transposed evacuated chain w_in late_in projected v_mm v_copied v_ready v_tr v_back "
        "rows_ready rows_tr rows_back consts pool_chain qk_free q_loaded scale_neg scored s_taken bias_ready exp_done "
        "rounded p_tr p_back pv_done normalised bchain inverted o_tr o_back out_done added scale_ready pair_free").split()}
    sc = ctx.enter_context(ExitStack())
    psT = sc.enter_context(nc.psum_tensor("c_psT", [P, 2, BLK], F32))
    psQ = sc.enter_context(nc.psum_tensor("c_psQ", [P, 2, BLK], F32))
    psV = sc.enter_context(nc.psum_tensor("c_psV", [P, 2, BLK], F32))
    psR = sc.enter_context(nc.psum_tensor("c_psR", [P, 2, PAIRS, P], BF16))
    with nc.Block() as block:
        @block.sync
        def _(sp):
            sp.dma_start(wkv[:, :, :], g["wkv_d"].rearrange("(c p) n -> p c n", p=P)).then_inc(s["w_in"], 16)
            sp.dma_start(bv[:, :], g["bv_d"]).then_inc(s["w_in"], 16)
            sp.dma_start(wq[:, :, :], g["wq_d"].rearrange("(c p) n -> p c n", p=P)).then_inc(s["w_in"], 16)
            sp.dma_start(bq[:, 0:DIM], g["bq_d"].to_broadcast([P, DIM])).then_inc(s["w_in"], 16)
            sp.dma_start(bq[:, DIM:], g["bkv_d"][:, 0:DIM].to_broadcast([P, DIM])).then_inc(s["w_in"], 16)
            sp.dma_start(bp[:, :], g["bp_d"].to_broadcast([P, DIM])).then_inc(s["late_in"], 16)
            sp.dma_start(wp[:, :, :], g["wp_d"].rearrange("(c p) n -> p c n", p=P)).then_inc(s["late_in"], 16)

        @block.gpsimd
        def _(pool):
            nc.gpsimd.tensor_copy(identb[:, :], ident[:, :])
            nc.gpsimd.memset(qrows[:, :, :, :], 0.0)
            nc.gpsimd.memset(krows[:, :, :, :], 0.0).then_inc(s["consts"], 1)

        def store_rows(i, act):
            for n, dst in ((2 * i, qT), (2 * i + 1, kT)):
                act.wait_ge(s["rows_tr"], n + 1)
                nc.scalar.activation(dst[:, :, i * P:(i + 1) * P], psR[:, n % 2, :, :], ACT.Copy).then_inc(s["rows_back"], 1)

        @block.scalar
        def _(act):
            act.wait_ge(s["w_in"], 80)
            for n in range(CH * BLKS):
                c, b = n // BLKS, n % BLKS
                act.wait_ge(s["v_mm"], n + 1)
                nc.scalar.activation(vT[:, c, b * BLK:(b + 1) * BLK], psV[:, n % 2, :], ACT.Identity,
                                     bias=bv[:, c:c + 1]).then_inc(s["v_copied"], 1)
            norm_std(nc, act, work, s["var"], s["std"])
            for i in range(TILES):
                act.wait_ge(s["transposed"], i + 1)
                nc.scalar.activation(xnT[:, :, i * P:(i + 1) * P],
                                     psT[:, i % 2, 0:DIM].rearrange("p (c t) -> p c t", c=CH),
                                     ACT.Copy).then_inc(s["evacuated"], 1)
                if i:
                    store_rows(i - 1, act)
            store_rows(TILES - 1, act)

        @block.vector
        def _(dve):
            link = counter(dve, s["chain"])
            norm_statistics(nc, dve, link, resid, stats, mv, work, s["var"], s["std"])
            for i in range(2):
                norm_tile(nc, dve, i, resid, xn, mv, work, s["normed"], s["transposed"])
            dve.wait_ge(s["v_copied"], CH * BLKS)
            for c in range(CH):
                last = nc.vector.tensor_reduce(v_scale[:, c, 0:1], vT[:, c, :], AX.X, ALU.max, apply_absolute_value=True)
            link(last)
            link(nc.vector.tensor_scalar(v_scale[:, :, 1], v_scale[:, :, 0], 1.0 / 127.0, 1e-8, ALU.mult, ALU.max))
            link(nc.vector.reciprocal(v_scale[:, :, 2], v_scale[:, :, 1]))
            for c in range(CH):
                last = nc.vector.tensor_scalar(vT[:, c, :], vT[:, c, :], v_scale[:, c, 2:3], ROUND, ALU.mult, ALU.add)
            link(last)
            for c in range(CH):
                nc.vector.tensor_scalar(v_int[:, c, :], vT[:, c, :], ROUND, None, ALU.subtract).then_inc(s["v_ready"], 1)
            dve.wait_ge(s["late_in"], 32)
            for c in range(CH):
                nc.vector.tensor_scalar(wp[:, c, :], wp[:, c, :], v_scale[:, c, 1:2], None, ALU.mult)
            dve.wait_ge(s["consts"], 1)
            for i in range(TILES):
                if i + 2 < TILES:
                    norm_tile(nc, dve, i + 2, resid, xn, mv, work, s["normed"], s["transposed"])
                u = i % 2
                t = qk[:, u, :, :, :]
                tf = t.rearrange("p z h d -> p z (h d)")
                dve.wait_ge(s["projected"], i + 1)
                link(nc.vector.tensor_tensor(t.rearrange("p z h d -> p (z h d)"), psQ[:, u, :], bq[:, :], ALU.add))
                m = amax[:, u, :, :, :]
                link(nc.vector.tensor_reduce(m[:, 0, :, :], t, AX.X, ALU.max, apply_absolute_value=True))
                nc.vector.tensor_scalar(m[:, 1, 0, :], m[:, 0, 0, :], 0.25 / 127.0, 1e-8, ALU.mult, ALU.max)
                link(nc.vector.tensor_scalar(m[:, 1, 1, :], m[:, 0, 1, :], 1.0 / 127.0, 1e-8, ALU.mult, ALU.max))
                link(nc.vector.reciprocal(m[:, 2, :, :], m[:, 1, :, :]))
                nc.vector.tensor_copy(q_scale[:, :, i], m[:, 1, 0, :])
                link(nc.vector.tensor_scalar(m[:, 2, 0, :], m[:, 2, 0, :], 0.25, None, ALU.mult))
                link(nc.vector.tensor_tensor(t, t, m[:, 2, :, :].unsqueeze(3).to_broadcast([P, 2, HEADS, HD]), ALU.mult))
                link(nc.vector.tensor_scalar(tf, tf, ROUND, ROUND, ALU.add, ALU.subtract))
                if i >= 2:
                    dve.wait_ge(s["rows_tr"], 2 * i - 2)
                qd = qrows[:, u, :, 0:K3].rearrange("p h (j d) -> p h j d", j=3)
                nc.vector.tensor_copy(qd, t[:, 0, :, :].unsqueeze(2).to_broadcast([P, HEADS, 3, HD])).then_inc(s["rows_ready"], 1)
                link(nc.vector.tensor_tensor(khat[:, 0, :, :], t[:, 1, :, :],
                                             m[:, 1, 1, :].unsqueeze(2).to_broadcast([P, HEADS, HD]), ALU.mult))
                for part in range(3):
                    kp = krows[:, u, :, part * HD:(part + 1) * HD]
                    copy = nc.vector.tensor_copy(kp, khat[:, part, :, :])
                    if part == 2:
                        copy.then_inc(s["rows_ready"], 1)
                    else:
                        link(copy)
                        link(nc.vector.tensor_tensor(khat[:, part + 1, :, :], khat[:, part, :, :], kp, ALU.subtract))
            for i in range(TILES):
                dve.wait_ge(s["v_tr"], i + 1)
                nc.vector.tensor_copy(values[:, i, :], psV[:, i % 2, 0:P].bitcast(BF16)).then_inc(s["v_back"], 1)

        @block.tensor
        def _(pe):
            pe.wait_ge(s["w_in"], 80)
            for n in range(CH * BLKS):
                c, b = n // BLKS, n % BLKS
                if n >= 2:
                    pe.wait_ge(s["v_copied"], n - 1)
                for k in range(CH):
                    last = nc.tensor.matmul(psV[:, n % 2, :], wkv[:, k, DIM + c * P:DIM + (c + 1) * P],
                                            ctxT[:, k, b * BLK:(b + 1) * BLK], start=(k == 0), stop=(k == CH - 1))
                last.then_inc(s["v_mm"], 1)
            pe.wait_ge(s["consts"], 1)

            def rows_of(i):
                for n, src in ((2 * i, qrows), (2 * i + 1, krows)):
                    pe.wait_ge(s["rows_ready"], n + 1)
                    if n >= 2:
                        pe.wait_ge(s["rows_back"], n - 1)
                    for p in range(PAIRS):
                        last = nc.tensor.transpose(psR[:, n % 2, p, :],
                                                   src[:, i % 2, 2 * p:2 * p + 2, :].rearrange("p h d -> p (h d)"), identb[:, :])
                    last.then_inc(s["rows_tr"], 1)

            for i in range(TILES):
                transpose_tile(nc, pe, i, xn, psT, ident, s["normed"], s["transposed"], s["evacuated"])
                pe.wait_ge(s["evacuated"], i + 1)
                if i >= 2:
                    pe.wait_ge(s["rows_ready"], 2 * i - 2)
                for z in range(2):
                    src, w = ((xnT, wq), (ctxT, wkv))[z]
                    for k in range(CH):
                        last = nc.tensor.matmul(psQ[:, i % 2, z * DIM:(z + 1) * DIM], src[:, k, i * P:(i + 1) * P],
                                                w[:, k, 0:DIM], start=(k == 0), stop=(k == CH - 1))
                last.then_inc(s["projected"], 1)
                if i:
                    rows_of(i - 1)
            rows_of(TILES - 1)
            pe.wait_ge(s["v_ready"], CH)
            for i in range(TILES):
                if i >= 2:
                    pe.wait_ge(s["v_back"], i - 1)
                for c in range(CH):
                    last = nc.tensor.transpose(psV[:, i % 2, 0:P].bitcast(BF16)[:, c * P:(c + 1) * P],
                                               v_int[:, c, i * P:(i + 1) * P], identb[:, :])
                last.then_inc(s["v_tr"], 1)

    sc.close()
    scratch.close()
    qh = sb("c_qh", [P, TOKENS], BF16)
    kh = sb("c_kh", [P, TOKENS], BF16)
    sq = sb("c_sq", [P, 2, TILES, 2])
    scores = sb("c_scores", [P, 2, TOKENS])
    exps = sb("c_exps", [P, 2, TOKENS])
    probs = sb("c_probs", [P, 2, TOKENS], BF16)
    probsT = sb("c_probsT", [P, 2, TILES, P], BF16)
    row = sb("c_row", [P, 4, 6])
    UNITS = 2 * TILES
    HALFW = TOKENS // 2
    TR, PV = 2, 3
    sc = ctx.enter_context(ExitStack())
    psS = sc.enter_context(nc.psum_tensor("c_psS", [P, 2, HALFW], F32))
    psP = sc.enter_context(nc.psum_tensor("c_psP", [P, TILES, P], BF16))
    psO = sc.enter_context(nc.psum_tensor("c_psO", [P, 2, BLK], F32))
    with nc.Block() as block:
        @block.tensor
        def _(pe):
            for credited in ("s_taken", "p_back", "normalised"):
                pe.sem_inc(s[credited], 1)
            with pe.Fori(0, PAIRS) as p:
                base = p * UNITS
                pe.wait_ge(s["q_loaded"], p + 1)
                for n in range(UNITS + PV):
                    if n < UNITS:
                        u, i = n // TILES, n % TILES
                        r0 = PADDED * u
                        for half in range(2):
                            pe.wait_ge(s["s_taken"], (base + n) * 2 + half if n or half else base * 2 + 1)
                            for b in range(2):
                                k0 = half * HALFW + b * BLK
                                last = nc.tensor.matmul(psS[:, half, b * BLK:(b + 1) * BLK], qh[r0:r0 + K3, i * P:(i + 1) * P],
                                                        kh[r0:r0 + K3, k0:k0 + BLK],
                                                        start=True, stop=True)
                            last.then_inc(s["scored"], 1)
                    m = n - TR
                    if 0 <= m < UNITS:
                        pe.wait_ge(s["rounded"], base + m + 1)
                        pe.wait_ge(s["p_back"], base + m + 1)
                        for c in range(TILES):
                            last = nc.tensor.transpose(psP[:, c, :], probs[:, m % 2, c * P:(c + 1) * P], identb[:, :])
                        last.then_inc(s["p_tr"], 1)
                    m = n - PV
                    if m >= 0:
                        u = m // TILES
                        pe.wait_ge(s["normalised"], base + m if m else base + 1)
                        pe.wait_ge(s["p_back"], base + m + 2)
                        for c in range(TILES):
                            last = nc.tensor.matmul(psO[:, m % 2, 0:HD], probsT[:, m % 2, c, :],
                                                    values[:, c, bass.ds((p * 2 + u) * HD, HD)],
                                                    start=(c == 0), stop=(c == TILES - 1))
                        last.then_inc(s["pv_done"], 1)

        @block.gpsimd
        def _(pool):
            pool.sem_inc(s["pair_free"], 1)
            with pool.Fori(0, PAIRS) as p:
                pool.wait_ge(s["pair_free"], p + 1)
                nc.gpsimd.tensor_copy(qh[:, :], qT[:, bass.ds(p, 1), :].rearrange("p a t -> p (a t)"))
                nc.gpsimd.tensor_copy(kh[:, :], kT[:, bass.ds(p, 1), :].rearrange("p a t -> p (a t)")).then_inc(s["q_loaded"], 1)
                nc.gpsimd.tensor_copy(sq[:, 0, :, :], q_scale[:, bass.ds(p * 2, 2), :].rearrange("p h i -> p i h")).then_inc(s["pool_chain"], 1)
                pool.wait_ge(s["pool_chain"], p + 1)
                pool.sem_inc(s["scale_ready"], 1)

        @block.scalar
        def _(act):
            with act.Fori(0, PAIRS) as p:
                base = p * UNITS
                act.wait_ge(s["scale_ready"], p + 1)
                for n in range(UNITS + TR):
                    if n < UNITS:
                        u, i = n // TILES, n % TILES
                        act.wait_ge(s["bias_ready"], base + n + 1)
                        if n >= 2:
                            act.wait_ge(s["rounded"], base + n - 1)
                        nc.scalar.activation(exps[:, n % 2, :], scores[:, n % 2, :], ACT.Exp, bias=row[:, n % 4, 3:4],
                                             scale=sq[:, 0, i, u:u + 1], accum_out=row[:, n % 4, 4:5]).then_inc(s["exp_done"], 1)
                    m = n - TR
                    if m >= 0:
                        act.wait_ge(s["p_tr"], base + m + 1)
                        if m >= 2:
                            act.wait_ge(s["pv_done"], base + m - 1)
                        nc.scalar.activation(probsT[:, m % 2, :, :], psP[:, :, :], ACT.Copy).then_inc(s["p_back"], 1)

        @block.vector
        def _(dve):
            with dve.Fori(0, PAIRS) as p:
                base = p * UNITS
                dve.wait_ge(s["scale_ready"], p + 1)
                nc.vector.tensor_scalar(sq[:, 1, :, :], sq[:, 0, :, :], -1.0, None, ALU.mult).then_inc(s["scale_neg"], 1)
                dve.wait_ge(s["scale_neg"], p + 1)
                for n in range(UNITS + PV):
                    if n < UNITS:
                        u, i = n // TILES, n % TILES
                        r = row[:, n % 4, :]
                        if n >= 2:
                            dve.wait_ge(s["exp_done"], base + n - 1)
                        for half in range(2):
                            dve.wait_ge(s["scored"], (base + n) * 2 + half + 1)
                            nc.vector.tensor_scalar(scores[:, n % 2, half * HALFW:(half + 1) * HALFW], psS[:, half, :], 0.0, -3.0e38,
                                                    ALU.add, ALU.max, accum_out=r[:, half:half + 1]).then_inc(s["s_taken"], 1)
                        dve.wait_ge(s["s_taken"], (base + n) * 2 + 3)
                        nc.vector.tensor_tensor(r[:, 2:3], r[:, 0:1], r[:, 1:2], ALU.max).then_inc(s["bchain"], 1)
                        dve.wait_ge(s["bchain"], base + n + 1)
                        nc.vector.tensor_scalar(r[:, 3:4], r[:, 2:3], sq[:, 1, i, u:u + 1], LN255, ALU.mult, ALU.add).then_inc(s["bias_ready"], 1)
                    m = n - 1
                    if 0 <= m < UNITS:
                        dve.wait_ge(s["exp_done"], base + m + 1)
                        if m >= 2:
                            dve.wait_ge(s["p_tr"], base + m - 1)
                        nc.vector.tensor_scalar(probs[:, m % 2, :], exps[:, m % 2, :], ROUND, ROUND, ALU.add,
                                                ALU.subtract).then_inc(s["rounded"], 1)
                    m = n - PV
                    if m >= 0:
                        h, i, r = p * 2 + m // TILES, m % TILES, row[:, m % 4, :]
                        nc.vector.reciprocal(r[:, 5:6], r[:, 4:5]).then_inc(s["inverted"], 1)
                        dve.wait_ge(s["inverted"], base + m + 1)
                        dve.wait_ge(s["pv_done"], base + m + 1)
                        nc.vector.tensor_scalar(heads_out[:, i, bass.ds(h * HD, HD)], psO[:, m % 2, 0:HD], r[:, 5:6], None,
                                                ALU.mult).then_inc(s["normalised"], 1)
                dve.sem_inc(s["pair_free"], 1)

    sc.close()
    sc = ctx.enter_context(ExitStack())
    oT = sb("c_oT", [P, 2, DIM])
    psT2 = sc.enter_context(nc.psum_tensor("c_psT2", [P, 2, BLK], F32))
    psO2 = sc.enter_context(nc.psum_tensor("c_psO2", [P, 2, BLK], F32))
    with nc.Block() as block:
        @block.tensor
        def _(pe):
            for i in range(TILES + 1):
                if i < TILES:
                    if i >= 2:
                        pe.wait_ge(s["o_back"], i - 1)
                    for c in range(CH):
                        last = nc.tensor.transpose(psT2[:, i % 2, c * P:(c + 1) * P], heads_out[:, i, c * P:(c + 1) * P], ident[:, :])
                    last.then_inc(s["o_tr"], 1)
                if i:
                    j = i - 1
                    pe.wait_ge(s["o_back"], j + 1)
                    if j >= 2:
                        pe.wait_ge(s["added"], j - 1)
                    for c in range(CH):
                        last = nc.tensor.matmul(psO2[:, j % 2, 0:DIM], oT[:, j % 2, c * P:(c + 1) * P], wp[:, c, :],
                                                start=(c == 0), stop=(c == CH - 1))
                    last.then_inc(s["out_done"], 1)

        @block.scalar
        def _(act):
            for i in range(TILES):
                act.wait_ge(s["o_tr"], i + 1)
                if i >= 2:
                    act.wait_ge(s["out_done"], i - 1)
                nc.scalar.activation(oT[:, i % 2, :], psT2[:, i % 2, 0:DIM], ACT.Copy).then_inc(s["o_back"], 1)

        @block.vector
        def _(dve):
            dve.wait_ge(s["late_in"], 32)
            for i in range(TILES):
                nc.vector.tensor_tensor(resid[:, i, :], resid[:, i, :], bp[:, :], ALU.add).then_inc(s["bchain"], 1)
            dve.wait_ge(s["bchain"], PAIRS * UNITS + TILES)
            for i in range(TILES):
                dve.wait_ge(s["out_done"], i + 1)
                nc.vector.tensor_tensor(resid[:, i, :], psO2[:, i % 2, 0:DIM], resid[:, i, :], ALU.add).then_inc(s["added"], 1)
    sc.close()


def stage_experts(nc, ctx, sem, sb, ps, g):
    resid, xnT, ident, xn = g["resid"], g["xnT"], g["ident"], g["xn"]
    stats, mv, work = g["stats"], g["mv"], g["work"]
    LOG = MOE + 1
    gates = sb("d_gates", [P, CH, LOG])
    iota = sb("d_iota", [P, MOE])
    route = sb("d_route", [P, TILES, EXPERTS])
    logits = sb("d_logits", [P, 2, LOG])
    pr = sb("d_probs", [P, 2, LOG])
    small = sb("d_small", [P, 2, 6])
    top = sb("d_top", [P, 2, 8])
    top_i = sb("d_top_i", [P, 2, 8], U32)
    top_f = sb("d_top_f", [P, 2, 8])
    term = sb("d_term", [P, 2, MOE])
    w_up = sb("d_w_up", [P, 2, CH, UPCOLS])
    w_down = sb("d_w_down", [P, 2, 2, DIM])
    gate = sb("d_gate", [P, 2, 2, BLK])
    hidden = sb("d_hidden", [P, 2, 2, BLK])
    s = {n: sem("d_" + n) for n in (
        "var std normed transposed evacuated chain g_in iota logged lready exp_done routed "
        "w0_in w1_in up_done h0_done silu h_ready down_done added sig used0 used1").split()}
    sc = ctx.enter_context(ExitStack())
    psT = sc.enter_context(nc.psum_tensor("d_psT", [P, 2, BLK], F32))
    psL = sc.enter_context(nc.psum_tensor("d_psL", [P, 2, BLK], F32))
    with nc.Block() as block:
        @block.sync
        def _(sp):
            sp.dma_start(gates[:, :, :], g["gates_d"].rearrange("(c p) n -> p c n", p=P)).then_inc(s["g_in"], 16)

        @block.gpsimd
        def _(pool):
            nc.gpsimd.iota(iota[:, :], [[1, MOE]], base=0, channel_multiplier=0,
                           allow_small_or_imprecise_dtypes=True).then_inc(s["iota"], 1)

        @block.scalar
        def _(act):
            norm_std(nc, act, work, s["var"], s["std"])
            for i in range(TILES + 1):
                if i < TILES:
                    act.wait_ge(s["transposed"], i + 1)
                    nc.scalar.activation(xnT[:, :, i * P:(i + 1) * P],
                                         psT[:, i % 2, 0:DIM].rearrange("p (c t) -> p c t", c=CH),
                                         ACT.Copy).then_inc(s["evacuated"], 1)
                if i:
                    j, u = i - 1, (i - 1) % 2
                    act.wait_ge(s["lready"], j + 1)
                    nc.scalar.activation(pr[:, u, 0:MOE], logits[:, u, 0:MOE], ACT.Exp, bias=small[:, u, 0:1],
                                         accum_out=small[:, u, 1:2])
                    nc.scalar.activation(pr[:, u, MOE:LOG], logits[:, u, MOE:LOG], ACT.Exp, scale=-1.0).then_inc(s["exp_done"], 1)

        @block.vector
        def _(dve):
            link = counter(dve, s["chain"])
            norm_statistics(nc, dve, link, resid, stats, mv, work, s["var"], s["std"])
            for i in range(2):
                norm_tile(nc, dve, i, resid, xn, mv, work, s["normed"], s["transposed"])
            dve.wait_ge(s["iota"], 1)
            for i in range(TILES):
                if i + 2 < TILES:
                    norm_tile(nc, dve, i + 2, resid, xn, mv, work, s["normed"], s["transposed"])
                u = i % 2
                dve.wait_ge(s["logged"], i + 1)
                link(nc.vector.tensor_copy(logits[:, u, :], psL[:, u, 0:LOG]))
                nc.vector.tensor_reduce(small[:, u, 0:1], logits[:, u, 0:MOE], AX.X, ALU.max, negate=True).then_inc(s["lready"], 1)
                dve.wait_ge(s["exp_done"], i + 1)
                link(nc.vector.reciprocal(small[:, u, 2:3], small[:, u, 1:2]))
                link(nc.vector.tensor_scalar(pr[:, u, 0:MOE], pr[:, u, 0:MOE], small[:, u, 2:3], None, ALU.mult))
                link(nc.vector.max(top[:, u, :], pr[:, u, 0:MOE]))
                link(nc.vector.max_index(top_i[:, u, :], top[:, u, :], pr[:, u, 0:MOE]))
                link(nc.vector.tensor_copy(top_f[:, u, :], top_i[:, u, :]))
                w = route[:, i, 0:MOE]
                link(nc.vector.tensor_scalar(w, iota[:, :], top_f[:, u, 0:1], top[:, u, 0:1], ALU.is_equal, ALU.mult))
                for k in range(1, MOE_TOP):
                    link(nc.vector.tensor_scalar(term[:, u, :], iota[:, :], top_f[:, u, k:k + 1], top[:, u, k:k + 1],
                                                 ALU.is_equal, ALU.mult))
                    link(nc.vector.tensor_tensor(w, w, term[:, u, :], ALU.add))
                link(nc.vector.tensor_scalar(small[:, u, 3:4], pr[:, u, MOE:LOG], 1.0, None, ALU.add))
                link(nc.vector.reciprocal(small[:, u, 4:5], small[:, u, 3:4]))
                link(nc.vector.tensor_copy(route[:, i, MOE:EXPERTS], small[:, u, 4:5].to_broadcast([P, SHARED])))

        @block.tensor
        def _(pe):
            pe.wait_ge(s["g_in"], 16)
            for i in range(TILES + 1):
                if i < TILES:
                    transpose_tile(nc, pe, i, xn, psT, ident, s["normed"], s["transposed"], s["evacuated"])
                if i:
                    j = i - 1
                    pe.wait_ge(s["evacuated"], j + 1)
                    if j >= 2:
                        pe.wait_ge(s["lready"], j - 1)
                    for c in range(CH):
                        last = nc.tensor.matmul(psL[:, j % 2, 0:LOG], xnT[:, c, j * P:(j + 1) * P], gates[:, c, :],
                                                start=(c == 0), stop=(c == CH - 1))
                    last.then_inc(s["logged"], 1)
    sc.close()
    sc = ctx.enter_context(ExitStack())
    psU = sc.enter_context(nc.psum_tensor("d_psU", [P, 2, 3, BLK], F32))
    psD = sc.enter_context(nc.psum_tensor("d_psD", [P, 2, BLK], F32))
    STEPS = 2 * BLKS
    loads = (s["w0_in"], s["w1_in"])
    with nc.Block() as block:
        @block.sync
        def _(sp):
            sp.sem_inc(s["used0"], 1)
            sp.sem_inc(s["used1"], 1)
            with sp.Fori(0, EXPERTS // 2) as e:
                for x in range(2):
                    sp.wait_ge((s["used0"], s["used1"])[x], e + 1)
                    sp.dma_start(w_up[:, x, :, :], g["up13_d"][bass.ds(e * 2 + x, 1), :, :].rearrange("e (c p) n -> p (e c) n", p=P)).then_inc(loads[x], 16)
                    sp.dma_start(w_down[:, x, 0, :], g["w2_d"][bass.ds(e * 2 + x, 1), 0:P, :].rearrange("e i d -> i (e d)")).then_inc(loads[x], 16)
                    sp.dma_start(w_down[0:REST, x, 1, :], g["w2_d"][bass.ds(e * 2 + x, 1), P:INTER, :].rearrange("e i d -> i (e d)")).then_inc(loads[x], 16)

        @block.tensor
        def _(pe):
            pe.sem_inc(s["added"], 1)
            with pe.Fori(0, EXPERTS // 2) as e:
                base = e * STEPS
                for n in range(STEPS + 1):
                    if n < STEPS:
                        x, b = n // BLKS, n % BLKS
                        if b == 0:
                            pe.wait_ge(loads[x], (e + 1) * 48)
                        if n >= 2:
                            pe.wait_ge(s["h_ready"], base + n - 1)
                        cols = xnT[:, :, b * BLK:(b + 1) * BLK]
                        for k in range(3):
                            width = P if k < 2 else UPCOLS - 2 * P
                            for c in range(CH):
                                last = nc.tensor.matmul(psU[0:width, n % 2, k, :], w_up[:, x, c, k * P:k * P + width], cols[:, c, :],
                                                        start=(c == 0), stop=(c == CH - 1))
                        last.then_inc(s["up_done"], 1)
                    if n:
                        m = n - 1
                        x, b = m // BLKS, m % BLKS
                        pe.wait_ge(s["h_ready"], base + m + 1)
                        for half in range(2):
                            pe.wait_ge(s["added"], (base + m) * 2 + half if m or half else base * 2 + 1)
                            for j in range(2):
                                t0 = (2 * half + j) * P
                                out = psD[:, half, j * DIM:(j + 1) * DIM]
                                nc.tensor.matmul(out, hidden[:, m % 2, 0, t0:t0 + P], w_down[:, x, 0, :], start=True, stop=False)
                                last = nc.tensor.matmul(out, hidden[0:REST, m % 2, 1, t0:t0 + P], w_down[0:REST, x, 1, :], start=False, stop=True)
                            last.then_inc(s["down_done"], 1)
                        if b == BLKS - 1:
                            pe.wait_ge(s["down_done"], (base + m) * 2 + 2)
                            pe.sem_inc((s["used0"], s["used1"])[x], 1)

        @block.scalar
        def _(act):
            with act.Fori(0, EXPERTS // 2) as e:
                base = e * STEPS
                for n in range(STEPS):
                    act.wait_ge(s["up_done"], base + n + 1)
                    if n >= 2:
                        act.wait_ge(s["h_ready"], base + n - 1)
                    nc.scalar.activation(gate[:, n % 2, 0, :], psU[:, n % 2, 0, :], ACT.Silu)
                    nc.scalar.activation(gate[0:REST, n % 2, 1, :], psU[0:REST, n % 2, 2, :], ACT.Silu).then_inc(s["silu"], 1)

        @block.vector
        def _(dve):
            with dve.Fori(0, EXPERTS // 2) as e:
                base = e * STEPS
                for n in range(STEPS + 1):
                    if n < STEPS:
                        dve.wait_ge(s["silu"], base + n + 1)
                        if n >= 2:
                            dve.wait_ge(s["down_done"], (base + n - 1) * 2)
                        nc.vector.tensor_tensor(hidden[:, n % 2, 0, :], gate[:, n % 2, 0, :], psU[:, n % 2, 1, :], ALU.mult)
                        nc.vector.tensor_tensor(hidden[0:REST, n % 2, 1, :], gate[0:REST, n % 2, 1, :], psU[64:64 + REST, n % 2, 2, :],
                                                ALU.mult).then_inc(s["h_ready"], 1)
                    if n:
                        m = n - 1
                        x, b = m // BLKS, m % BLKS
                        for half in range(2):
                            dve.wait_ge(s["down_done"], (base + m) * 2 + half + 1)
                            for j in range(2):
                                i = b * BLK // P + 2 * half + j
                                last = nc.vector.scalar_tensor_tensor(resid[:, i, :], psD[:, half, j * DIM:(j + 1) * DIM],
                                                                      route[:, i, bass.ds(e * 2 + x, 1)], resid[:, i, :],
                                                                      ALU.mult, ALU.add)
                            last.then_inc(s["added"], 1)
    sc.close()


def stage_store(nc, ctx, sem, sb, ps, g):
    stored = sem("stored")
    with nc.Block() as block:
        @block.sync
        def _(sp):
            sp.dma_start(g["out"].rearrange("b t d -> t b d"), g["resid"][:, :, :]).then_inc(stored, 16)
            sp.wait_ge(stored, 16)


def build(nc, arrays, out, stages=4):
    with ExitStack() as ctx:
        def sem(name):
            return ctx.enter_context(nc.semaphore(name))

        def sb(name, shape, dtype=F32):
            return ctx.enter_context(nc.sbuf_tensor(name, shape, dtype))

        def ps(name, shape, dtype=F32):
            return ctx.enter_context(nc.psum_tensor(name, shape, dtype))

        g = dict(arrays)
        g["out"] = out
        g["resid"] = sb("resid", [P, TILES, DIM])
        g["ctxT"] = sb("ctxT", [P, CH, TOKENS])
        g["xnT"] = sb("xnT", [P, CH, TOKENS])
        g["ident"] = sb("ident", [P, P])
        g["stats"] = sb("stats", [P, TILES, 6])
        g["mv"] = sb("mv", [P, TILES, 2])
        g["work"] = sb("work", [P, 4, TILES])
        g["xn"] = sb("xn", [P, 4, DIM])
        for name in ("x_in", "ctx_in", "ident_ready"):
            g[name] = sem(name)
        for n, stage in enumerate((stage_recurrence, stage_product_keys, stage_attention, stage_experts)[:stages]):
            with ExitStack() as own:
                def own_sb(name, shape, dtype=F32):
                    return own.enter_context(nc.sbuf_tensor(name, shape, dtype))

                def own_ps(name, shape, dtype=F32):
                    return own.enter_context(nc.psum_tensor(name, shape, dtype))

                stage(nc, own, sem, own_sb, own_ps, g)
        stage_store(nc, ctx, sem, sb, ps, g)


def layouts(inputs):
    import numpy as np

    a = {k: np.asarray(v) for k, v in inputs.items()}
    x = np.ascontiguousarray(a["x"].reshape(TOKENS, DIM))
    ctxT = np.ascontiguousarray(a["ctx_2048"].reshape(TOKENS, DIM).T)
    w13 = a["L1_ffn_w13"]
    se = a["L1_ffn_se_gate_up_w"]
    gate = np.concatenate([w13[:, :INTER], se[:SH_INTER].reshape(SHARED, INTER, DIM)])
    upw = np.concatenate([w13[:, INTER:], se[SH_INTER:].reshape(SHARED, INTER, DIM)])
    up13 = np.zeros((EXPERTS, UPCOLS, DIM), np.float32)
    up13[:, 0:P] = gate[:, 0:P]
    up13[:, P:2 * P] = upw[:, 0:P]
    up13[:, 2 * P:2 * P + REST] = gate[:, P:]
    up13[:, 2 * P + 64:] = upw[:, P:]
    w2 = np.concatenate([a["L1_ffn_w2"], a["L1_ffn_se_down_w"].reshape(DIM, SHARED, INTER).transpose(1, 0, 2)])
    c = np.ascontiguousarray
    return {
        "x": x, "ctxT_d": ctxT, "td": np.ascontiguousarray(a["L0_xattn_time_decay"].reshape(CH, P).T),
        "tf": np.ascontiguousarray(a["L0_xattn_time_first"].reshape(CH, P).T),
        "pk_wqT_d": c(a["L0_ffn_Wq"].T),
        "pk_keysT_d": c(a["L0_ffn_keys"].transpose(0, 2, 3, 1).reshape(PK_HEADS * 2 * PK_DK, PK_KEYS)),
        "pk_downT_d": c(a["L0_ffn_e_down"].T), "pk_up_d": c(a["L0_ffn_e_up"]),
        "wq_d": c(a["L1_xattn_Wq"]), "bq_d": c(a["L1_xattn_bq"].reshape(1, -1)),
        "wkv_d": c(a["L1_xattn_Wkv"]), "bkv_d": c(a["L1_xattn_bkv"].reshape(1, -1)),
        "bv_d": c(a["L1_xattn_bkv"][DIM:].reshape(CH, P).T),
        "wp_d": c(a["L1_xattn_Wp"]), "bp_d": c(a["L1_xattn_bp"].reshape(1, -1)),
        "gates_d": c(np.concatenate([a["L1_ffn_gate_w"], a["L1_ffn_shared_gate_w"]]).T),
        "up13_d": c(up13.transpose(0, 2, 1)),
        "w2_d": c(w2.transpose(0, 2, 1)),
    }


def kernel(**inputs):
    import numpy as np
    import concourse.bacc as bacc
    from concourse.bass_utils import run_bass_kernel_spmd

    arrays = layouts(inputs)
    nc = bacc.Bacc("TRN2", target_bir_lowering=False, num_devices=1)
    aps = {n: nc.dram_tensor("in_" + n, a.shape, mybir.dt.from_np(a.dtype), kind="ExternalInput").ap() for n, a in arrays.items()}
    out = nc.dram_tensor("out", (BATCH, SEQ, DIM), F32, kind="ExternalOutput").ap()
    build(nc, aps, out)
    result = run_bass_kernel_spmd(nc, [{"in_" + n: a for n, a in arrays.items()}], core_ids=[0])
    return result.results[0]["out"]
```

```python
import concourse.bass as bass
from concourse import mybir
from contextlib import ExitStack

F32 = mybir.dt.float32
BF16 = mybir.dt.bfloat16
U32 = mybir.dt.uint32
ALU = mybir.AluOpType
ACT = mybir.ActivationFunctionType
AX = mybir.AxisListType

P = 128
BATCH, SEQ, DIM = 16, 128, 256
TILES = BATCH * SEQ // P
TOKENS = TILES * P
CH = DIM // P
EPS = 1e-5
ROUND = 12582912.0
BLK = 512
BLKS = TOKENS // BLK

PK_HEADS, PK_KEYS, PK_TOP, PK_DK = 4, 128, 8, 64
PK_EXPERTS = 2048
PK_ROWS = PK_EXPERTS // P

HEADS, HD = 16, 16
LN255 = 5.541263545158426

MOE, INTER, SH_INTER, MOE_TOP = 60, 176, 704, 4
SHARED = SH_INTER // INTER
BLOCKS = -(-((TOKENS * MOE_TOP + MOE * (P - 1)) // P) // 4) * 4
REST = INTER - P
UPCOLS = 2 * P + 64 + REST


def counter(engine, semaphore):
    count = [0]

    def link(instruction):
        instruction.then_inc(semaphore, 1)
        count[0] += 1
        engine.wait_ge(semaphore, count[0])

    return link


def norm_statistics(nc, dve, link, resid, stats, mv, work, var_ready, std_ready):
    for i in range(TILES):
        last = nc.vector.bn_stats(stats[:, i, :], resid[:, i, :])
    link(last)
    for i in range(TILES):
        last = nc.vector.bn_aggr(mv[:, i, :], stats[:, i, :])
    link(last)
    nc.vector.tensor_scalar(work[:, 0, :], mv[:, :, 1], EPS, None, ALU.add).then_inc(var_ready, 1)
    dve.wait_ge(std_ready, 1)
    link(nc.vector.reciprocal(work[:, 2, :], work[:, 1, :]))
    link(nc.vector.tensor_tensor(work[:, 3, :], work[:, 2, :], work[:, 2, :], ALU.mult))
    link(nc.vector.tensor_tensor(work[:, 3, :], work[:, 3, :], work[:, 0, :], ALU.mult))
    link(nc.vector.tensor_scalar(work[:, 3, :], work[:, 3, :], -0.5, 1.5, ALU.mult, ALU.add))
    link(nc.vector.tensor_tensor(work[:, 2, :], work[:, 2, :], work[:, 3, :], ALU.mult))


def norm_std(nc, act, work, var_ready, std_ready):
    act.wait_ge(var_ready, 1)
    nc.scalar.activation(work[:, 1, :], work[:, 0, :], ACT.Sqrt).then_inc(std_ready, 1)


def norm_tile(nc, dve, i, resid, xn, mv, work, normed, transposed):
    if i >= 4:
        dve.wait_ge(transposed, i - 3)
    nc.vector.tensor_scalar(xn[:, i % 4, :], resid[:, i, :], mv[:, i, 0:1], work[:, 2, i:i + 1],
                            ALU.subtract, ALU.mult).then_inc(normed, 1)


def transpose_tile(nc, pe, i, xn, psT, ident, normed, transposed, evacuated):
    pe.wait_ge(normed, i + 1)
    if i >= 2:
        pe.wait_ge(evacuated, i - 1)
    for c in range(CH):
        last = nc.tensor.transpose(psT[:, i % 2, c * P:(c + 1) * P], xn[:, i % 4, c * P:(c + 1) * P], ident[:, :])
    last.then_inc(transposed, 1)


def stage_recurrence(nc, ctx, sem, sb, ps, g):
    resid, ctxT, ident = g["resid"], g["ctxT"], g["ident"]
    stats, mv, work, xn = g["stats"], g["mv"], g["work"], g["xn"]
    par = sb("wkv_par", [P, 8, CH])
    ek = sb("ek", [P, CH, TOKENS])
    ev = sb("ev", [P, CH, TOKENS])
    decay = sb("decay", [P, TOKENS])
    acc_v = sb("acc_v", [P, TOKENS])
    acc_k = sb("acc_k", [P, TOKENS])
    cur_v = sb("cur_v", [P, TOKENS])
    cur_k = sb("cur_k", [P, TOKENS])
    yT = sb("yT", [P, CH, TOKENS])
    psT = ps("a_psT", [P, 2, BLK])
    psY = ps("a_psY", [P, 2, BLK])
    var_ready, std_ready, normed = sem("a_var"), sem("a_std"), sem("a_normed")
    transposed, evacuated = sem("a_transposed"), sem("a_evacuated")
    chain, achain = sem("a_chain"), sem("a_achain")
    m_ready, par_ready, decay_ready, cur_ready = sem("a_m"), sem("a_par"), sem("a_decay"), sem("a_cur")
    ev_ready, scans_done, num_done = sem("a_ev"), sem("a_scans"), sem("a_num")
    y_ready, y_back, pool_ms = sem("a_y"), sem("a_yback"), sem("a_pool")
    y_added, par_in = sem("a_yadded"), sem("a_parin")

    with nc.Block() as block:
        @block.sync
        def _(sp):
            sp.dma_start(resid[:, :, :], g["x"].rearrange("(i p) d -> p i d", p=P)).then_inc(g["x_in"], 16)
            sp.dma_start(par[:, 0, :], g["td"]).then_inc(par_in, 16)
            sp.dma_start(par[:, 1, :], g["tf"]).then_inc(par_in, 16)
            sp.dma_start(ctxT[:, :, :], g["ctxT_d"].rearrange("(c p) t -> p c t", p=P)).then_inc(g["ctx_in"], 16)

        @block.gpsimd
        def _(pool):
            nc.gpsimd.memset(g["zeros"][:, :], 0.0).then_inc(g["zeros_ready"], 1)
            nc.gpsimd.memset(ident[:, :], 0.0).then_inc(pool_ms, 1)
            pool.wait_ge(pool_ms, 1)
            nc.gpsimd.affine_select(out=ident[:, :], in_=ident[:, :], compare_op=ALU.not_equal, fill=1.0,
                                    base=0, pattern=[[-1, P]], channel_multiplier=1).then_inc(g["ident_ready"], 1)
            pool.wait_ge(par_ready, 1)
            for c in range(CH):
                if c:
                    pool.wait_ge(scans_done, 2 * c)
                nc.gpsimd.memset(decay[:, :], 1.0).then_inc(pool_ms, 1)
                pool.wait_ge(pool_ms, 3 * c + 2)
                nc.gpsimd.tensor_scalar(decay[:, :], decay[:, :], par[:, 5, c:c + 1], None, ALU.mult).then_inc(pool_ms, 1)
                pool.wait_ge(pool_ms, 3 * c + 3)
                nc.gpsimd.memset(decay[:, :].rearrange("p (b t) -> p b t", t=SEQ)[:, :, 0], 0.0).then_inc(pool_ms, 1)
                pool.wait_ge(pool_ms, 3 * c + 4)
                pool.sem_inc(decay_ready, 1)
                pool.wait_ge(ev_ready, c + 1)
                if c:
                    pool.wait_ge(num_done, c)
                nc.gpsimd.tensor_scalar(cur_v[:, :], ev[:, c, :], par[:, 7, c:c + 1], None, ALU.mult)
                nc.gpsimd.tensor_scalar(cur_k[:, :], ek[:, c, :], par[:, 7, c:c + 1], None, ALU.mult).then_inc(cur_ready, 1)

        @block.scalar
        def _(act):
            norm_std(nc, act, work, var_ready, std_ready)
            act.wait_ge(par_in, 32)
            nc.scalar.activation(par[:, 4, :], par[:, 0, :], ACT.Exp).then_inc(achain, 1)
            act.wait_ge(achain, 1)
            nc.scalar.activation(par[:, 5, :], par[:, 4, :], ACT.Exp, scale=-1.0)
            act.wait_ge(m_ready, 1)
            nc.scalar.activation(par[:, 6, :], par[:, 2, :], ACT.Exp, scale=-1.0)
            nc.scalar.activation(par[:, 7, :], par[:, 3, :], ACT.Exp).then_inc(par_ready, 1)
            for i in range(TILES):
                act.wait_ge(transposed, i + 1)
                nc.scalar.activation(ek[:, :, i * P:(i + 1) * P],
                                     psT[:, i % 2, 0:DIM].rearrange("p (c t) -> p c t", c=CH),
                                     ACT.Exp).then_inc(evacuated, 1)

        @block.vector
        def _(dve):
            link = counter(dve, chain)
            dve.wait_ge(par_in, 32)
            link(nc.vector.tensor_scalar(par[:, 2, :], par[:, 1, :], 0.0, None, ALU.max))
            nc.vector.tensor_tensor(par[:, 3, :], par[:, 1, :], par[:, 2, :], ALU.subtract).then_inc(m_ready, 1)
            dve.wait_ge(g["x_in"], 16)
            norm_statistics(nc, dve, link, resid, stats, mv, work, var_ready, std_ready)
            for i in range(TILES):
                norm_tile(nc, dve, i, resid, xn, mv, work, normed, transposed)
            dve.wait_ge(g["ctx_in"], 16)
            dve.wait_ge(evacuated, TILES)
            for c in range(CH):
                nc.vector.tensor_tensor(ev[:, c, :], ek[:, c, :], ctxT[:, c, :], ALU.mult).then_inc(ev_ready, 1)
            for c in range(CH):
                dve.wait_ge(ev_ready, c + 1)
                dve.wait_ge(decay_ready, c + 1)
                nc.vector.tensor_tensor_scan(acc_v[:, :], decay[:, :], ev[:, c, :], 0.0, ALU.mult, ALU.add).then_inc(scans_done, 1)
                nc.vector.tensor_tensor_scan(acc_k[:, :], decay[:, :], ek[:, c, :], 0.0, ALU.mult, ALU.add).then_inc(scans_done, 1)
                dve.wait_ge(scans_done, 2 * c + 2)
                dve.wait_ge(cur_ready, c + 1)
                for cur, acc in ((cur_v, acc_v), (cur_k, acc_k)):
                    later = cur[:, :].rearrange("p (b t) -> p b t", t=SEQ)[:, :, 1:SEQ]
                    earlier = acc[:, :].rearrange("p (b t) -> p b t", t=SEQ)[:, :, 0:SEQ - 1]
                    last = nc.vector.scalar_tensor_tensor(later, earlier, par[:, 6, c:c + 1], later, ALU.mult, ALU.add)
                link(last)
                link(nc.vector.reciprocal(cur_k[:, :], cur_k[:, :]))
                link(nc.vector.tensor_tensor(yT[:, c, :], cur_v[:, :], cur_k[:, :], ALU.mult))
                nc.vector.tensor_copy(yT[:, c, :].rearrange("p (b t) -> p b t", t=SEQ)[:, :, 0],
                                      ctxT[:, c, :].rearrange("p (b t) -> p b t", t=SEQ)[:, :, 0]).then_inc(num_done, 1)
            for i in range(TILES):
                dve.wait_ge(y_back, i + 1)
                nc.vector.tensor_tensor(resid[:, i, :], psY[:, i % 2, 0:DIM], resid[:, i, :], ALU.add).then_inc(y_added, 1)

        @block.tensor
        def _(pe):
            pe.wait_ge(g["ident_ready"], 1)
            for i in range(TILES):
                transpose_tile(nc, pe, i, xn, psT, ident, normed, transposed, evacuated)
            pe.wait_ge(num_done, CH)
            for i in range(TILES):
                if i >= 2:
                    pe.wait_ge(y_added, i - 1)
                for c in range(CH):
                    last = nc.tensor.transpose(psY[:, i % 2, c * P:(c + 1) * P], yT[:, c, i * P:(i + 1) * P], ident[:, :])
                last.then_inc(y_back, 1)


def stage_product_keys(nc, ctx, sem, sb, ps, g):
    resid, ident, xn = g["resid"], g["ident"], g["xn"]
    stats, mv, work = g["stats"], g["mv"], g["work"]
    G8 = 2 * PK_HEADS
    PICKS = PK_HEADS * PK_TOP
    TPG = P // PICKS
    GROUPS = TOKENS // TPG
    GPT = P // TPG
    HALF = GPT // 2
    xnT = g["xnT"]
    nsel = TILES * PK_HEADS
    downT = sb("pk_downT", [P, CH, PK_EXPERTS])
    up = sb("pk_up", [P, PK_ROWS, DIM])
    iota128 = sb("pk_iota128", [P, P])
    rowtab = sb("pk_rowtab", [P, PK_ROWS, TPG])
    packed = sb("pk_packed", [P, 3, TILES, PICKS])
    choice = ctx.enter_context(ExitStack())

    def first(name, shape, dtype=F32):
        return choice.enter_context(nc.sbuf_tensor(name, shape, dtype))

    wqT = first("pk_wqT", [PK_DK, G8, DIM])
    keysT = first("pk_keysT", [PK_DK, G8, PK_KEYS])
    mix = first("pk_mix", [P, CH, G8 * PK_KEYS])
    top_v = first("pk_top_v", [P, 2, G8, PK_TOP])
    top_i = first("pk_top_i", [P, TILES, G8, PK_TOP], U32)
    sums = first("pk_sums", [P, PK_HEADS, PK_TOP, PK_TOP])
    best = first("pk_best", [P, TILES, PK_HEADS, PK_TOP])
    best_i = first("pk_best_i", [P, TILES, PK_HEADS, PK_TOP], U32)
    iota8 = first("pk_iota8", [P, PK_TOP])
    top_f = first("pk_top_f", [P, nsel, 2, PK_TOP])
    pos_u = first("pk_pos_u", [P, 2, nsel * PK_TOP], U32)
    pos_f = first("pk_pos_f", [P, 2, nsel, PK_TOP])
    picked = first("pk_picked", [P, 2, nsel * PK_TOP])
    onehot = first("pk_onehot", [P, nsel // 2 * PK_TOP * PK_TOP])
    scratch = nc.dram_tensor("pk_scratch", (3, TOKENS, PICKS), F32, kind="Internal").ap()

    s = {n: sem("b_" + n) for n in (
        "var std normed transposed evacuated chain w_in wide_in mix_ready mix_copied scored scores_used "
        "packed_ready packed_out rows_in rows_tr groups_ready iotas col_ready row_ready spread down_done act_ready hid_ready "
        "hid_used out_done added pool_chain act_used").split()}
    sc = ctx.enter_context(ExitStack())
    psT = sc.enter_context(nc.psum_tensor("b_psT", [P, 2, BLK], F32))
    psS = sc.enter_context(nc.psum_tensor("b_psS", [P, 2, G8 * PK_KEYS], F32))
    with nc.Block() as block:
        @block.sync
        def _(sp):
            sp.dma_start(wqT[:, :, :], g["pk_wqT_d"].rearrange("(q p) c -> p q c", p=PK_DK)).then_inc(s["w_in"], 16)
            sp.dma_start(keysT[:, :, :], g["pk_keysT_d"].rearrange("(q p) k -> p q k", p=PK_DK)).then_inc(s["w_in"], 16)
            sp.dma_start(downT[:, :, :], g["pk_downT_d"].rearrange("(c p) e -> p c e", p=P)).then_inc(s["wide_in"], 16)
            sp.dma_start(up[:, :, :], g["pk_up_d"].rearrange("(r p) c -> p r c", p=P)).then_inc(s["wide_in"], 16)

        @block.gpsimd
        def _(pool):
            for table, pattern in ((iota8, [[1, PK_TOP]]), (iota128, [[1, P]])):
                nc.gpsimd.iota(table[:, :], pattern, base=0, channel_multiplier=0,
                               allow_small_or_imprecise_dtypes=True).then_inc(s["iotas"], 1)
            nc.gpsimd.iota(rowtab[:, :, :], [[1, PK_ROWS], [0, TPG]], base=0, channel_multiplier=0,
                           allow_small_or_imprecise_dtypes=True).then_inc(s["pool_chain"], 1)
            pool.wait_ge(s["pool_chain"], 1)
            nc.gpsimd.affine_select(out=rowtab[:, :, :], in_=rowtab[:, :, :], compare_op=ALU.is_ge, fill=-1.0,
                                    base=0, pattern=[[0, PK_ROWS], [-PICKS, TPG]], channel_multiplier=1).then_inc(s["pool_chain"], 1)
            pool.wait_ge(s["pool_chain"], 2)
            nc.gpsimd.affine_select(out=rowtab[:, :, :], in_=rowtab[:, :, :], compare_op=ALU.is_ge, fill=-1.0,
                                    base=PICKS - 1, pattern=[[0, PK_ROWS], [PICKS, TPG]], channel_multiplier=-1).then_inc(s["iotas"], 1)

        @block.scalar
        def _(act):
            norm_std(nc, act, work, s["var"], s["std"])
            act.wait_ge(s["mix_ready"], 1)
            for c in range(CH):
                last = nc.scalar.activation(mix[:, c, :], psS[:, c, :], ACT.Copy)
            last.then_inc(s["mix_copied"], 1)
            for i in range(TILES):
                act.wait_ge(s["transposed"], i + 1)
                nc.scalar.activation(xnT[:, :, i * P:(i + 1) * P],
                                     psT[:, i % 2, 0:DIM].rearrange("p (c t) -> p c t", c=CH),
                                     ACT.Copy).then_inc(s["evacuated"], 1)

        @block.vector
        def _(dve):
            link = counter(dve, s["chain"])
            norm_statistics(nc, dve, link, resid, stats, mv, work, s["var"], s["std"])
            for i in range(2):
                norm_tile(nc, dve, i, resid, xn, mv, work, s["normed"], s["transposed"])
            for i in range(TILES):
                if i + 2 < TILES:
                    norm_tile(nc, dve, i + 2, resid, xn, mv, work, s["normed"], s["transposed"])
                dve.wait_ge(s["scored"], i + 1)
                part = psS[:, i % 2, :].rearrange("p (g k) -> p g k", g=G8)
                tv = top_v[:, i % 2, :, :]
                for q in range(G8):
                    last = nc.vector.max(tv[:, q, :], part[:, q, :])
                link(last)
                for q in range(G8):
                    last = nc.vector.max_index(top_i[:, i, q, :], tv[:, q, :], part[:, q, :])
                last.then_inc(s["scores_used"], 1)
                pair = tv.rearrange("p (h z) k -> p h z k", z=2)
                link(nc.vector.tensor_tensor(sums[:, :, :, :],
                                             pair[:, :, 0, :].unsqueeze(3).to_broadcast([P, PK_HEADS, PK_TOP, PK_TOP]),
                                             pair[:, :, 1, :].unsqueeze(2).to_broadcast([P, PK_HEADS, PK_TOP, PK_TOP]), ALU.add))
                flat = sums[:, :, :, :].rearrange("p h a b -> p h (a b)")
                for h in range(PK_HEADS):
                    last = nc.vector.max(best[:, i, h, :], flat[:, h, :])
                link(last)
                for h in range(PK_HEADS):
                    last = nc.vector.max_index(best_i[:, i, h, :], best[:, i, h, :], flat[:, h, :])
                link(last)
            bi = best_i[:, :, :, :].rearrange("p i h k -> p (i h k)")
            link(nc.vector.tensor_scalar(pos_u[:, 0, :], bi, 3, None, ALU.logical_shift_right))
            link(nc.vector.tensor_scalar(pos_u[:, 1, :], bi, PK_TOP - 1, None, ALU.bitwise_and))
            link(nc.vector.tensor_copy(pos_f[:, :, :, :].rearrange("p z n k -> p (z n k)"), pos_u[:, :, :].rearrange("p z n -> p (z n)")))
            link(nc.vector.tensor_copy(top_f[:, :, :, :].rearrange("p n z k -> p (n z k)"),
                                       top_i[:, :, :, :].rearrange("p i g k -> p (i g k)")))
            dve.wait_ge(s["iotas"], 3)
            hot = onehot[:, :].rearrange("p (n k a) -> p n k a", k=PK_TOP, a=PK_TOP)
            for z in range(2):
                for q in range(nsel // 32):
                    n0 = 32 * q
                    shape = [P, 32, PK_TOP, PK_TOP]
                    flat3 = [P, 32 * PK_TOP, PK_TOP]
                    hotf = hot.rearrange("p n k a -> p (n k) a")
                    link(nc.vector.tensor_tensor(hotf, pos_f[:, z, n0:n0 + 32, :].rearrange("p n k -> p (n k)").unsqueeze(2).to_broadcast(flat3),
                                                 iota8[:, :].unsqueeze(1).to_broadcast(flat3), ALU.is_equal))
                    link(nc.vector.tensor_tensor(hot, hot, top_f[:, n0:n0 + 32, z, :].unsqueeze(2).to_broadcast(shape), ALU.mult))
                    link(nc.vector.reduce_sum(picked[:, z, n0 * PK_TOP:(n0 + 32) * PK_TOP].unsqueeze(2), hotf, AX.X))
            link(nc.vector.scalar_tensor_tensor(picked[:, 0, :], picked[:, 0, :], float(PK_KEYS), picked[:, 1, :], ALU.mult, ALU.add))
            link(nc.vector.tensor_scalar(pos_u[:, 0, :], picked[:, 0, :], float(PK_EXPERTS - 1), None, ALU.min))
            link(nc.vector.tensor_scalar(pos_u[:, 1, :], pos_u[:, 0, :], 7, None, ALU.logical_shift_right))
            link(nc.vector.tensor_copy(packed[:, 0, :, :].rearrange("p i k -> p (i k)"), pos_u[:, 1, :]))
            link(nc.vector.tensor_scalar(pos_u[:, 1, :], pos_u[:, 0, :], P - 1, None, ALU.bitwise_and))
            link(nc.vector.tensor_copy(packed[:, 1, :, :].rearrange("p i k -> p (i k)"), pos_u[:, 1, :]))
            nc.vector.tensor_scalar(packed[:, 2, :, :].rearrange("p i k -> p (i k)"),
                                    best[:, :, :, :].rearrange("p i h k -> p (i h k)"), 0.0, None, ALU.max).then_inc(s["packed_ready"], 1)

        @block.tensor
        def _(pe):
            pe.wait_ge(s["w_in"], 32)
            for c in range(CH):
                for q in range(G8):
                    last = nc.tensor.matmul(psS[:, c, q * PK_KEYS:(q + 1) * PK_KEYS], wqT[:, q, c * P:(c + 1) * P],
                                            keysT[:, q, :], start=True, stop=True)
            last.then_inc(s["mix_ready"], 1)
            for i in range(TILES + 1):
                if i < TILES:
                    transpose_tile(nc, pe, i, xn, psT, ident, s["normed"], s["transposed"], s["evacuated"])
                if i == 0:
                    pe.wait_ge(s["mix_copied"], 1)
                    continue
                j = i - 1
                pe.wait_ge(s["evacuated"], j + 1)
                if j >= 2:
                    pe.wait_ge(s["scores_used"], j - 1)
                for n in range(2):
                    for c in range(CH):
                        last = nc.tensor.matmul(psS[:, j % 2, n * BLK:(n + 1) * BLK], xnT[:, c, j * P:(j + 1) * P],
                                                mix[:, c, n * BLK:(n + 1) * BLK], start=(c == 0), stop=(c == CH - 1))
                last.then_inc(s["scored"], 1)

    choice.close()
    rows = sb("pk_rows", [P, 3, GROUPS // P, P])
    groups = sb("pk_groups", [P, 3, GROUPS])
    colhot = sb("pk_colhot", [P, 2, HALF, P])
    rowhot = sb("pk_rowhot", [P, 2, HALF, PK_ROWS * TPG])
    act_d = sb("pk_act", [P, PK_ROWS, BLK])
    hid = sb("pk_hid", [P, PK_ROWS, P])
    sc.close()
    sc = ctx.enter_context(ExitStack())
    psR = sc.enter_context(nc.psum_tensor("b_psR", [P, BLK], F32))
    psD = sc.enter_context(nc.psum_tensor("b_psD", [P, 2, BLK], F32))
    psG = sc.enter_context(nc.psum_tensor("b_psG", [P, GPT, PK_ROWS, TPG], F32))
    psO = sc.enter_context(nc.psum_tensor("b_psO", [P, BLK], F32))
    with nc.Block() as block:
        @block.sync
        def _(sp):
            sp.wait_ge(s["packed_ready"], 1)
            for v in range(3):
                sp.dma_start(scratch[v].rearrange("(i p) k -> p i k", p=P), packed[:, v, :, :]).then_inc(s["packed_out"], 16)
            sp.wait_ge(s["packed_out"], 48)
            for v in range(3):
                sp.dma_start(rows[:, v, :, :],
                             scratch[v].rearrange("(j p t) k -> p j (t k)", p=P, t=TPG)).then_inc(s["rows_in"], 16)
            sp.wait_ge(g["zeros_ready"], 1)
            sp.dma_start(g["sorted_x"].rearrange("(n p) d -> p n d", p=P),
                         g["zeros"][:, :].unsqueeze(1).to_broadcast([P, BLOCKS, DIM])).then_inc(g["zeroed"], 16)

        @block.vector
        def _(dve):
            link = counter(dve, s["hid_used"])
            for v in range(3):
                dve.wait_ge(s["rows_tr"], v + 1)
                nc.vector.tensor_copy(groups[:, v, :], psR[:, :]).then_inc(s["groups_ready"], 1)
            dve.wait_ge(s["groups_ready"], 3)

            def hot_tables(i):
                for q in range(2):
                    n = 2 * i + q
                    if n >= 2:
                        dve.wait_ge(s["spread"], n - 1)
                    g0 = i * GPT + q * HALF
                    shape = [P, HALF, PK_ROWS * TPG]
                    tab = rowtab[:, :, :].rearrange("p r t -> p (r t)").unsqueeze(1).to_broadcast(shape)
                    link(nc.vector.tensor_tensor(rowhot[:, q, :, :], tab,
                                                 groups[:, 0, g0:g0 + HALF].unsqueeze(2).to_broadcast(shape), ALU.is_equal))
                    nc.vector.tensor_tensor(rowhot[:, q, :, :], rowhot[:, q, :, :],
                                            groups[:, 2, g0:g0 + HALF].unsqueeze(2).to_broadcast(shape), ALU.mult).then_inc(s["row_ready"], 1)

            hot_tables(0)
            for i in range(TILES):
                if i + 1 < TILES:
                    hot_tables(i + 1)
                blk = i * P // BLK
                dve.wait_ge(s["act_ready"], (blk + 1) * PK_ROWS)
                dve.wait_ge(s["spread"], 2 * i + 2)
                if i:
                    dve.wait_ge(s["out_done"], i)
                off = i * P % BLK
                for r in range(PK_ROWS):
                    last = nc.vector.tensor_tensor(hid[:, r, :].rearrange("p (g t) -> p g t", t=TPG), psG[:, :, r, :],
                                                   act_d[:, r, off:off + P].rearrange("p (g t) -> p g t", t=TPG), ALU.mult)
                last.then_inc(s["hid_ready"], 1)
                dve.wait_ge(s["out_done"], i + 1)
                nc.vector.tensor_tensor(resid[:, i, :], psO[:, 0:DIM], resid[:, i, :], ALU.add).then_inc(s["added"], 1)

        @block.gpsimd
        def _(pool):
            pool.wait_ge(s["groups_ready"], 3)
            for n in range(2 * TILES):
                if n >= 2:
                    pool.wait_ge(s["spread"], n - 1)
                g0 = n * HALF
                for k in range(HALF):
                    last = nc.gpsimd.tensor_scalar(colhot[:, n % 2, k, :], iota128[:, :], groups[:, 1, g0 + k:g0 + k + 1], None,
                                                   ALU.is_equal)
                last.then_inc(s["col_ready"], 1)

        @block.scalar
        def _(act):
            for n in range(BLKS * PK_ROWS):
                blk, r = n // PK_ROWS, n % PK_ROWS
                act.wait_ge(s["down_done"], n + 1)
                if r == 0 and blk:
                    act.wait_ge(s["hid_ready"], blk * BLK // P)
                nc.scalar.activation(act_d[:, r, :], psD[:, n % 2, :], ACT.Silu).then_inc(s["act_ready"], 1)

        @block.tensor
        def _(pe):
            pe.wait_ge(s["rows_in"], 48)
            for v in range(3):
                if v:
                    pe.wait_ge(s["groups_ready"], v)
                for j in range(GROUPS // P):
                    last = nc.tensor.transpose(psR[:, j * P:(j + 1) * P], rows[:, v, j, :], ident[:, :])
                last.then_inc(s["rows_tr"], 1)
            pe.wait_ge(s["wide_in"], 32)
            for i in range(TILES):
                blk = i * P // BLK
                if i * P % BLK == 0:
                    for r in range(PK_ROWS):
                        n = blk * PK_ROWS + r
                        if n >= 2:
                            pe.wait_ge(s["act_ready"], n - 1)
                        for c in range(CH):
                            last = nc.tensor.matmul(psD[:, n % 2, :], downT[:, c, r * P:(r + 1) * P],
                                                    xnT[:, c, blk * BLK:(blk + 1) * BLK], start=(c == 0), stop=(c == CH - 1))
                        last.then_inc(s["down_done"], 1)
                if i:
                    pe.wait_ge(s["hid_ready"], i)
                for q in range(2):
                    pe.wait_ge(s["col_ready"], 2 * i + q + 1)
                    pe.wait_ge(s["row_ready"], 2 * i + q + 1)
                    for k in range(HALF):
                        last = nc.tensor.matmul(psG[:, q * HALF + k, :, :].rearrange("p r t -> p (r t)"), colhot[:, q, k, :],
                                                rowhot[:, q, k, :], start=True, stop=True)
                    last.then_inc(s["spread"], 1)
                pe.wait_ge(s["hid_ready"], i + 1)
                if i:
                    pe.wait_ge(s["added"], i)
                for r in range(PK_ROWS):
                    last = nc.tensor.matmul(psO[:, 0:DIM], hid[:, r, :], up[:, r, :], start=(r == 0), stop=(r == PK_ROWS - 1))
                last.then_inc(s["out_done"], 1)
    sc.close()


def stage_attention(nc, ctx, sem, sb, ps, g):
    resid, ctxT, xnT, ident, xn = g["resid"], g["ctxT"], g["xnT"], g["ident"], g["xn"]
    stats, mv, work = g["stats"], g["mv"], g["work"]
    PAIRS = HEADS // 2
    K3 = 3 * HD
    PADDED = 64
    identb = sb("c_identb", [P, P], BF16)
    qT = sb("c_qT", [P, PAIRS, TOKENS], BF16)
    kT = sb("c_kT", [P, PAIRS, TOKENS], BF16)
    values = sb("c_values", [P, TILES, DIM], BF16)
    heads_out = sb("c_heads_out", [P, TILES, DIM])
    wp = sb("c_wp", [P, CH, DIM])
    bp = sb("c_bp", [P, DIM])
    v_scale = sb("c_v_scale", [P, CH, 3])
    q_scale = sb("c_q_scale", [P, HEADS, TILES])
    scratch = ctx.enter_context(ExitStack())

    def first(name, shape, dtype=F32):
        return scratch.enter_context(nc.sbuf_tensor(name, shape, dtype))

    wq = first("c_wq", [P, CH, DIM])
    wkv = first("c_wkv", [P, CH, 2 * DIM])
    bq = first("c_bq", [P, 2 * DIM])
    bv = first("c_bv", [P, CH])
    vT = first("c_vT", [P, CH, TOKENS])
    v_int = first("c_v_int", [P, CH, TOKENS], BF16)
    qk = first("c_qk", [P, 2, 2, HEADS, HD])
    amax = first("c_amax", [P, 2, 3, 2, HEADS])
    khat = first("c_khat", [P, 3, HEADS, HD])
    qrows = first("c_qrows", [P, 2, HEADS, PADDED], BF16)
    krows = first("c_krows", [P, 2, HEADS, PADDED], BF16)

    s = {n: sem("c_" + n) for n in (
        "var std normed transposed evacuated chain w_in late_in projected v_mm v_copied v_ready v_tr v_back "
        "rows_ready rows_tr rows_back consts pool_chain qk_free q_loaded scale_neg scored s_taken bias_ready exp_done "
        "rounded p_tr p_back pv_done normalised bchain inverted o_tr o_back out_done added scale_ready pair_free").split()}
    sc = ctx.enter_context(ExitStack())
    psT = sc.enter_context(nc.psum_tensor("c_psT", [P, 2, BLK], F32))
    psQ = sc.enter_context(nc.psum_tensor("c_psQ", [P, 2, BLK], F32))
    psV = sc.enter_context(nc.psum_tensor("c_psV", [P, 2, BLK], F32))
    psR = sc.enter_context(nc.psum_tensor("c_psR", [P, 2, PAIRS, P], BF16))
    with nc.Block() as block:
        @block.sync
        def _(sp):
            sp.dma_start(wkv[:, :, :], g["wkv_d"].rearrange("(c p) n -> p c n", p=P)).then_inc(s["w_in"], 16)
            sp.dma_start(bv[:, :], g["bv_d"]).then_inc(s["w_in"], 16)
            sp.dma_start(wq[:, :, :], g["wq_d"].rearrange("(c p) n -> p c n", p=P)).then_inc(s["w_in"], 16)
            sp.dma_start(bq[:, 0:DIM], g["bq_d"].to_broadcast([P, DIM])).then_inc(s["w_in"], 16)
            sp.dma_start(bq[:, DIM:], g["bkv_d"][:, 0:DIM].to_broadcast([P, DIM])).then_inc(s["w_in"], 16)
            sp.dma_start(bp[:, :], g["bp_d"].to_broadcast([P, DIM])).then_inc(s["late_in"], 16)
            sp.dma_start(wp[:, :, :], g["wp_d"].rearrange("(c p) n -> p c n", p=P)).then_inc(s["late_in"], 16)

        @block.gpsimd
        def _(pool):
            nc.gpsimd.tensor_copy(identb[:, :], ident[:, :])
            nc.gpsimd.memset(qrows[:, :, :, :], 0.0)
            nc.gpsimd.memset(krows[:, :, :, :], 0.0).then_inc(s["consts"], 1)

        def store_rows(i, act):
            for n, dst in ((2 * i, qT), (2 * i + 1, kT)):
                act.wait_ge(s["rows_tr"], n + 1)
                nc.scalar.activation(dst[:, :, i * P:(i + 1) * P], psR[:, n % 2, :, :], ACT.Copy).then_inc(s["rows_back"], 1)

        @block.scalar
        def _(act):
            act.wait_ge(s["w_in"], 80)
            for n in range(CH * BLKS):
                c, b = n // BLKS, n % BLKS
                act.wait_ge(s["v_mm"], n + 1)
                nc.scalar.activation(vT[:, c, b * BLK:(b + 1) * BLK], psV[:, n % 2, :], ACT.Identity,
                                     bias=bv[:, c:c + 1]).then_inc(s["v_copied"], 1)
            norm_std(nc, act, work, s["var"], s["std"])
            for i in range(TILES):
                act.wait_ge(s["transposed"], i + 1)
                nc.scalar.activation(xnT[:, :, i * P:(i + 1) * P],
                                     psT[:, i % 2, 0:DIM].rearrange("p (c t) -> p c t", c=CH),
                                     ACT.Copy).then_inc(s["evacuated"], 1)
                if i:
                    store_rows(i - 1, act)
            store_rows(TILES - 1, act)

        @block.vector
        def _(dve):
            link = counter(dve, s["chain"])
            norm_statistics(nc, dve, link, resid, stats, mv, work, s["var"], s["std"])
            for i in range(2):
                norm_tile(nc, dve, i, resid, xn, mv, work, s["normed"], s["transposed"])
            dve.wait_ge(s["v_copied"], CH * BLKS)
            for c in range(CH):
                last = nc.vector.tensor_reduce(v_scale[:, c, 0:1], vT[:, c, :], AX.X, ALU.max, apply_absolute_value=True)
            link(last)
            link(nc.vector.tensor_scalar(v_scale[:, :, 1], v_scale[:, :, 0], 1.0 / 127.0, 1e-8, ALU.mult, ALU.max))
            link(nc.vector.reciprocal(v_scale[:, :, 2], v_scale[:, :, 1]))
            for c in range(CH):
                last = nc.vector.tensor_scalar(vT[:, c, :], vT[:, c, :], v_scale[:, c, 2:3], ROUND, ALU.mult, ALU.add)
            link(last)
            for c in range(CH):
                nc.vector.tensor_scalar(v_int[:, c, :], vT[:, c, :], ROUND, None, ALU.subtract).then_inc(s["v_ready"], 1)
            dve.wait_ge(s["late_in"], 32)
            for c in range(CH):
                nc.vector.tensor_scalar(wp[:, c, :], wp[:, c, :], v_scale[:, c, 1:2], None, ALU.mult)
            dve.wait_ge(s["consts"], 1)
            for i in range(TILES):
                if i + 2 < TILES:
                    norm_tile(nc, dve, i + 2, resid, xn, mv, work, s["normed"], s["transposed"])
                u = i % 2
                t = qk[:, u, :, :, :]
                tf = t.rearrange("p z h d -> p z (h d)")
                dve.wait_ge(s["projected"], i + 1)
                link(nc.vector.tensor_tensor(t.rearrange("p z h d -> p (z h d)"), psQ[:, u, :], bq[:, :], ALU.add))
                m = amax[:, u, :, :, :]
                link(nc.vector.tensor_reduce(m[:, 0, :, :], t, AX.X, ALU.max, apply_absolute_value=True))
                nc.vector.tensor_scalar(m[:, 1, 0, :], m[:, 0, 0, :], 0.25 / 127.0, 1e-8, ALU.mult, ALU.max)
                link(nc.vector.tensor_scalar(m[:, 1, 1, :], m[:, 0, 1, :], 1.0 / 127.0, 1e-8, ALU.mult, ALU.max))
                link(nc.vector.reciprocal(m[:, 2, :, :], m[:, 1, :, :]))
                nc.vector.tensor_copy(q_scale[:, :, i], m[:, 1, 0, :])
                link(nc.vector.tensor_scalar(m[:, 2, 0, :], m[:, 2, 0, :], 0.25, None, ALU.mult))
                link(nc.vector.tensor_tensor(t, t, m[:, 2, :, :].unsqueeze(3).to_broadcast([P, 2, HEADS, HD]), ALU.mult))
                link(nc.vector.tensor_scalar(tf, tf, ROUND, ROUND, ALU.add, ALU.subtract))
                if i >= 2:
                    dve.wait_ge(s["rows_tr"], 2 * i - 2)
                qd = qrows[:, u, :, 0:K3].rearrange("p h (j d) -> p h j d", j=3)
                nc.vector.tensor_copy(qd, t[:, 0, :, :].unsqueeze(2).to_broadcast([P, HEADS, 3, HD])).then_inc(s["rows_ready"], 1)
                link(nc.vector.tensor_tensor(khat[:, 0, :, :], t[:, 1, :, :],
                                             m[:, 1, 1, :].unsqueeze(2).to_broadcast([P, HEADS, HD]), ALU.mult))
                for part in range(3):
                    kp = krows[:, u, :, part * HD:(part + 1) * HD]
                    copy = nc.vector.tensor_copy(kp, khat[:, part, :, :])
                    if part == 2:
                        copy.then_inc(s["rows_ready"], 1)
                    else:
                        link(copy)
                        link(nc.vector.tensor_tensor(khat[:, part + 1, :, :], khat[:, part, :, :], kp, ALU.subtract))
            for i in range(TILES):
                dve.wait_ge(s["v_tr"], i + 1)
                nc.vector.tensor_copy(values[:, i, :], psV[:, i % 2, 0:P].bitcast(BF16)).then_inc(s["v_back"], 1)

        @block.tensor
        def _(pe):
            pe.wait_ge(s["w_in"], 80)
            for n in range(CH * BLKS):
                c, b = n // BLKS, n % BLKS
                if n >= 2:
                    pe.wait_ge(s["v_copied"], n - 1)
                for k in range(CH):
                    last = nc.tensor.matmul(psV[:, n % 2, :], wkv[:, k, DIM + c * P:DIM + (c + 1) * P],
                                            ctxT[:, k, b * BLK:(b + 1) * BLK], start=(k == 0), stop=(k == CH - 1))
                last.then_inc(s["v_mm"], 1)
            pe.wait_ge(s["consts"], 1)

            def rows_of(i):
                for n, src in ((2 * i, qrows), (2 * i + 1, krows)):
                    pe.wait_ge(s["rows_ready"], n + 1)
                    if n >= 2:
                        pe.wait_ge(s["rows_back"], n - 1)
                    for p in range(PAIRS):
                        last = nc.tensor.transpose(psR[:, n % 2, p, :],
                                                   src[:, i % 2, 2 * p:2 * p + 2, :].rearrange("p h d -> p (h d)"), identb[:, :])
                    last.then_inc(s["rows_tr"], 1)

            for i in range(TILES):
                transpose_tile(nc, pe, i, xn, psT, ident, s["normed"], s["transposed"], s["evacuated"])
                pe.wait_ge(s["evacuated"], i + 1)
                if i >= 2:
                    pe.wait_ge(s["rows_ready"], 2 * i - 2)
                for z in range(2):
                    src, w = ((xnT, wq), (ctxT, wkv))[z]
                    for k in range(CH):
                        last = nc.tensor.matmul(psQ[:, i % 2, z * DIM:(z + 1) * DIM], src[:, k, i * P:(i + 1) * P],
                                                w[:, k, 0:DIM], start=(k == 0), stop=(k == CH - 1))
                last.then_inc(s["projected"], 1)
                if i:
                    rows_of(i - 1)
            rows_of(TILES - 1)
            pe.wait_ge(s["v_ready"], CH)
            for i in range(TILES):
                if i >= 2:
                    pe.wait_ge(s["v_back"], i - 1)
                for c in range(CH):
                    last = nc.tensor.transpose(psV[:, i % 2, 0:P].bitcast(BF16)[:, c * P:(c + 1) * P],
                                               v_int[:, c, i * P:(i + 1) * P], identb[:, :])
                last.then_inc(s["v_tr"], 1)

    sc.close()
    scratch.close()
    qh = sb("c_qh", [P, TOKENS], BF16)
    kh = sb("c_kh", [P, TOKENS], BF16)
    sq = sb("c_sq", [P, 2, TILES, 2])
    scores = sb("c_scores", [P, 2, TOKENS])
    exps = sb("c_exps", [P, 2, TOKENS])
    probs = sb("c_probs", [P, 2, TOKENS], BF16)
    probsT = sb("c_probsT", [P, 2, TILES, P], BF16)
    row = sb("c_row", [P, 4, 6])
    UNITS = 2 * TILES
    HALFW = TOKENS // 2
    TR, PV = 2, 3
    sc = ctx.enter_context(ExitStack())
    psS = sc.enter_context(nc.psum_tensor("c_psS", [P, 2, HALFW], F32))
    psP = sc.enter_context(nc.psum_tensor("c_psP", [P, TILES, P], BF16))
    psO = sc.enter_context(nc.psum_tensor("c_psO", [P, 2, BLK], F32))
    with nc.Block() as block:
        @block.tensor
        def _(pe):
            for credited in ("s_taken", "p_back", "normalised"):
                pe.sem_inc(s[credited], 1)
            with pe.Fori(0, PAIRS) as p:
                base = p * UNITS
                pe.wait_ge(s["q_loaded"], p + 1)
                for n in range(UNITS + PV):
                    if n < UNITS:
                        u, i = n // TILES, n % TILES
                        r0 = PADDED * u
                        for half in range(2):
                            pe.wait_ge(s["s_taken"], (base + n) * 2 + half if n or half else base * 2 + 1)
                            for b in range(2):
                                k0 = half * HALFW + b * BLK
                                last = nc.tensor.matmul(psS[:, half, b * BLK:(b + 1) * BLK], qh[r0:r0 + K3, i * P:(i + 1) * P],
                                                        kh[r0:r0 + K3, k0:k0 + BLK],
                                                        start=True, stop=True)
                            last.then_inc(s["scored"], 1)
                    m = n - TR
                    if 0 <= m < UNITS:
                        pe.wait_ge(s["rounded"], base + m + 1)
                        pe.wait_ge(s["p_back"], base + m + 1)
                        for c in range(TILES):
                            last = nc.tensor.transpose(psP[:, c, :], probs[:, m % 2, c * P:(c + 1) * P], identb[:, :])
                        last.then_inc(s["p_tr"], 1)
                    m = n - PV
                    if m >= 0:
                        u = m // TILES
                        pe.wait_ge(s["normalised"], base + m if m else base + 1)
                        pe.wait_ge(s["p_back"], base + m + 2)
                        for c in range(TILES):
                            last = nc.tensor.matmul(psO[:, m % 2, 0:HD], probsT[:, m % 2, c, :],
                                                    values[:, c, bass.ds((p * 2 + u) * HD, HD)],
                                                    start=(c == 0), stop=(c == TILES - 1))
                        last.then_inc(s["pv_done"], 1)

        @block.gpsimd
        def _(pool):
            pool.sem_inc(s["pair_free"], 1)
            with pool.Fori(0, PAIRS) as p:
                pool.wait_ge(s["pair_free"], p + 1)
                nc.gpsimd.tensor_copy(qh[:, :], qT[:, bass.ds(p, 1), :].rearrange("p a t -> p (a t)"))
                nc.gpsimd.tensor_copy(kh[:, :], kT[:, bass.ds(p, 1), :].rearrange("p a t -> p (a t)")).then_inc(s["q_loaded"], 1)
                nc.gpsimd.tensor_copy(sq[:, 0, :, :], q_scale[:, bass.ds(p * 2, 2), :].rearrange("p h i -> p i h")).then_inc(s["pool_chain"], 1)
                pool.wait_ge(s["pool_chain"], p + 1)
                pool.sem_inc(s["scale_ready"], 1)

        @block.scalar
        def _(act):
            with act.Fori(0, PAIRS) as p:
                base = p * UNITS
                act.wait_ge(s["scale_ready"], p + 1)
                for n in range(UNITS + TR):
                    if n < UNITS:
                        u, i = n // TILES, n % TILES
                        act.wait_ge(s["bias_ready"], base + n + 1)
                        if n >= 2:
                            act.wait_ge(s["rounded"], base + n - 1)
                        nc.scalar.activation(exps[:, n % 2, :], scores[:, n % 2, :], ACT.Exp, bias=row[:, n % 4, 3:4],
                                             scale=sq[:, 0, i, u:u + 1], accum_out=row[:, n % 4, 4:5]).then_inc(s["exp_done"], 1)
                    m = n - TR
                    if m >= 0:
                        act.wait_ge(s["p_tr"], base + m + 1)
                        if m >= 2:
                            act.wait_ge(s["pv_done"], base + m - 1)
                        nc.scalar.activation(probsT[:, m % 2, :, :], psP[:, :, :], ACT.Copy).then_inc(s["p_back"], 1)

        @block.vector
        def _(dve):
            with dve.Fori(0, PAIRS) as p:
                base = p * UNITS
                dve.wait_ge(s["scale_ready"], p + 1)
                nc.vector.tensor_scalar(sq[:, 1, :, :], sq[:, 0, :, :], -1.0, None, ALU.mult).then_inc(s["scale_neg"], 1)
                dve.wait_ge(s["scale_neg"], p + 1)
                for n in range(UNITS + PV):
                    if n < UNITS:
                        u, i = n // TILES, n % TILES
                        r = row[:, n % 4, :]
                        if n >= 2:
                            dve.wait_ge(s["exp_done"], base + n - 1)
                        for half in range(2):
                            dve.wait_ge(s["scored"], (base + n) * 2 + half + 1)
                            nc.vector.tensor_scalar(scores[:, n % 2, half * HALFW:(half + 1) * HALFW], psS[:, half, :], 0.0, -3.0e38,
                                                    ALU.add, ALU.max, accum_out=r[:, half:half + 1]).then_inc(s["s_taken"], 1)
                        dve.wait_ge(s["s_taken"], (base + n) * 2 + 3)
                        nc.vector.tensor_tensor(r[:, 2:3], r[:, 0:1], r[:, 1:2], ALU.max).then_inc(s["bchain"], 1)
                        dve.wait_ge(s["bchain"], base + n + 1)
                        nc.vector.tensor_scalar(r[:, 3:4], r[:, 2:3], sq[:, 1, i, u:u + 1], LN255, ALU.mult, ALU.add).then_inc(s["bias_ready"], 1)
                    m = n - 1
                    if 0 <= m < UNITS:
                        dve.wait_ge(s["exp_done"], base + m + 1)
                        if m >= 2:
                            dve.wait_ge(s["p_tr"], base + m - 1)
                        nc.vector.tensor_scalar(probs[:, m % 2, :], exps[:, m % 2, :], ROUND, ROUND, ALU.add,
                                                ALU.subtract).then_inc(s["rounded"], 1)
                    m = n - PV
                    if m >= 0:
                        h, i, r = p * 2 + m // TILES, m % TILES, row[:, m % 4, :]
                        nc.vector.reciprocal(r[:, 5:6], r[:, 4:5]).then_inc(s["inverted"], 1)
                        dve.wait_ge(s["inverted"], base + m + 1)
                        dve.wait_ge(s["pv_done"], base + m + 1)
                        nc.vector.tensor_scalar(heads_out[:, i, bass.ds(h * HD, HD)], psO[:, m % 2, 0:HD], r[:, 5:6], None,
                                                ALU.mult).then_inc(s["normalised"], 1)
                dve.sem_inc(s["pair_free"], 1)

    sc.close()
    sc = ctx.enter_context(ExitStack())
    oT = sb("c_oT", [P, 2, DIM])
    psT2 = sc.enter_context(nc.psum_tensor("c_psT2", [P, 2, BLK], F32))
    psO2 = sc.enter_context(nc.psum_tensor("c_psO2", [P, 2, BLK], F32))
    with nc.Block() as block:
        @block.tensor
        def _(pe):
            for i in range(TILES + 1):
                if i < TILES:
                    if i >= 2:
                        pe.wait_ge(s["o_back"], i - 1)
                    for c in range(CH):
                        last = nc.tensor.transpose(psT2[:, i % 2, c * P:(c + 1) * P], heads_out[:, i, c * P:(c + 1) * P], ident[:, :])
                    last.then_inc(s["o_tr"], 1)
                if i:
                    j = i - 1
                    pe.wait_ge(s["o_back"], j + 1)
                    if j >= 2:
                        pe.wait_ge(s["added"], j - 1)
                    for c in range(CH):
                        last = nc.tensor.matmul(psO2[:, j % 2, 0:DIM], oT[:, j % 2, c * P:(c + 1) * P], wp[:, c, :],
                                                start=(c == 0), stop=(c == CH - 1))
                    last.then_inc(s["out_done"], 1)

        @block.scalar
        def _(act):
            for i in range(TILES):
                act.wait_ge(s["o_tr"], i + 1)
                if i >= 2:
                    act.wait_ge(s["out_done"], i - 1)
                nc.scalar.activation(oT[:, i % 2, :], psT2[:, i % 2, 0:DIM], ACT.Copy).then_inc(s["o_back"], 1)

        @block.vector
        def _(dve):
            dve.wait_ge(s["late_in"], 32)
            for i in range(TILES):
                nc.vector.tensor_tensor(resid[:, i, :], resid[:, i, :], bp[:, :], ALU.add).then_inc(s["bchain"], 1)
            dve.wait_ge(s["bchain"], PAIRS * UNITS + TILES)
            for i in range(TILES):
                dve.wait_ge(s["out_done"], i + 1)
                nc.vector.tensor_tensor(resid[:, i, :], psO2[:, i % 2, 0:DIM], resid[:, i, :], ALU.add).then_inc(s["added"], 1)
    sc.close()


def stage_experts(nc, ctx, sem, sb, ps, g):
    resid, xnT, ident = g["resid"], g["xnT"], g["ident"]
    stats, mv, work = g["stats"], g["mv"], g["work"]
    LOG = MOE + 1
    PER_BANK = TILES // 2
    CHOICES = TILES * MOE_TOP
    HIDDEN = (P, UPCOLS - 2 * P)
    scattered_rows, expert_rows = g["sorted_x"], g["sorted_y"]
    expert_of = nc.dram_tensor("d_expert_of", (P, 1), U32, kind="Internal").ap()

    slot_u = sb("d_slot_u", [P, CHOICES], U32)
    top = sb("d_top", [P, TILES, 8])
    shared_gate = sb("d_shared_gate", [P, TILES])
    block_expert = sb("d_block_expert", [1, P], U32)
    xn_all = sb("d_xn_all", [P, TILES, DIM])
    s = {n: sem("d_" + n) for n in (
        "var std normed transposed evacuated chain g_in consts pool_chain logged lready exp_done masked ranked totalled "
        "slots_ready expert_ready expert_out expert_in scattered sw_in0 sw_in1 up_done silu h_ready down_done added used0 used1 "
        "x_tr x_back b_up b_silu b_h b_down b_y gathered combined stored "
        "in0 in1 in2 in3 out0 out1 out2 out3").split()}

    routing = ctx.enter_context(ExitStack())

    def first(name, shape, dtype=F32):
        return routing.enter_context(nc.sbuf_tensor(name, shape, dtype))

    gates = first("d_gates", [P, CH, LOG])
    iota = first("d_iota", [P, MOE])
    block_no = first("d_block_no", [P, 1])
    before = first("d_before", [P, P])
    ones = first("d_ones", [P, P])
    logits = first("d_logits", [P, TILES, LOG])
    pr = first("d_probs", [P, TILES, LOG])
    small = first("d_small", [P, 3, TILES])
    top_i = first("d_top_i", [P, TILES, 8], U32)
    top_f = first("d_top_f", [P, TILES, 8])
    chosen = first("d_chosen", [P, TILES, MOE_TOP, MOE])
    mask = first("d_mask", [P, TILES, MOE])
    earlier = first("d_earlier", [P, TILES + 1, MOE])
    blocks_u = first("d_blocks_u", [P, MOE], U32)
    blocks = first("d_blocks", [P, 4, MOE])
    slot_of = first("d_slot_of", [P, TILES, MOE])
    slot_f = first("d_slot_f", [P, CHOICES])
    be = first("d_be", [P, 2])
    be_u = first("d_be_u", [P, 1], U32)

    sc = ctx.enter_context(ExitStack())
    psT = sc.enter_context(nc.psum_tensor("d_psT", [P, 2, BLK], F32))
    psL = sc.enter_context(nc.psum_tensor("d_psL", [P, 2, BLK], F32))
    psR = sc.enter_context(nc.psum_tensor("d_psR", [P, 2, BLK], F32))
    psN = sc.enter_context(nc.psum_tensor("d_psN", [P, BLK], F32))
    with nc.Block() as block:
        @block.sync
        def _(sp):
            sp.dma_start(gates[:, :, :], g["gates_d"].rearrange("(c p) n -> p c n", p=P)).then_inc(s["g_in"], 16)
            sp.wait_ge(s["expert_ready"], 1)
            sp.dma_start(expert_of, be_u[:, :]).then_inc(s["expert_out"], 16)
            sp.wait_ge(s["expert_out"], 16)
            sp.dma_start(block_expert[:, :], expert_of.rearrange("p a -> a p")).then_inc(s["expert_in"], 16)
            sp.wait_ge(s["expert_in"], 16)

        @block.gpsimd
        def _(pool):
            nc.gpsimd.iota(iota[:, :], [[1, MOE]], base=0, channel_multiplier=0, allow_small_or_imprecise_dtypes=True)
            nc.gpsimd.iota(block_no[:, :], [[0, 1]], base=0, channel_multiplier=1, allow_small_or_imprecise_dtypes=True)
            nc.gpsimd.memset(ones[:, :], 1.0)
            nc.gpsimd.memset(earlier[:, 0, :], 0.0)
            nc.gpsimd.memset(before[:, :], 1.0).then_inc(s["pool_chain"], 1)
            pool.wait_ge(s["pool_chain"], 1)
            nc.gpsimd.affine_select(out=before[:, :], in_=before[:, :], compare_op=ALU.is_ge, fill=0.0,
                                    base=-1, pattern=[[1, P]], channel_multiplier=-1).then_inc(s["consts"], 1)

        @block.scalar
        def _(act):
            norm_std(nc, act, work, s["var"], s["std"])
            for i in range(TILES):
                act.wait_ge(s["transposed"], i + 1)
                nc.scalar.activation(xnT[:, :, i * P:(i + 1) * P],
                                     psT[:, i % 2, 0:DIM].rearrange("p (c t) -> p c t", c=CH),
                                     ACT.Copy).then_inc(s["evacuated"], 1)
            act.wait_ge(s["lready"], 1)
            nc.scalar.activation(pr[:, :, 0:MOE], logits[:, :, 0:MOE], ACT.Exp)
            nc.scalar.activation(pr[:, :, MOE], logits[:, :, MOE], ACT.Exp, scale=-1.0).then_inc(s["exp_done"], 1)

        @block.vector
        def _(dve):
            link = counter(dve, s["chain"])
            norm_statistics(nc, dve, link, resid, stats, mv, work, s["var"], s["std"])
            for i in range(TILES):
                nc.vector.tensor_scalar(xn_all[:, i, :], resid[:, i, :], mv[:, i, 0:1], work[:, 2, i:i + 1],
                                        ALU.subtract, ALU.mult).then_inc(s["normed"], 1)
            dve.wait_ge(s["logged"], TILES)
            for b in range(2):
                last = nc.vector.tensor_copy(logits[:, b * PER_BANK:(b + 1) * PER_BANK, :],
                                             psL[:, b, 0:PER_BANK * LOG].rearrange("p (i e) -> p i e", e=LOG))
            link(last)
            routed = logits[:, :, 0:MOE]
            wide = [P, TILES, MOE]
            link(nc.vector.tensor_reduce(small[:, 0, :], routed, AX.X, ALU.max))
            nc.vector.tensor_tensor(routed, routed, small[:, 0, :].unsqueeze(2).to_broadcast(wide), ALU.subtract).then_inc(s["lready"], 1)
            dve.wait_ge(s["exp_done"], 1)
            link(nc.vector.reduce_sum(small[:, 1, :], pr[:, :, 0:MOE], AX.X))
            link(nc.vector.reciprocal(small[:, 1, :], small[:, 1, :]))
            link(nc.vector.tensor_tensor(pr[:, :, 0:MOE], pr[:, :, 0:MOE], small[:, 1, :].unsqueeze(2).to_broadcast(wide), ALU.mult))
            for i in range(TILES):
                last = nc.vector.max(top[:, i, :], pr[:, i, 0:MOE])
            link(last)
            for i in range(TILES):
                last = nc.vector.max_index(top_i[:, i, :], top[:, i, :], pr[:, i, 0:MOE])
            link(last)
            link(nc.vector.tensor_copy(top_f[:, :, :], top_i[:, :, :]))
            dve.wait_ge(s["consts"], 1)
            for k in range(MOE_TOP):
                last = nc.vector.tensor_tensor(chosen[:, :, k, :], top_f[:, :, k:k + 1].to_broadcast(wide),
                                               iota[:, :].unsqueeze(1).to_broadcast(wide), ALU.is_equal)
            link(last)
            link(nc.vector.reduce_sum(mask[:, :, :].unsqueeze(3), chosen[:, :, :, :].rearrange("p i k e -> p i e k"), AX.X))
            for i in range(TILES):
                ins = nc.vector.tensor_tensor(earlier[:, i + 1, :], earlier[:, i, :], mask[:, i, :], ALU.add)
                if i < TILES - 1:
                    link(ins)
            ins.then_inc(s["masked"], 1)
            link(nc.vector.tensor_scalar(small[:, 2, :], pr[:, :, MOE], 1.0, None, ALU.add))
            link(nc.vector.reciprocal(shared_gate[:, :], small[:, 2, :]))
            dve.wait_ge(s["totalled"], 1)
            link(nc.vector.tensor_scalar(blocks_u[:, :], psN[:, 0:MOE], float(P - 1), None, ALU.add))
            link(nc.vector.tensor_scalar(blocks_u[:, :], blocks_u[:, :], 7, None, ALU.logical_shift_right))
            link(nc.vector.tensor_copy(blocks[:, 0, :], blocks_u[:, :]))
            link(nc.vector.tensor_tensor_scan(blocks[:, 1, :], ones[:, 0:MOE], blocks[:, 0, :], 0.0, ALU.mult, ALU.add))
            link(nc.vector.tensor_tensor(blocks[:, 2, :], blocks[:, 1, :], blocks[:, 0, :], ALU.subtract))
            link(nc.vector.tensor_scalar(blocks[:, 2, :], blocks[:, 2, :], float(P), None, ALU.mult))
            link(nc.vector.tensor_scalar(blocks[:, 3, :], blocks[:, 1, :], block_no[:, 0:1], None, ALU.is_le))
            link(nc.vector.reduce_sum(be[:, 0:1], blocks[:, 3, :], AX.X))
            nc.vector.tensor_scalar(be_u[:, :], be[:, 0:1], float(MOE - 1), None, ALU.min).then_inc(s["expert_ready"], 1)
            dve.wait_ge(s["ranked"], 1)
            for b in range(2):
                half = [P, PER_BANK, MOE]
                last = nc.vector.tensor_tensor(slot_of[:, b * PER_BANK:(b + 1) * PER_BANK, :],
                                               psR[:, b, 0:PER_BANK * MOE].rearrange("p (i e) -> p i e", e=MOE),
                                               blocks[:, 2, :].unsqueeze(1).to_broadcast(half), ALU.add)
            link(last)
            for k in range(MOE_TOP):
                last = nc.vector.tensor_tensor(chosen[:, :, k, :], chosen[:, :, k, :], slot_of[:, :, :], ALU.mult)
            link(last)
            link(nc.vector.reduce_sum(slot_f[:, :].unsqueeze(2), chosen[:, :, :, :].rearrange("p i k e -> p (i k) e"), AX.X))
            nc.vector.tensor_copy(slot_u[:, :], slot_f[:, :]).then_inc(s["slots_ready"], 1)

        @block.tensor
        def _(pe):
            pe.wait_ge(s["g_in"], 16)
            for i in range(TILES + 1):
                if i < TILES:
                    pe.wait_ge(s["normed"], i + 1)
                    if i >= 2:
                        pe.wait_ge(s["evacuated"], i - 1)
                    for c in range(CH):
                        last = nc.tensor.transpose(psT[:, i % 2, c * P:(c + 1) * P], xn_all[:, i, c * P:(c + 1) * P], ident[:, :])
                    last.then_inc(s["transposed"], 1)
                if i:
                    j = i - 1
                    pe.wait_ge(s["evacuated"], j + 1)
                    o = (j % PER_BANK) * LOG
                    for c in range(CH):
                        last = nc.tensor.matmul(psL[:, j // PER_BANK, o:o + LOG], xnT[:, c, j * P:(j + 1) * P], gates[:, c, :],
                                                start=(c == 0), stop=(c == CH - 1))
                    last.then_inc(s["logged"], 1)
            pe.wait_ge(s["masked"], 1)
            pe.wait_ge(s["consts"], 1)
            nc.tensor.matmul(psN[:, 0:MOE], ones[:, :], earlier[:, TILES, :], start=True, stop=True).then_inc(s["totalled"], 1)
            for i in range(TILES):
                o = (i % PER_BANK) * MOE
                dst = psR[:, i // PER_BANK, o:o + MOE]
                nc.tensor.matmul(dst, before[:, :], mask[:, i, :], start=True, stop=False)
                last = nc.tensor.matmul(dst, ones[:, :], earlier[:, i, :], start=False, stop=True)
            last.then_inc(s["ranked"], 1)
    sc.close()
    routing.close()

    w_up = sb("d_w_up", [P, 4, CH, UPCOLS])
    w_down = sb("d_w_down", [P, 4, 2, DIM])
    gate = sb("d_gate", [P, 2, 2, BLK])
    hidden = sb("d_hidden", [P, 2, 2, BLK])
    sc = ctx.enter_context(ExitStack())
    psU = sc.enter_context(nc.psum_tensor("d_psU", [P, 2, 3, BLK], F32))
    psD = sc.enter_context(nc.psum_tensor("d_psD", [P, 2, BLK], F32))
    STEPS = 2 * BLKS
    loads = (s["sw_in0"], s["sw_in1"])
    used = (s["used0"], s["used1"])
    with nc.Block() as block:
        @block.sync
        def _(sp):
            for x in range(2):
                sp.sem_inc(used[x], 1)
            with sp.Fori(0, SHARED // 2) as e:
                for x in range(2):
                    sp.wait_ge(used[x], e + 1)
                    sp.dma_start(w_up[:, x, :, :], g["sup_d"][bass.ds(e * 2 + x, 1), :, :].rearrange("e (c p) n -> p (e c) n", p=P)).then_inc(loads[x], 16)
                    sp.dma_start(w_down[:, x, 0, :], g["sdown_d"][bass.ds(e * 2 + x, 1), 0:P, :].rearrange("e i d -> i (e d)")).then_inc(loads[x], 16)
                    sp.dma_start(w_down[0:REST, x, 1, :], g["sdown_d"][bass.ds(e * 2 + x, 1), P:INTER, :].rearrange("e i d -> i (e d)")).then_inc(loads[x], 16)

        @block.gpsimd
        def _(pool):
            pool.wait_ge(s["slots_ready"], 1)
            pool.wait_ge(g["zeroed"], 16)
            for i in range(TILES):
                for k in range(MOE_TOP):
                    c = i * MOE_TOP + k
                    nc.gpsimd.indirect_dma_start(out=scattered_rows, out_offset=bass.IndirectOffsetOnAxis(ap=slot_u[:, c:c + 1], axis=0),
                                                 in_=xn_all[:, i, :], in_offset=None).then_inc(s["scattered"], 16)
            pool.wait_ge(s["scattered"], 16 * CHOICES)

        @block.tensor
        def _(pe):
            pe.sem_inc(s["added"], 1)
            with pe.Fori(0, SHARED // 2) as e:
                base = e * STEPS
                for n in range(STEPS + 1):
                    if n < STEPS:
                        x, b = n // BLKS, n % BLKS
                        if b == 0:
                            pe.wait_ge(loads[x], (e + 1) * 48)
                        if n >= 2:
                            pe.wait_ge(s["h_ready"], base + n - 1)
                        for k in range(3):
                            width = P if k < 2 else HIDDEN[1]
                            for c in range(CH):
                                last = nc.tensor.matmul(psU[0:width, n % 2, k, :], w_up[:, x, c, k * P:k * P + width],
                                                        xnT[:, c, b * BLK:(b + 1) * BLK], start=(c == 0), stop=(c == CH - 1))
                        last.then_inc(s["up_done"], 1)
                    if n:
                        m = n - 1
                        x, b = m // BLKS, m % BLKS
                        pe.wait_ge(s["h_ready"], base + m + 1)
                        for half in range(2):
                            pe.wait_ge(s["added"], (base + m) * 2 + half if m or half else base * 2 + 1)
                            for j in range(2):
                                t0 = (2 * half + j) * P
                                out = psD[:, half, j * DIM:(j + 1) * DIM]
                                nc.tensor.matmul(out, hidden[:, m % 2, 0, t0:t0 + P], w_down[:, x, 0, :], start=True, stop=False)
                                last = nc.tensor.matmul(out, hidden[0:REST, m % 2, 1, t0:t0 + P], w_down[0:REST, x, 1, :], start=False, stop=True)
                            last.then_inc(s["down_done"], 1)
                        if b == BLKS - 1:
                            pe.wait_ge(s["down_done"], (base + m) * 2 + 2)
                            pe.sem_inc(used[x], 1)

        @block.scalar
        def _(act):
            with act.Fori(0, SHARED // 2) as e:
                base = e * STEPS
                for n in range(STEPS):
                    act.wait_ge(s["up_done"], base + n + 1)
                    if n >= 2:
                        act.wait_ge(s["h_ready"], base + n - 1)
                    nc.scalar.activation(gate[:, n % 2, 0, :], psU[:, n % 2, 0, :], ACT.Silu)
                    nc.scalar.activation(gate[0:REST, n % 2, 1, :], psU[0:REST, n % 2, 2, :], ACT.Silu).then_inc(s["silu"], 1)

        @block.vector
        def _(dve):
            with dve.Fori(0, SHARED // 2) as e:
                base = e * STEPS
                for n in range(STEPS + 1):
                    if n < STEPS:
                        dve.wait_ge(s["silu"], base + n + 1)
                        if n >= 2:
                            dve.wait_ge(s["down_done"], (base + n - 1) * 2)
                        nc.vector.tensor_tensor(hidden[:, n % 2, 0, :], gate[:, n % 2, 0, :], psU[:, n % 2, 1, :], ALU.mult)
                        nc.vector.tensor_tensor(hidden[0:REST, n % 2, 1, :], gate[0:REST, n % 2, 1, :], psU[64:64 + REST, n % 2, 2, :],
                                                ALU.mult).then_inc(s["h_ready"], 1)
                    if n:
                        m = n - 1
                        b = m % BLKS
                        for half in range(2):
                            dve.wait_ge(s["down_done"], (base + m) * 2 + half + 1)
                            for j in range(2):
                                i = b * BLK // P + 2 * half + j
                                last = nc.vector.scalar_tensor_tensor(resid[:, i, :], psD[:, half, j * DIM:(j + 1) * DIM],
                                                                      shared_gate[:, i:i + 1], resid[:, i, :], ALU.mult, ALU.add)
                            last.then_inc(s["added"], 1)
    sc.close()

    SLOTS = 4
    rows_in = sb("d_rows_in", [P, SLOTS, DIM])
    colsT = sb("d_colsT", [P, 2, CH, P])
    b_gate = sb("d_b_gate", [P, 2, 2, P])
    b_hidden = sb("d_b_hidden", [P, 2, 2, P])
    rows_out = sb("d_rows_out", [P, SLOTS, DIM])
    sc = ctx.enter_context(ExitStack())
    psX = sc.enter_context(nc.psum_tensor("d_psX", [P, 2, BLK], F32))
    psH = sc.enter_context(nc.psum_tensor("d_psH", [P, 2, BLK], F32))
    psY = sc.enter_context(nc.psum_tensor("d_psY", [P, 2, BLK], F32))
    arrived = [s[f"in{x}"] for x in range(SLOTS)]
    left = [s[f"out{x}"] for x in range(SLOTS)]
    LAST = BLOCKS // SLOTS - 1
    IN = 4 * 16
    with nc.Block() as block:
        @block.sync
        def _(sp):
            def load(n, x):
                expert = sp.value_load(block_expert[0:1, n:n + 1] if isinstance(n, int) else block_expert[0:1, bass.ds(n, 1)],
                                       min_val=0, max_val=MOE - 1)
                r = slice(n * P, (n + 1) * P) if isinstance(n, int) else bass.ds(n * P, P)
                sp.dma_start(w_up[:, x, :, :], g["up_d"][bass.ds(expert, 1), :, :].rearrange("e (c p) n -> p (e c) n", p=P)).then_inc(arrived[x], 16)
                sp.dma_start(w_down[:, x, 0, :], g["down_d"][bass.ds(expert, 1), 0:P, :].rearrange("e i d -> i (e d)")).then_inc(arrived[x], 16)
                sp.dma_start(w_down[0:REST, x, 1, :], g["down_d"][bass.ds(expert, 1), P:INTER, :].rearrange("e i d -> i (e d)")).then_inc(arrived[x], 16)
                sp.dma_start(rows_in[:, x, :], scattered_rows[r, :]).then_inc(arrived[x], 16)

            def store(n, x):
                sp.wait_ge(s["b_y"], n + 1)
                r = slice(n * P, (n + 1) * P) if isinstance(n, int) else bass.ds(n * P, P)
                sp.dma_start(expert_rows[r, :], rows_out[:, x, :]).then_inc(left[x], 16)

            for x in range(SLOTS):
                load(x, x)
            with sp.Fori(0, LAST) as it:
                for x in range(SLOTS):
                    n = it * SLOTS + x
                    sp.wait_ge(s["b_down"], n + 1)
                    load(n + SLOTS, x)
                    store(n, x)
            for x in range(SLOTS):
                store(LAST * SLOTS + x, x)
            for x in range(SLOTS):
                sp.wait_ge(left[x], 16 * (LAST + 1))

        @block.tensor
        def _(pe):
            def turn(n, x, it):
                pe.wait_ge(arrived[x], (it + 1) * IN)
                if not isinstance(n, int) or n >= 2:
                    pe.wait_ge(s["x_back"], n - 1)
                for c in range(CH):
                    last = nc.tensor.transpose(psX[:, x % 2, c * P:(c + 1) * P], rows_in[:, x, c * P:(c + 1) * P], ident[:, :])
                last.then_inc(s["x_tr"], 1)

            def up(n, x):
                pe.wait_ge(s["x_back"], n + 1)
                if not isinstance(n, int) or n >= 2:
                    pe.wait_ge(s["b_h"], n - 1)
                for k in range(3):
                    width = P if k < 2 else HIDDEN[1]
                    for c in range(CH):
                        last = nc.tensor.matmul(psH[0:width, x % 2, k * P:(k + 1) * P], w_up[:, x, c, k * P:k * P + width],
                                                colsT[:, x % 2, c, :], start=(c == 0), stop=(c == CH - 1))
                last.then_inc(s["b_up"], 1)

            def down(n, x):
                pe.wait_ge(s["b_h"], n + 1)
                if not isinstance(n, int) or n >= 2:
                    pe.wait_ge(s["b_y"], n - 1)
                nc.tensor.matmul(psY[:, x % 2, 0:DIM], b_hidden[:, x % 2, 0, :], w_down[:, x, 0, :], start=True, stop=False)
                nc.tensor.matmul(psY[:, x % 2, 0:DIM], b_hidden[0:REST, x % 2, 1, :], w_down[0:REST, x, 1, :],
                                 start=False, stop=True).then_inc(s["b_down"], 1)

            def steps(it, first, last):
                for x in range(SLOTS):
                    n = it * SLOTS + x
                    if not (last and x == SLOTS - 1):
                        turn(n + 1, (x + 1) % SLOTS, it + (x + 1) // SLOTS)
                    up(n, x)
                    if not (first and x == 0):
                        down(n - 1, (x - 1) % SLOTS)

            turn(0, 0, 0)
            steps(0, True, False)
            with pe.Fori(1, LAST) as it:
                steps(it, False, False)
            steps(LAST, False, True)
            down(LAST * SLOTS + SLOTS - 1, SLOTS - 1)

        @block.scalar
        def _(act):
            def columns(n, x):
                act.wait_ge(s["x_tr"], n + 1)
                if not isinstance(n, int) or n >= 2:
                    act.wait_ge(s["b_up"], n - 1)
                nc.scalar.activation(colsT[:, x % 2, :, :], psX[:, x % 2, 0:DIM].rearrange("p (c t) -> p c t", c=CH),
                                     ACT.Copy).then_inc(s["x_back"], 1)

            def silu(n, x):
                act.wait_ge(s["b_up"], n + 1)
                if not isinstance(n, int) or n >= 2:
                    act.wait_ge(s["b_h"], n - 1)
                nc.scalar.activation(b_gate[:, x % 2, 0, :], psH[:, x % 2, 0:P], ACT.Silu)
                nc.scalar.activation(b_gate[0:REST, x % 2, 1, :], psH[0:REST, x % 2, 2 * P:3 * P], ACT.Silu).then_inc(s["b_silu"], 1)

            def steps(it, last):
                for x in range(SLOTS):
                    n = it * SLOTS + x
                    if not (last and x == SLOTS - 1):
                        columns(n + 1, (x + 1) % SLOTS)
                    silu(n, x)

            columns(0, 0)
            steps(0, False)
            with act.Fori(1, LAST) as it:
                steps(it, False)
            steps(LAST, True)

        @block.vector
        def _(dve):
            def gated(n, x):
                dve.wait_ge(s["b_silu"], n + 1)
                if not isinstance(n, int) or n >= 2:
                    dve.wait_ge(s["b_down"], n - 1)
                nc.vector.tensor_tensor(b_hidden[:, x % 2, 0, :], b_gate[:, x % 2, 0, :], psH[:, x % 2, P:2 * P], ALU.mult)
                nc.vector.tensor_tensor(b_hidden[0:REST, x % 2, 1, :], b_gate[0:REST, x % 2, 1, :], psH[64:64 + REST, x % 2, 2 * P:3 * P],
                                        ALU.mult).then_inc(s["b_h"], 1)

            def result(n, x, it):
                dve.wait_ge(s["b_down"], n + 1)
                if not isinstance(it, int) or it >= 1:
                    dve.wait_ge(left[x], it * 16)
                nc.vector.tensor_copy(rows_out[:, x, :], psY[:, x % 2, 0:DIM]).then_inc(s["b_y"], 1)

            def steps(it, first):
                for x in range(SLOTS):
                    n = it * SLOTS + x
                    gated(n, x)
                    if not (first and x == 0):
                        result(n - 1, (x - 1) % SLOTS, it if x else it - 1)

            steps(0, True)
            with dve.Fori(1, LAST) as it:
                steps(it, False)
            steps(LAST, False)
            result(LAST * SLOTS + SLOTS - 1, SLOTS - 1, LAST)
    sc.close()

    RING = 8
    picked = sb("d_picked", [P, RING, DIM])
    ring = [sem(f"d_ring{r}") for r in range(RING)]
    with nc.Block() as block:
        @block.gpsimd
        def _(pool):
            for c in range(CHOICES):
                if c >= RING:
                    pool.wait_ge(s["combined"], c - RING + 1)
                nc.gpsimd.indirect_dma_start(out=picked[:, c % RING, :], out_offset=None, in_=expert_rows,
                                             in_offset=bass.IndirectOffsetOnAxis(ap=slot_u[:, c:c + 1], axis=0)).then_inc(ring[c % RING], 16)

        @block.vector
        def _(dve):
            for c in range(CHOICES):
                i, k = c // MOE_TOP, c % MOE_TOP
                dve.wait_ge(ring[c % RING], 16 * (c // RING + 1))
                if k:
                    dve.wait_ge(s["combined"], c)
                nc.vector.scalar_tensor_tensor(resid[:, i, :], picked[:, c % RING, :], top[:, i, k:k + 1], resid[:, i, :],
                                               ALU.mult, ALU.add).then_inc(s["combined"], 1)

        @block.sync
        def _(sp):
            for i in range(TILES):
                sp.wait_ge(s["combined"], MOE_TOP * (i + 1))
                sp.dma_start(g["out"][i, :, :], resid[:, i, :]).then_inc(s["stored"], 16)
            sp.wait_ge(s["stored"], 16 * TILES)


def stage_store(nc, ctx, sem, sb, ps, g):
    stored = sem("stored")
    with nc.Block() as block:
        @block.sync
        def _(sp):
            sp.dma_start(g["out"].rearrange("b t d -> t b d"), g["resid"][:, :, :]).then_inc(stored, 16)
            sp.wait_ge(stored, 16)


def build(nc, arrays, out, stages=4):
    with ExitStack() as ctx:
        def sem(name):
            return ctx.enter_context(nc.semaphore(name))

        def sb(name, shape, dtype=F32):
            return ctx.enter_context(nc.sbuf_tensor(name, shape, dtype))

        def ps(name, shape, dtype=F32):
            return ctx.enter_context(nc.psum_tensor(name, shape, dtype))

        g = dict(arrays)
        g["out"] = out
        g["resid"] = sb("resid", [P, TILES, DIM])
        g["ctxT"] = sb("ctxT", [P, CH, TOKENS])
        g["xnT"] = sb("xnT", [P, CH, TOKENS])
        g["ident"] = sb("ident", [P, P])
        g["stats"] = sb("stats", [P, TILES, 6])
        g["mv"] = sb("mv", [P, TILES, 2])
        g["work"] = sb("work", [P, 4, TILES])
        g["xn"] = sb("xn", [P, 4, DIM])
        g["sorted_x"] = nc.dram_tensor("sorted_x", (BLOCKS * P, DIM), F32, kind="Internal").ap()
        g["sorted_y"] = nc.dram_tensor("sorted_y", (BLOCKS * P, DIM), F32, kind="Internal").ap()
        g["zeros"] = sb("zeros", [P, DIM])
        for name in ("x_in", "ctx_in", "ident_ready", "zeros_ready", "zeroed"):
            g[name] = sem(name)
        for n, stage in enumerate((stage_recurrence, stage_product_keys, stage_attention, stage_experts)[:stages]):
            with ExitStack() as own:
                def own_sb(name, shape, dtype=F32):
                    return own.enter_context(nc.sbuf_tensor(name, shape, dtype))

                def own_ps(name, shape, dtype=F32):
                    return own.enter_context(nc.psum_tensor(name, shape, dtype))

                stage(nc, own, sem, own_sb, own_ps, g)
        if stages < 4:
            stage_store(nc, ctx, sem, sb, ps, g)


def layouts(inputs):
    import numpy as np

    a = {k: np.asarray(v) for k, v in inputs.items()}
    x = np.ascontiguousarray(a["x"].reshape(TOKENS, DIM))
    ctxT = np.ascontiguousarray(a["ctx_2048"].reshape(TOKENS, DIM).T)
    w13 = a["L1_ffn_w13"]
    se = a["L1_ffn_se_gate_up_w"]

    def up_layout(gate, up):
        out = np.zeros((len(gate), UPCOLS, DIM), np.float32)
        out[:, 0:P] = gate[:, 0:P]
        out[:, P:2 * P] = up[:, 0:P]
        out[:, 2 * P:2 * P + REST] = gate[:, P:]
        out[:, 2 * P + 64:] = up[:, P:]
        return np.ascontiguousarray(out.transpose(0, 2, 1))

    c = np.ascontiguousarray
    return {
        "x": x, "ctxT_d": ctxT, "td": np.ascontiguousarray(a["L0_xattn_time_decay"].reshape(CH, P).T),
        "tf": np.ascontiguousarray(a["L0_xattn_time_first"].reshape(CH, P).T),
        "pk_wqT_d": c(a["L0_ffn_Wq"].T),
        "pk_keysT_d": c(a["L0_ffn_keys"].transpose(0, 2, 3, 1).reshape(PK_HEADS * 2 * PK_DK, PK_KEYS)),
        "pk_downT_d": c(a["L0_ffn_e_down"].T), "pk_up_d": c(a["L0_ffn_e_up"]),
        "wq_d": c(a["L1_xattn_Wq"]), "bq_d": c(a["L1_xattn_bq"].reshape(1, -1)),
        "wkv_d": c(a["L1_xattn_Wkv"]), "bkv_d": c(a["L1_xattn_bkv"].reshape(1, -1)),
        "bv_d": c(a["L1_xattn_bkv"][DIM:].reshape(CH, P).T),
        "wp_d": c(a["L1_xattn_Wp"]), "bp_d": c(a["L1_xattn_bp"].reshape(1, -1)),
        "gates_d": c(np.concatenate([a["L1_ffn_gate_w"], a["L1_ffn_shared_gate_w"]]).T),
        "up_d": up_layout(w13[:, :INTER], w13[:, INTER:]),
        "down_d": c(a["L1_ffn_w2"].transpose(0, 2, 1)),
        "sup_d": up_layout(se[:SH_INTER].reshape(SHARED, INTER, DIM), se[SH_INTER:].reshape(SHARED, INTER, DIM)),
        "sdown_d": c(a["L1_ffn_se_down_w"].T.reshape(SHARED, INTER, DIM)),
    }


def kernel(**inputs):
    import numpy as np
    import concourse.bacc as bacc
    from concourse.bass_utils import run_bass_kernel_spmd

    arrays = layouts(inputs)
    nc = bacc.Bacc("TRN2", target_bir_lowering=False, num_devices=1)
    aps = {n: nc.dram_tensor("in_" + n, a.shape, mybir.dt.from_np(a.dtype), kind="ExternalInput").ap() for n, a in arrays.items()}
    out = nc.dram_tensor("out", (BATCH, SEQ, DIM), F32, kind="ExternalOutput").ap()
    build(nc, aps, out)
    result = run_bass_kernel_spmd(nc, [{"in_" + n: a for n, a in arrays.items()}], core_ids=[0])
    return result.results[0]["out"]
```

```python
import concourse.bass as bass
from concourse import mybir
from contextlib import ExitStack

F32 = mybir.dt.float32
BF16 = mybir.dt.bfloat16
U32 = mybir.dt.uint32
ALU = mybir.AluOpType
ACT = mybir.ActivationFunctionType
AX = mybir.AxisListType

P = 128
BATCH, SEQ, DIM = 16, 128, 256
TILES = BATCH * SEQ // P
TOKENS = TILES * P
CH = DIM // P
EPS = 1e-5
ROUND = 12582912.0
BLK = 512
BLKS = TOKENS // BLK

PK_HEADS, PK_KEYS, PK_TOP, PK_DK = 4, 128, 8, 64
PK_EXPERTS = 2048
G8 = 2 * PK_HEADS
PK_ROWS = PK_EXPERTS // P

HEADS, HD = 16, 16
LN255 = 5.541263545158426

MOE, INTER, SH_INTER, MOE_TOP = 60, 176, 704, 4
SHARED = SH_INTER // INTER
SLOTS = 8
BLOCKS = -(-((TOKENS * MOE_TOP + MOE * (P - 1)) // P) // SLOTS) * SLOTS
REST = INTER - P
UPCOLS = 2 * P + 64 + REST
DOWN0 = CH * UPCOLS
WCOLS = DOWN0 + DIM
TAG = DIM
ROWW = DIM + 4


def counter(engine, semaphore):
    count = [0]

    def link(instruction):
        instruction.then_inc(semaphore, 1)
        count[0] += 1
        engine.wait_ge(semaphore, count[0])

    return link


def norm_statistics(nc, dve, link, stats, mv, work, var_ready, std_ready):
    for i in range(TILES):
        last = nc.vector.bn_aggr(mv[:, i, :], stats[:, i, :])
    link(last)
    nc.vector.tensor_scalar(work[:, 0, :], mv[:, :, 1], EPS, None, ALU.add).then_inc(var_ready, 1)
    dve.wait_ge(std_ready, 1)
    link(nc.vector.reciprocal(work[:, 2, :], work[:, 1, :]))
    link(nc.vector.tensor_tensor(work[:, 3, :], work[:, 2, :], work[:, 2, :], ALU.mult))
    link(nc.vector.tensor_tensor(work[:, 3, :], work[:, 3, :], work[:, 0, :], ALU.mult))
    link(nc.vector.tensor_scalar(work[:, 3, :], work[:, 3, :], -0.5, 1.5, ALU.mult, ALU.add))
    link(nc.vector.tensor_tensor(work[:, 2, :], work[:, 2, :], work[:, 3, :], ALU.mult))


def norm_std(nc, act, work, var_ready, std_ready):
    act.wait_ge(var_ready, 1)
    nc.scalar.activation(work[:, 1, :], work[:, 0, :], ACT.Sqrt).then_inc(std_ready, 1)


def norm_tile(nc, dve, i, resid, xn, mv, work, normed, transposed):
    if i >= 4:
        dve.wait_ge(transposed, i - 3)
    nc.vector.tensor_scalar(xn[:, i % 4, :], resid[:, i, :], mv[:, i, 0:1], work[:, 2, i:i + 1],
                            ALU.subtract, ALU.mult).then_inc(normed, 1)


def transpose_tile(nc, pe, i, xn, psT, ident, normed, transposed, evacuated):
    pe.wait_ge(normed, i + 1)
    if i >= 2:
        pe.wait_ge(evacuated, i - 1)
    for c in range(CH):
        last = nc.tensor.transpose(psT[:, i % 2, c * P:(c + 1) * P], xn[:, i % 4, c * P:(c + 1) * P], ident[:, :])
    last.then_inc(transposed, 1)


def stage_recurrence(nc, ctx, sem, sb, ps, g):
    resid, ctxT, ident = g["resid"], g["ctxT"], g["ident"]
    stats, mv, work, xn = g["stats"], g["mv"], g["work"], g["xn"]
    par = sb("wkv_par", [P, 8, CH])
    ek = sb("ek", [P, CH, TOKENS])
    ev = sb("ev", [P, CH, TOKENS])
    decay = sb("decay", [P, CH, TOKENS])
    acc_v = sb("acc_v", [P, TOKENS])
    acc_k = sb("acc_k", [P, TOKENS])
    cur_v = sb("cur_v", [P, TOKENS])
    cur_k = sb("cur_k", [P, TOKENS])
    yT = sb("yT", [P, CH, TOKENS])
    psT = ps("a_psT", [P, 2, BLK])
    psY = ps("a_psY", [P, 2, BLK])
    wqT = sb("pk_wqT", [PK_DK, G8, DIM])
    keysT = sb("pk_keysT", [PK_DK, G8, PK_KEYS])
    mix = g["buffer"][:, :].rearrange("p (c n) -> p c n", c=CH)
    psM = ps("a_psM", [P, G8 * PK_KEYS])
    mix_in, mix_ready, mix_copied = sem("a_mix_in"), sem("a_mix_ready"), sem("a_mix_copied")
    wv = sb("a_wv", [P, CH, DIM])
    bv = sb("a_bv", [P, CH])
    vT = sb("a_vT", [P, CH, TOKENS])
    psV = ps("a_psV", [P, 2, BLK])
    v_in, v_mm, v_copied, v_saved = sem("a_v_in"), sem("a_v_mm"), sem("a_v_copied"), sem("a_v_saved")
    var_ready, std_ready, normed = sem("a_var"), sem("a_std"), sem("a_normed")
    transposed, evacuated = sem("a_transposed"), sem("a_evacuated")
    chain, achain = sem("a_chain"), sem("a_achain")
    m_ready, par_ready, decay_ready, cur_ready = sem("a_m"), sem("a_par"), sem("a_decay"), sem("a_cur")
    ev_ready, scans_done, num_done = sem("a_ev"), sem("a_scans"), sem("a_num")
    y_back, pool_ms = sem("a_yback"), sem("a_pool")
    X_PARTS = 2
    x_in = [sem(f"a_x_in{part}") for part in range(X_PARTS)]
    y_added, par_in = sem("a_yadded"), sem("a_parin")

    with nc.Block() as block:
        @block.sync
        def _(sp):
            sp.dma_start(par[:, 0, :], g["td"]).then_inc(par_in, 16)
            sp.dma_start(par[:, 1, :], g["tf"]).then_inc(par_in, 16)
            for part in range(X_PARTS):
                tiles = slice(part * TILES // X_PARTS, (part + 1) * TILES // X_PARTS)
                sp.dma_start(resid[:, tiles, :], g["x"].rearrange("(i p) d -> p i d", p=P)[:, tiles, :]).then_inc(x_in[part], 16)
            sp.dma_start(ctxT[:, :, :], g["ctxT_d"].rearrange("(c p) t -> p c t", p=P)).then_inc(g["ctx_in"], 16)
            sp.dma_start(wqT[:, :, :], g["pk_wqT_d"].rearrange("(q p) c -> p q c", p=PK_DK)).then_inc(mix_in, 16)
            sp.dma_start(keysT[:, :, :], g["pk_keysT_d"].rearrange("(q p) k -> p q k", p=PK_DK)).then_inc(mix_in, 16)
            sp.dma_start(wv[:, :, :], g["wkv_d"][:, DIM:2 * DIM].rearrange("(c p) n -> p c n", p=P)).then_inc(v_in, 16)
            sp.dma_start(bv[:, :], g["bv_d"]).then_inc(v_in, 16)
            sp.wait_ge(v_copied, CH * BLKS)
            sp.dma_start(g["values_d"].rearrange("(c p) t -> p c t", p=P), vT[:, :, :]).then_inc(v_saved, 16)
            sp.wait_ge(v_saved, 16)

        @block.gpsimd
        def _(pool):
            nc.gpsimd.memset(g["zeros"][:, :], 0.0)
            nc.gpsimd.iota(g["pad_tags"][:, :, :], [[P, BLOCKS], [0, ROWW - TAG]], base=MOE_TOP * TOKENS,
                           channel_multiplier=1).then_inc(g["zeros_ready"], 1)
            nc.gpsimd.memset(ident[:, :], 0.0).then_inc(pool_ms, 1)
            pool.wait_ge(pool_ms, 1)
            nc.gpsimd.affine_select(out=ident[:, :], in_=ident[:, :], compare_op=ALU.not_equal, fill=1.0,
                                    base=0, pattern=[[-1, P]], channel_multiplier=1).then_inc(g["ident_ready"], 1)
            nc.gpsimd.memset(decay[:, :, :], 1.0).then_inc(pool_ms, 1)
            pool.wait_ge(par_ready, 1)
            pool.wait_ge(pool_ms, 2)
            for c in range(CH):
                nc.gpsimd.tensor_scalar(decay[:, c, :], decay[:, c, :], par[:, 5, c:c + 1], None, ALU.mult).then_inc(pool_ms, 1)
                pool.wait_ge(pool_ms, 3 + c)
                nc.gpsimd.memset(decay[:, c, :].rearrange("p (b t) -> p b t", t=SEQ)[:, :, 0], 0.0).then_inc(decay_ready, 1)

        @block.scalar
        def _(act):
            norm_std(nc, act, work, var_ready, std_ready)
            act.wait_ge(par_in, 32)
            nc.scalar.activation(par[:, 4, :], par[:, 0, :], ACT.Exp).then_inc(achain, 1)
            act.wait_ge(achain, 1)
            nc.scalar.activation(par[:, 5, :], par[:, 4, :], ACT.Exp, scale=-1.0)
            act.wait_ge(m_ready, 1)
            nc.scalar.activation(par[:, 6, :], par[:, 2, :], ACT.Exp, scale=-1.0)
            nc.scalar.activation(par[:, 7, :], par[:, 3, :], ACT.Exp).then_inc(par_ready, 1)
            for i in range(TILES):
                act.wait_ge(transposed, i + 1)
                nc.scalar.activation(ek[:, :, i * P:(i + 1) * P],
                                     psT[:, i % 2, 0:DIM].rearrange("p (c t) -> p c t", c=CH),
                                     ACT.Exp).then_inc(evacuated, 1)
            def side_products(c):
                act.wait_ge(mix_ready, c + 1)
                nc.scalar.activation(mix[:, c, :], psM[:, :], ACT.Copy).then_inc(mix_copied, 1)
                for b in range(BLKS):
                    n = c * BLKS + b
                    act.wait_ge(v_mm, n + 1)
                    if n == 0:
                        act.wait_ge(v_in, 32)
                    nc.scalar.activation(vT[:, c, b * BLK:(b + 1) * BLK], psV[:, n % 2, :], ACT.Identity,
                                         bias=bv[:, c:c + 1]).then_inc(v_copied, 1)

            act.wait_ge(evacuated, TILES)
            for c in range(CH):
                if c:
                    for m in range(CH):
                        side_products(m)
                act.wait_ge(ev_ready, c + 1)
                if c:
                    act.wait_ge(num_done, c)
                nc.scalar.activation(cur_v[:, :], ev[:, c, :], ACT.Copy, scale=par[:, 7, c:c + 1])
                nc.scalar.activation(cur_k[:, :], ek[:, c, :], ACT.Copy, scale=par[:, 7, c:c + 1]).then_inc(cur_ready, 1)

        @block.vector
        def _(dve):
            link = counter(dve, chain)
            dve.wait_ge(par_in, 32)
            link(nc.vector.tensor_scalar(par[:, 2, :], par[:, 1, :], 0.0, None, ALU.max))
            nc.vector.tensor_tensor(par[:, 3, :], par[:, 1, :], par[:, 2, :], ALU.subtract).then_inc(m_ready, 1)
            for i in range(TILES):
                if i % (TILES // X_PARTS) == 0:
                    dve.wait_ge(x_in[i // (TILES // X_PARTS)], 16)
                last = nc.vector.bn_stats(stats[:, i, :], resid[:, i, :])
            link(last)
            norm_statistics(nc, dve, link, stats, mv, work, var_ready, std_ready)
            for i in range(TILES):
                norm_tile(nc, dve, i, resid, xn, mv, work, normed, transposed)
            dve.wait_ge(g["ctx_in"], 16)
            dve.wait_ge(evacuated, TILES)
            for c in range(CH):
                nc.vector.tensor_tensor(ev[:, c, :], ek[:, c, :], ctxT[:, c, :], ALU.mult).then_inc(ev_ready, 1)
            for c in range(CH):
                dve.wait_ge(ev_ready, c + 1)
                dve.wait_ge(decay_ready, c + 1)
                nc.vector.tensor_tensor_scan(acc_v[:, :], decay[:, c, :], ev[:, c, :], 0.0, ALU.mult, ALU.add).then_inc(scans_done, 1)
                nc.vector.tensor_tensor_scan(acc_k[:, :], decay[:, c, :], ek[:, c, :], 0.0, ALU.mult, ALU.add).then_inc(scans_done, 1)
                dve.wait_ge(scans_done, 2 * c + 2)
                dve.wait_ge(cur_ready, c + 1)
                for cur, acc in ((cur_v, acc_v), (cur_k, acc_k)):
                    later = cur[:, :].rearrange("p (b t) -> p b t", t=SEQ)[:, :, 1:SEQ]
                    earlier = acc[:, :].rearrange("p (b t) -> p b t", t=SEQ)[:, :, 0:SEQ - 1]
                    last = nc.vector.scalar_tensor_tensor(later, earlier, par[:, 6, c:c + 1], later, ALU.mult, ALU.add)
                link(last)
                link(nc.vector.reciprocal(cur_k[:, :], cur_k[:, :]))
                link(nc.vector.tensor_tensor(yT[:, c, :], cur_v[:, :], cur_k[:, :], ALU.mult))
                nc.vector.tensor_copy(yT[:, c, :].rearrange("p (b t) -> p b t", t=SEQ)[:, :, 0],
                                      ctxT[:, c, :].rearrange("p (b t) -> p b t", t=SEQ)[:, :, 0]).then_inc(num_done, 1)
            for i in range(TILES):
                dve.wait_ge(y_back, i + 1)
                nc.vector.tensor_tensor(resid[:, i, :], psY[:, i % 2, 0:DIM], resid[:, i, :], ALU.add).then_inc(y_added, 1)
                if i:
                    dve.wait_ge(y_added, i)
                    nc.vector.bn_stats(stats[:, i - 1, :], resid[:, i - 1, :])
            dve.wait_ge(y_added, TILES)
            nc.vector.bn_stats(stats[:, TILES - 1, :], resid[:, TILES - 1, :])

        @block.tensor
        def _(pe):
            pe.wait_ge(g["ident_ready"], 1)
            for i in range(TILES):
                transpose_tile(nc, pe, i, xn, psT, ident, normed, transposed, evacuated)
            pe.wait_ge(mix_in, 32)
            pe.wait_ge(v_in, 32)
            pe.wait_ge(g["ctx_in"], 16)
            for c in range(CH):
                if c:
                    pe.wait_ge(mix_copied, c)
                for q in range(G8):
                    last = nc.tensor.matmul(psM[:, q * PK_KEYS:(q + 1) * PK_KEYS], wqT[:, q, c * P:(c + 1) * P],
                                            keysT[:, q, :], start=True, stop=True)
                last.then_inc(mix_ready, 1)
                for b in range(BLKS):
                    n = c * BLKS + b
                    if n >= 2:
                        pe.wait_ge(v_copied, n - 1)
                    for k in range(CH):
                        last = nc.tensor.matmul(psV[:, n % 2, :], wv[:, k, c * P:(c + 1) * P],
                                                ctxT[:, k, b * BLK:(b + 1) * BLK], start=(k == 0), stop=(k == CH - 1))
                    last.then_inc(v_mm, 1)
            pe.wait_ge(num_done, CH)
            for i in range(TILES):
                if i >= 2:
                    pe.wait_ge(y_added, i - 1)
                for c in range(CH):
                    last = nc.tensor.transpose(psY[:, i % 2, c * P:(c + 1) * P], yT[:, c, i * P:(i + 1) * P], ident[:, :])
                last.then_inc(y_back, 1)


def stage_product_keys(nc, ctx, sem, sb, ps, g):
    resid, ident, xn = g["resid"], g["ident"], g["xn"]
    stats, mv, work = g["stats"], g["mv"], g["work"]
    PICKS = PK_HEADS * PK_TOP
    TPG = P // PICKS
    GROUPS = TOKENS // TPG
    GPT = P // TPG
    HALF = GPT // 2
    xnT = g["xnT"]
    nsel = TILES * PK_HEADS
    downT = sb("pk_downT", [P, CH, PK_EXPERTS])
    up = sb("pk_up", [P, PK_ROWS, DIM])
    col_table = sb("pk_col_table", [P, P, HALF], BF16)
    row_table = sb("pk_row_table", [P, PK_ROWS * TPG, HALF], BF16)
    packed = sb("pk_packed", [P, 3, TILES, PICKS])
    act0 = sb("pk_act0", [P, PK_ROWS, BLK])
    psD = ps("b_psD", [P, 2, BLK])
    TPB = BLK // P
    EARLY, EARLIER = 12, 6

    def products(pe, blk, r):
        n = blk * PK_ROWS + r
        if n >= 2:
            pe.wait_ge(s["act_ready"], n - 1)
        for c in range(CH):
            last = nc.tensor.matmul(psD[:, n % 2, :], downT[:, c, r * P:(r + 1) * P],
                                    xnT[:, c, blk * BLK:(blk + 1) * BLK], start=(c == 0), stop=(c == CH - 1))
        last.then_inc(s["down_done"], 1)

    def product_silu(act, slots, n):
        blk, r = n // PK_ROWS, n % PK_ROWS
        act.wait_ge(s["down_done"], n + 1)
        if r == 0 and blk >= 2:
            act.wait_ge(s["hid_ready"], (blk - 1) * TPB)
        nc.scalar.activation(slots[blk % 2][:, r, :], psD[:, n % 2, :], ACT.Silu).then_inc(s["act_ready"], 1)

    choice = ctx.enter_context(ExitStack())

    def first(name, shape, dtype=F32):
        return choice.enter_context(nc.sbuf_tensor(name, shape, dtype))

    mix = g["buffer"][:, :].rearrange("p (c n) -> p c n", c=CH)
    top_v = first("pk_top_v", [P, 2, G8, PK_TOP])
    top_i = first("pk_top_i", [P, TILES, G8, PK_TOP], U32)
    sums = first("pk_sums", [P, PK_HEADS, PK_TOP, PK_TOP])
    best = first("pk_best", [P, TILES, PK_HEADS, PK_TOP])
    best_i = first("pk_best_i", [P, TILES, PK_HEADS, PK_TOP], U32)
    iota128 = first("pk_iota128", [P, P])
    rowtab = first("pk_rowtab", [P, PK_ROWS, TPG])
    top_b = first("pk_top_b", [P, 2, PK_TOP, nsel], BF16)
    pos_u = first("pk_pos_u", [P, 2, nsel * PK_TOP], U32)
    pos_b = first("pk_pos_b", [P, 2, PK_TOP, nsel], BF16)
    picked = first("pk_picked", [P, 2, PK_TOP, nsel], BF16)
    expert = first("pk_expert", [P, PK_TOP, nsel])
    onehot = first("pk_onehot", [P, PK_TOP, PK_TOP, nsel], BF16)
    scratch = nc.dram_tensor("pk_scratch", (3, TOKENS, PICKS), F32, kind="Internal").ap()

    s = {n: sem("b_" + n) for n in (
        "tables var std normed transposed evacuated chain wide_in scored scores_used "
        "packed_ready packed_out rows_in rows_tr groups_ready iotas spread down_done act_ready hid_ready "
        "hot_chain hot_ready out_done added pool_chain").split()}
    sc = ctx.enter_context(ExitStack())
    psT = sc.enter_context(nc.psum_tensor("b_psT", [P, 2, BLK], F32))
    psS = sc.enter_context(nc.psum_tensor("b_psS", [P, 2, G8 * PK_KEYS], F32))
    with nc.Block() as block:
        @block.sync
        def _(sp):
            sp.dma_start(downT[:, :, :], g["pk_downT_d"].rearrange("(c p) e -> p c e", p=P)).then_inc(s["wide_in"], 16)
            sp.dma_start(up[:, :, :], g["pk_up_d"].rearrange("(r p) c -> p r c", p=P)).then_inc(s["wide_in"], 16)

        @block.gpsimd
        def _(pool):
            nc.gpsimd.iota(iota128[:, :], [[1, P]], base=0, channel_multiplier=0,
                           allow_small_or_imprecise_dtypes=True).then_inc(s["iotas"], 1)
            nc.gpsimd.iota(rowtab[:, :, :], [[1, PK_ROWS], [0, TPG]], base=0, channel_multiplier=0,
                           allow_small_or_imprecise_dtypes=True).then_inc(s["pool_chain"], 1)
            pool.wait_ge(s["pool_chain"], 1)
            nc.gpsimd.affine_select(out=rowtab[:, :, :], in_=rowtab[:, :, :], compare_op=ALU.is_ge, fill=-1.0,
                                    base=0, pattern=[[0, PK_ROWS], [-PICKS, TPG]], channel_multiplier=1).then_inc(s["pool_chain"], 1)
            pool.wait_ge(s["pool_chain"], 2)
            nc.gpsimd.affine_select(out=rowtab[:, :, :], in_=rowtab[:, :, :], compare_op=ALU.is_ge, fill=-1.0,
                                    base=PICKS - 1, pattern=[[0, PK_ROWS], [PICKS, TPG]], channel_multiplier=-1).then_inc(s["iotas"], 1)
            pool.wait_ge(s["iotas"], 2)
            nc.gpsimd.tensor_copy(col_table[:, :, :], iota128[:, :].unsqueeze(2).to_broadcast([P, P, HALF]))
            nc.gpsimd.tensor_copy(row_table[:, :, :], rowtab[:, :, :].rearrange("p r t -> p (r t)").unsqueeze(2)
                                  .to_broadcast([P, PK_ROWS * TPG, HALF])).then_inc(s["tables"], 1)

        @block.scalar
        def _(act):
            norm_std(nc, act, work, s["var"], s["std"])
            for i in range(TILES):
                act.wait_ge(s["transposed"], i + 1)
                nc.scalar.activation(xnT[:, :, i * P:(i + 1) * P],
                                     psT[:, i % 2, 0:DIM].rearrange("p (c t) -> p c t", c=CH),
                                     ACT.Copy).then_inc(s["evacuated"], 1)
            for n in range(PK_ROWS):
                product_silu(act, (act0,), n)

        @block.vector
        def _(dve):
            link = counter(dve, s["chain"])
            norm_statistics(nc, dve, link, stats, mv, work, s["var"], s["std"])
            for i in range(2):
                norm_tile(nc, dve, i, resid, xn, mv, work, s["normed"], s["transposed"])
            for i in range(TILES):
                if i + 2 < TILES:
                    norm_tile(nc, dve, i + 2, resid, xn, mv, work, s["normed"], s["transposed"])
                dve.wait_ge(s["scored"], i + 1)
                part = psS[:, i % 2, :].rearrange("p (g k) -> p g k", g=G8)
                tv = top_v[:, i % 2, :, :]
                for q in range(G8):
                    last = nc.vector.max(tv[:, q, :], part[:, q, :])
                link(last)
                for q in range(G8):
                    last = nc.vector.max_index(top_i[:, i, q, :], tv[:, q, :], part[:, q, :])
                last.then_inc(s["scores_used"], 1)
                pair = tv.rearrange("p (h z) k -> p h z k", z=2)
                link(nc.vector.tensor_tensor(sums[:, :, :, :],
                                             pair[:, :, 0, :].unsqueeze(3).to_broadcast([P, PK_HEADS, PK_TOP, PK_TOP]),
                                             pair[:, :, 1, :].unsqueeze(2).to_broadcast([P, PK_HEADS, PK_TOP, PK_TOP]), ALU.add))
                flat = sums[:, :, :, :].rearrange("p h a b -> p h (a b)")
                for h in range(PK_HEADS):
                    last = nc.vector.max(best[:, i, h, :], flat[:, h, :])
                link(last)
                for h in range(PK_HEADS):
                    last = nc.vector.max_index(best_i[:, i, h, :], best[:, i, h, :], flat[:, h, :])
                link(last)
            bi = best_i[:, :, :, :].rearrange("p i h k -> p (i h k)")
            link(nc.vector.tensor_scalar(pos_u[:, 0, :], bi, 3, None, ALU.logical_shift_right))
            link(nc.vector.tensor_scalar(pos_u[:, 1, :], bi, PK_TOP - 1, None, ALU.bitwise_and))
            for z in range(2):
                nc.vector.tensor_copy(pos_b[:, z, :, :], pos_u[:, z, :].rearrange("p (n k) -> p k n", k=PK_TOP))
                last = nc.vector.tensor_copy(top_b[:, z, :, :].rearrange("p a (i h) -> p a i h", i=TILES),
                                             top_i[:, :, :, :].rearrange("p i (h z) a -> p z a i h", z=2)[:, z])
            link(last)
            for z in range(2):
                for a in range(PK_TOP):
                    last = nc.vector.tensor_scalar(onehot[:, a, :, :], pos_b[:, z, :, :], float(a), None, ALU.is_equal)
                link(last)
                link(nc.vector.tensor_tensor(onehot[:, :, :, :], onehot[:, :, :, :],
                                             top_b[:, z, :, :].unsqueeze(2).to_broadcast([P, PK_TOP, PK_TOP, nsel]), ALU.mult))
                half = PK_TOP // 2
                while half:
                    out = onehot[:, 0:half, :, :] if half > 1 else picked[:, z:z + 1, :, :]
                    link(nc.vector.tensor_tensor(out, onehot[:, 0:half, :, :], onehot[:, half:2 * half, :, :], ALU.add))
                    half //= 2
            link(nc.vector.scalar_tensor_tensor(expert[:, :, :], picked[:, 0, :, :], float(PK_KEYS), picked[:, 1, :, :], ALU.mult, ALU.add))
            expert_u = pos_u[:, 0, :].rearrange("p (k n) -> p k n", k=PK_TOP)
            part_u = pos_u[:, 1, :].rearrange("p (k n) -> p k n", k=PK_TOP)
            by_pick = part_u.rearrange("p k (i h) -> p h k i", i=TILES)

            def pick_order(v):
                return packed[:, v, :, :].rearrange("p i (h k) -> p h k i", h=PK_HEADS)

            link(nc.vector.tensor_scalar(expert_u, expert[:, :, :], float(PK_EXPERTS - 1), None, ALU.min))
            for v, (op, operand) in enumerate(((ALU.logical_shift_right, 7), (ALU.bitwise_and, P - 1))):
                link(nc.vector.tensor_scalar(part_u, expert_u, operand, None, op))
                for h in range(PK_HEADS):
                    last = nc.vector.tensor_copy(pick_order(v)[:, h], by_pick[:, h])
                link(last)
            nc.vector.tensor_scalar(packed[:, 2, :, :].rearrange("p i k -> p (i k)"),
                                    best[:, :, :, :].rearrange("p i h k -> p (i h k)"), 0.0, None, ALU.max).then_inc(s["packed_ready"], 1)

        @block.tensor
        def _(pe):
            for i in range(TILES + 1):
                if i < TILES:
                    transpose_tile(nc, pe, i, xn, psT, ident, s["normed"], s["transposed"], s["evacuated"])
                if i == 0:
                    continue
                j = i - 1
                pe.wait_ge(s["evacuated"], j + 1)
                if j >= 2:
                    pe.wait_ge(s["scores_used"], j - 1)
                for n in range(2):
                    for c in range(CH):
                        last = nc.tensor.matmul(psS[:, j % 2, n * BLK:(n + 1) * BLK], xnT[:, c, j * P:(j + 1) * P],
                                                mix[:, c, n * BLK:(n + 1) * BLK], start=(c == 0), stop=(c == CH - 1))
                last.then_inc(s["scored"], 1)
            pe.wait_ge(s["wide_in"], 32)
            for r in range(PK_ROWS):
                products(pe, 0, r)

    choice.close()
    rows = sb("pk_rows", [P, 3, GROUPS // P, P])
    groups = sb("pk_groups", [P, 5, GROUPS], BF16)
    weight = xn[:, :, :].rearrange("p a d -> p (a d)")[:, 0:GROUPS]
    colhot = sb("pk_colhot", [P, 2, P, HALF], BF16)
    rowhot = sb("pk_rowhot", [P, 2, 4, PK_ROWS * TPG, HALF], BF16)
    act1 = sb("pk_act1", [P, PK_ROWS, BLK])
    hid = g["buffer"][:, :].rearrange("p (r t) -> p r t", r=PK_ROWS)
    sc.close()
    sc = ctx.enter_context(ExitStack())
    psR = sc.enter_context(nc.psum_tensor("b_psR", [P, BLK], F32))
    psG = sc.enter_context(nc.psum_tensor("b_psG", [P, GPT, PK_ROWS, TPG], F32))
    psO = sc.enter_context(nc.psum_tensor("b_psO", [P, BLK], F32))
    with nc.Block() as block:
        @block.sync
        def _(sp):
            sp.wait_ge(s["packed_ready"], 1)
            for v in range(3):
                sp.dma_start(scratch[v].rearrange("(i p) k -> p i k", p=P), packed[:, v, :, :]).then_inc(s["packed_out"], 16)
            sp.wait_ge(s["packed_out"], 48)
            for v in range(3):
                sp.dma_start(rows[:, v, :, :],
                             scratch[v].rearrange("(j p t) k -> p j (t k)", p=P, t=TPG)).then_inc(s["rows_in"], 16)
            sp.wait_ge(g["zeros_ready"], 1)
            padding = g["sorted_x"].rearrange("(n p) d -> p n d", p=P)
            sp.dma_start(padding[:, :, 0:DIM], g["zeros"][:, :].unsqueeze(1).to_broadcast([P, BLOCKS, DIM])).then_inc(g["zeroed"], 16)
            sp.dma_start(padding[:, :, TAG:ROWW], g["pad_tags"][:, :, :].bitcast(F32)).then_inc(g["zeroed"], 16)

        @block.vector
        def _(dve):
            link = counter(dve, s["hot_chain"])
            dve.wait_ge(s["tables"], 1)
            for v in range(3):
                dve.wait_ge(s["rows_tr"], v + 1)
                nc.vector.tensor_copy(groups[:, v, :] if v < 2 else weight, psR[:, :]).then_inc(s["groups_ready"], 1)
            dve.wait_ge(s["groups_ready"], 3)
            for v in range(2, 5):
                link(nc.vector.tensor_copy(groups[:, v, :], weight))
                if v < 4:
                    link(nc.vector.tensor_tensor(weight, weight, groups[:, v, :], ALU.subtract))

            def hot_tables(i):
                for q in range(2):
                    n = 2 * i + q
                    if n >= 2:
                        dve.wait_ge(s["spread"], n - 1)
                    g0 = n * HALF

                    def of_groups(v, shape):
                        return groups[:, v, g0:g0 + HALF].unsqueeze(1).to_broadcast(shape)

                    shape = [P, PK_ROWS * TPG, HALF]
                    link(nc.vector.tensor_tensor(rowhot[:, q, 0, :, :], row_table[:, :, :], of_groups(0, shape), ALU.is_equal))
                    for v in range(3):
                        nc.vector.tensor_tensor(rowhot[:, q, 1 + v, :, :], rowhot[:, q, 0, :, :], of_groups(2 + v, shape), ALU.mult)
                    shape = [P, P, HALF]
                    nc.vector.tensor_tensor(colhot[:, q, :, :], col_table[:, :, :], of_groups(1, shape),
                                            ALU.is_equal).then_inc(s["hot_ready"], 1)

            hot_tables(0)
            for i in range(TILES):
                blk, off = i // TPB, i % TPB * P
                dve.wait_ge(s["act_ready"], (blk + 1) * PK_ROWS)
                dve.wait_ge(s["spread"], 2 * i + 2)
                if i:
                    dve.wait_ge(s["out_done"], i)
                nc.vector.tensor_tensor(hid[:, :, :].rearrange("p r (g t) -> p r g t", t=TPG),
                                        psG[:, :, :, :].rearrange("p g r t -> p r g t"),
                                        (act0, act1)[blk % 2][:, :, off:off + P].rearrange("p r (g t) -> p r g t", t=TPG),
                                        ALU.mult).then_inc(s["hid_ready"], 1)
                if i:
                    nc.vector.tensor_tensor(resid[:, i - 1, :], psO[:, 0:DIM], resid[:, i - 1, :], ALU.add).then_inc(s["added"], 1)
                if i + 1 < TILES:
                    hot_tables(i + 1)
                if i:
                    dve.wait_ge(s["added"], i)
                    nc.vector.bn_stats(stats[:, i - 1, :], resid[:, i - 1, :])
            dve.wait_ge(s["out_done"], TILES)
            nc.vector.tensor_tensor(resid[:, TILES - 1, :], psO[:, 0:DIM], resid[:, TILES - 1, :], ALU.add).then_inc(s["added"], 1)
            dve.wait_ge(s["added"], TILES)
            nc.vector.bn_stats(stats[:, TILES - 1, :], resid[:, TILES - 1, :])

        @block.scalar
        def _(act):
            for n in range(PK_ROWS, BLKS * PK_ROWS):
                product_silu(act, (act0, act1), n)

        @block.tensor
        def _(pe):
            for r in range(EARLIER):
                products(pe, 1, r)
            pe.wait_ge(s["rows_in"], 48)
            for v in range(3):
                if v:
                    pe.wait_ge(s["groups_ready"], v)
                for j in range(GROUPS // P):
                    last = nc.tensor.transpose(psR[:, j * P:(j + 1) * P], rows[:, v, j, :], ident[:, :])
                last.then_inc(s["rows_tr"], 1)
            for r in range(EARLIER, EARLY):
                products(pe, 1, r)
            for i in range(TILES):
                blk = i // TPB
                if i:
                    pe.wait_ge(s["hid_ready"], i)
                for q in range(2):
                    pe.wait_ge(s["hot_ready"], 2 * i + q + 1)
                    for k in range(HALF):
                        for v in range(3):
                            last = nc.tensor.matmul(psG[:, q * HALF + k, :, :].rearrange("p r t -> p (r t)"), colhot[:, q, :, k],
                                                    rowhot[:, q, 1 + v, :, k], start=(v == 0), stop=(v == 2))
                    last.then_inc(s["spread"], 1)
                if blk + 1 < BLKS:
                    done = EARLY if blk == 0 else 0
                    for r in range(done + (PK_ROWS - done) * (i % TPB) // TPB, done + (PK_ROWS - done) * (i % TPB + 1) // TPB):
                        products(pe, blk + 1, r)
                pe.wait_ge(s["hid_ready"], i + 1)
                if i:
                    pe.wait_ge(s["added"], i)
                for r in range(PK_ROWS):
                    last = nc.tensor.matmul(psO[:, 0:DIM], hid[:, r, :], up[:, r, :], start=(r == 0), stop=(r == PK_ROWS - 1))
                last.then_inc(s["out_done"], 1)
    sc.close()


def stage_attention(nc, ctx, sem, sb, ps, g):
    resid, ctxT, xnT, ident, xn = g["resid"], g["ctxT"], g["xnT"], g["ident"], g["xn"]
    stats, mv, work = g["stats"], g["mv"], g["work"]
    PAIRS = HEADS // 2
    LAG = 3
    K3 = 3 * HD
    PADDED = 64
    identb = sb("c_identb", [P, P], BF16)
    qT = sb("c_qT", [P, PAIRS, TOKENS], BF16)
    kT = sb("c_kT", [P, PAIRS, TOKENS], BF16)
    values = sb("c_values", [P, TILES, DIM], BF16)
    heads_out = xnT[:, :, :].rearrange("p c t -> p (c t)").rearrange("p (i h d) -> p i h d", i=TILES, h=HEADS)
    wp = sb("c_wp", [P, CH, DIM])
    bp = sb("c_bp", [P, DIM])
    v_scale = sb("c_v_scale", [P, CH, 3])
    q_scale = sb("c_q_scale", [P, HEADS, TILES])
    scratch = ctx.enter_context(ExitStack())

    def first(name, shape, dtype=F32):
        return scratch.enter_context(nc.sbuf_tensor(name, shape, dtype))

    wq = first("c_wq", [P, CH, DIM])
    wk = first("c_wk", [P, CH, DIM])
    bq = first("c_bq", [P, 2 * DIM])
    vT = first("c_vT", [P, CH, TOKENS])
    v_int = first("c_v_int", [P, CH, TOKENS], BF16)
    qk = first("c_qk", [P, 2, 2, HEADS, HD])
    amax = first("c_amax", [P, 2, 3, 2, HEADS])
    khat = first("c_khat", [P, 2, 3, HEADS, HD])
    qrows = first("c_qrows", [P, 2, HEADS, PADDED], BF16)
    krows = first("c_krows", [P, 2, HEADS, PADDED], BF16)

    s = {n: sem("c_" + n) for n in (
        "var std normed transposed evacuated chain w_in late_in projected v_in v_ready v_tr v_back "
        "quantised q_rows k_rows k_scaled k_chain rows_tr rows_back consts pool_chain q_loaded scored s_taken bias_ready exp_done "
        "rounded p_tr p_back pv_done normalised bchain inverted o_tr o_back out_done added scale_ready passed biased").split()}
    sc = ctx.enter_context(ExitStack())
    psT = sc.enter_context(nc.psum_tensor("c_psT", [P, 2, BLK], F32))
    psQ = sc.enter_context(nc.psum_tensor("c_psQ", [P, 2, BLK], F32))
    psV = sc.enter_context(nc.psum_tensor("c_psV", [P, 2, BLK], F32))
    psR = sc.enter_context(nc.psum_tensor("c_psR", [P, 2, PAIRS, P], BF16))
    with nc.Block() as block:
        @block.sync
        def _(sp):
            sp.dma_start(wk[:, :, :], g["wkv_d"][:, 0:DIM].rearrange("(c p) n -> p c n", p=P)).then_inc(s["w_in"], 16)
            sp.dma_start(wq[:, :, :], g["wq_d"].rearrange("(c p) n -> p c n", p=P)).then_inc(s["w_in"], 16)
            sp.dma_start(bq[:, 0:DIM], g["bq_d"].to_broadcast([P, DIM])).then_inc(s["w_in"], 16)
            sp.dma_start(bq[:, DIM:], g["bkv_d"][:, 0:DIM].to_broadcast([P, DIM])).then_inc(s["w_in"], 16)
            sp.dma_start(vT[:, :, :], g["values_d"].rearrange("(c p) t -> p c t", p=P)).then_inc(s["v_in"], 16)
            sp.dma_start(bp[:, :], g["bp_d"].to_broadcast([P, DIM])).then_inc(s["late_in"], 16)
            sp.dma_start(wp[:, :, :], g["wp_d"].rearrange("(c p) n -> p c n", p=P)).then_inc(s["late_in"], 16)

        @block.gpsimd
        def _(pool):
            nc.gpsimd.tensor_copy(identb[:, :], ident[:, :])
            nc.gpsimd.memset(qrows[:, :, :, :], 0.0)
            nc.gpsimd.memset(krows[:, :, :, :], 0.0).then_inc(s["consts"], 1)
            steps = 0
            for i in range(TILES):
                u = i % 2
                pool.wait_ge(s["k_scaled"], i + 1)
                if i >= 2:
                    pool.wait_ge(s["rows_tr"], 2 * i - 2)
                for part in range(3):
                    kp = krows[:, u, :, part * HD:(part + 1) * HD]
                    copy = nc.gpsimd.tensor_copy(kp, khat[:, u, part, :, :])
                    if part == 2:
                        copy.then_inc(s["k_rows"], 1)
                    else:
                        copy.then_inc(s["k_chain"], 1)
                        pool.wait_ge(s["k_chain"], steps + 1)
                        nc.gpsimd.tensor_tensor(khat[:, u, part + 1, :, :], khat[:, u, part, :, :], kp, ALU.subtract).then_inc(s["k_chain"], 1)
                        pool.wait_ge(s["k_chain"], steps + 2)
                        steps += 2

        def store_rows(i, act):
            for n, dst in ((2 * i, qT), (2 * i + 1, kT)):
                act.wait_ge(s["rows_tr"], n + 1)
                nc.scalar.activation(dst[:, :, i * P:(i + 1) * P], psR[:, n % 2, :, :], ACT.Copy).then_inc(s["rows_back"], 1)

        def query_rows(i, act):
            act.wait_ge(s["quantised"], i + 1)
            act.wait_ge(s["consts"], 1)
            if i >= 2:
                act.wait_ge(s["rows_tr"], 2 * i - 2)
            nc.scalar.activation(qrows[:, i % 2, :, 0:K3].rearrange("p h (j d) -> p h j d", j=3),
                                 qk[:, i % 2, 0, :, :].unsqueeze(2).to_broadcast([P, HEADS, 3, HD]), ACT.Copy).then_inc(s["q_rows"], 1)

        @block.scalar
        def _(act):
            norm_std(nc, act, work, s["var"], s["std"])
            for i in range(TILES):
                act.wait_ge(s["transposed"], i + 1)
                nc.scalar.activation(xnT[:, :, i * P:(i + 1) * P],
                                     psT[:, i % 2, 0:DIM].rearrange("p (c t) -> p c t", c=CH),
                                     ACT.Copy).then_inc(s["evacuated"], 1)
                if i:
                    query_rows(i - 1, act)
                if i >= 3:
                    store_rows(i - 3, act)
            query_rows(TILES - 1, act)
            for i in range(TILES - 3, TILES):
                store_rows(i, act)

        @block.vector
        def _(dve):
            link = counter(dve, s["chain"])
            norm_statistics(nc, dve, link, stats, mv, work, s["var"], s["std"])
            for i in range(2):
                norm_tile(nc, dve, i, resid, xn, mv, work, s["normed"], s["transposed"])
            def quantise_values():
                dve.wait_ge(s["v_in"], 16)
                for c in range(CH):
                    last = nc.vector.tensor_reduce(v_scale[:, c, 0:1], vT[:, c, :], AX.X, ALU.max, apply_absolute_value=True)
                link(last)
                link(nc.vector.tensor_scalar(v_scale[:, :, 1], v_scale[:, :, 0], 1.0 / 127.0, 1e-8, ALU.mult, ALU.max))
                link(nc.vector.reciprocal(v_scale[:, :, 2], v_scale[:, :, 1]))
                for c in range(CH):
                    last = nc.vector.tensor_scalar(vT[:, c, :], vT[:, c, :], v_scale[:, c, 2:3], ROUND, ALU.mult, ALU.add)
                link(last)
                for c in range(CH):
                    nc.vector.tensor_scalar(v_int[:, c, :], vT[:, c, :], ROUND, None, ALU.subtract).then_inc(s["v_ready"], 1)
                dve.wait_ge(s["late_in"], 32)
                for c in range(CH):
                    nc.vector.tensor_scalar(wp[:, c, :], wp[:, c, :], v_scale[:, c, 1:2], None, ALU.mult)

            for i in range(TILES):
                if i == 8:
                    quantise_values()
                if i + 2 < TILES:
                    norm_tile(nc, dve, i + 2, resid, xn, mv, work, s["normed"], s["transposed"])
                u = i % 2
                if i >= 2:
                    dve.wait_ge(s["q_rows"], i - 1)
                    dve.wait_ge(s["k_rows"], i - 1)
                t = qk[:, u, :, :, :]
                tf = t.rearrange("p z h d -> p z (h d)")
                dve.wait_ge(s["projected"], i + 1)
                link(nc.vector.tensor_tensor(t.rearrange("p z h d -> p (z h d)"), psQ[:, u, :], bq[:, :], ALU.add))
                m = amax[:, u, :, :, :]
                link(nc.vector.tensor_reduce(m[:, 0, :, :], t, AX.X, ALU.max, apply_absolute_value=True))
                nc.vector.tensor_scalar(m[:, 1, 0, :], m[:, 0, 0, :], 0.25 / 127.0, 1e-8, ALU.mult, ALU.max)
                link(nc.vector.tensor_scalar(m[:, 1, 1, :], m[:, 0, 1, :], 1.0 / 127.0, 1e-8, ALU.mult, ALU.max))
                link(nc.vector.reciprocal(m[:, 2, :, :], m[:, 1, :, :]))
                nc.vector.tensor_copy(q_scale[:, :, i], m[:, 1, 0, :])
                link(nc.vector.tensor_scalar(m[:, 2, 0, :], m[:, 2, 0, :], 0.25, None, ALU.mult))
                link(nc.vector.tensor_tensor(t, t, m[:, 2, :, :].unsqueeze(3).to_broadcast([P, 2, HEADS, HD]), ALU.mult))
                nc.vector.tensor_scalar(tf, tf, ROUND, ROUND, ALU.add, ALU.subtract).then_inc(s["quantised"], 1)
                dve.wait_ge(s["quantised"], i + 1)
                nc.vector.tensor_tensor(khat[:, u, 0, :, :], t[:, 1, :, :],
                                        m[:, 1, 1, :].unsqueeze(2).to_broadcast([P, HEADS, HD]), ALU.mult).then_inc(s["k_scaled"], 1)
            for i in range(TILES):
                dve.wait_ge(s["v_tr"], i + 1)
                nc.vector.tensor_copy(values[:, i, :], psV[:, i % 2, 0:P].bitcast(BF16)).then_inc(s["v_back"], 1)

        @block.tensor
        def _(pe):
            pe.wait_ge(s["w_in"], 64)
            pe.wait_ge(s["consts"], 1)

            def rows_of(i):
                for n, src, ready in ((2 * i, qrows, "q_rows"), (2 * i + 1, krows, "k_rows")):
                    pe.wait_ge(s[ready], i + 1)
                    if n >= 2:
                        pe.wait_ge(s["rows_back"], n - 1)
                    for p in range(PAIRS):
                        last = nc.tensor.transpose(psR[:, n % 2, p, :],
                                                   src[:, i % 2, 2 * p:2 * p + 2, :].rearrange("p h d -> p (h d)"), identb[:, :])
                    last.then_inc(s["rows_tr"], 1)

            def project(i):
                pe.wait_ge(s["evacuated"], i + 1)
                if i >= 2:
                    pe.wait_ge(s["quantised"], i - 1)
                for z in range(2):
                    src, w = ((xnT, wq), (ctxT, wk))[z]
                    for k in range(CH):
                        last = nc.tensor.matmul(psQ[:, i % 2, z * DIM:(z + 1) * DIM], src[:, k, i * P:(i + 1) * P],
                                                w[:, k, 0:DIM], start=(k == 0), stop=(k == CH - 1))
                last.then_inc(s["projected"], 1)

            for i in range(TILES + LAG):
                if i < TILES:
                    transpose_tile(nc, pe, i, xn, psT, ident, s["normed"], s["transposed"], s["evacuated"])
                if 1 <= i <= TILES:
                    project(i - 1)
                if i >= LAG:
                    rows_of(i - LAG)
            pe.wait_ge(s["v_ready"], CH)
            for i in range(TILES):
                if i >= 2:
                    pe.wait_ge(s["v_back"], i - 1)
                for c in range(CH):
                    last = nc.tensor.transpose(psV[:, i % 2, 0:P].bitcast(BF16)[:, c * P:(c + 1) * P],
                                               v_int[:, c, i * P:(i + 1) * P], identb[:, :])
                last.then_inc(s["v_tr"], 1)

    sc.close()
    scratch.close()
    PER_BODY = 4 * TILES
    PER_PAIR = 2 * TILES
    BODIES = PAIRS // 2
    HALFW = TOKENS // 2
    ROUNDED, STORED, TURNED, SUMMED = 2, 3, 4, 5
    qh = sb("c_qh", [P, 2, TOKENS], BF16)
    kh = sb("c_kh", [P, 2, TOKENS], BF16)
    sq = sb("c_sq", [P, 2, 2, TILES, 2])
    scores = sb("c_scores", [P, 2, TOKENS])
    exps = sb("c_exps", [P, 2, TOKENS])
    probs = sb("c_probs", [P, 2, TOKENS], BF16)
    probsT = sb("c_probsT", [P, 2, TILES, P], BF16)
    row = sb("c_row", [P, 2, 4])
    sums = sb("c_sums", [P, 2, PER_PAIR])
    sc = ctx.enter_context(ExitStack())
    psS = sc.enter_context(nc.psum_tensor("c_psS", [P, 2, HALFW], F32))
    psP = sc.enter_context(nc.psum_tensor("c_psP", [P, TILES, P], BF16))
    psO = sc.enter_context(nc.psum_tensor("c_psO", [P, 2, PER_PAIR, HD], F32))

    def at(b, j):
        q = j % PER_BODY // PER_PAIR
        pair = b * 2 + (q if j >= 0 else q - 2)
        return b * PER_BODY + j, pair, q, j % PER_PAIR, j % PER_PAIR // TILES, j % TILES

    with nc.Block() as block:
        @block.tensor
        def _(pe):
            def score(b, j):
                n, pair, q, place, u, i = at(b, j)
                if isinstance(pair, int):
                    queries, keys = qT[:, pair, :], kT[:, pair, :]
                else:
                    queries, keys = qh[:, q, :], kh[:, q, :]
                    if place == 0:
                        pe.wait_ge(s["q_loaded"], pair - 1)
                r0 = PADDED * u
                for half in range(2):
                    if not isinstance(n, int) or n:
                        pe.wait_ge(s["s_taken"], n * 2 + half - 1)
                    for k in range(2):
                        k0 = half * HALFW + k * BLK
                        last = nc.tensor.matmul(psS[:, half, k * BLK:(k + 1) * BLK], queries[r0:r0 + K3, i * P:(i + 1) * P],
                                                keys[r0:r0 + K3, k0:k0 + BLK], start=True, stop=True)
                    last.then_inc(s["scored"], 1)

            def turn(b, j):
                n, pair, q, place, u, i = at(b, j)
                pe.wait_ge(s["rounded"], n + 1)
                if not isinstance(n, int) or n:
                    pe.wait_ge(s["p_back"], n)
                for c in range(TILES):
                    last = nc.tensor.transpose(psP[:, c, :], probs[:, j % 2, c * P:(c + 1) * P], identb[:, :])
                last.then_inc(s["p_tr"], 1)

            def weigh(b, j):
                n, pair, q, place, u, i = at(b, j)
                if place == 0 and not (isinstance(pair, int) and pair < 2):
                    pe.wait_ge(s["normalised"], pair - 1)
                pe.wait_ge(s["p_back"], n + 1)
                cols = slice((pair * 2 + u) * HD, (pair * 2 + u + 1) * HD) if isinstance(pair, int) else bass.ds((pair * 2 + u) * HD, HD)
                for c in range(TILES):
                    last = nc.tensor.matmul(psO[:, q, place, :], probsT[:, j % 2, c, :], values[:, c, cols],
                                            start=(c == 0), stop=(c == TILES - 1))
                last.then_inc(s["pv_done"], 1)

            def steps(b, first):
                for j in range(PER_BODY):
                    score(b, j)
                    if not first or j >= TURNED:
                        turn(b, j - TURNED)
                    if not first or j >= SUMMED:
                        weigh(b, j - SUMMED)

            steps(0, True)
            with pe.Fori(1, BODIES) as b:
                steps(b, False)
            for j in range(SUMMED):
                if j < TURNED:
                    turn(BODIES, j - TURNED)
                weigh(BODIES, j - SUMMED)

        @block.gpsimd
        def _(pool):
            def load(b, q):
                pair = b * 2 + q
                if not isinstance(b, int):
                    pool.wait_ge(s["exp_done"], (pair - 1) * PER_PAIR)
                one = slice(pair, pair + 1) if isinstance(b, int) else bass.ds(pair, 1)
                two = slice(pair * 2, pair * 2 + 2) if isinstance(b, int) else bass.ds(pair * 2, 2)
                if not isinstance(b, int):
                    nc.gpsimd.tensor_copy(qh[:, q, :], qT[:, one, :].rearrange("p a t -> p (a t)"))
                    nc.gpsimd.tensor_copy(kh[:, q, :], kT[:, one, :].rearrange("p a t -> p (a t)")).then_inc(s["q_loaded"], 1)
                nc.gpsimd.tensor_copy(sq[:, q, 0, :, :], q_scale[:, two, :].rearrange("p h i -> p i h")).then_inc(s["pool_chain"], 1)
                pool.wait_ge(s["pool_chain"], pair + 1)
                pool.sem_inc(s["passed"], 1)
                nc.gpsimd.tensor_scalar(sq[:, q, 1, :, :], sq[:, q, 0, :, :], -1.0, None, ALU.mult).then_inc(s["scale_ready"], 1)

            load(0, 0)
            load(0, 1)
            pool.wait_ge(s["late_in"], 32)
            for i in range(TILES):
                nc.gpsimd.tensor_tensor(resid[:, i, :], resid[:, i, :], bp[:, :], ALU.add).then_inc(s["biased"], 1)
            with pool.Fori(1, BODIES) as b:
                load(b, 0)
                load(b, 1)

        @block.scalar
        def _(act):
            def exponential(b, j):
                n, pair, q, place, u, i = at(b, j)
                if place == 0 and not (isinstance(pair, int) and pair < 2):
                    act.wait_ge(s["normalised"], pair - 1)
                act.wait_ge(s["bias_ready"], n + 1)
                nc.scalar.activation(exps[:, j % 2, :], scores[:, j % 2, :], ACT.Exp, bias=row[:, j % 2, 3:4],
                                     scale=sq[:, q, 0, i, u:u + 1], accum_out=sums[:, q, place:place + 1]).then_inc(s["exp_done"], 1)

            def store(b, j):
                n = at(b, j)[0]
                act.wait_ge(s["p_tr"], n + 1)
                if not isinstance(n, int) or n >= 2:
                    act.wait_ge(s["pv_done"], n - 1)
                nc.scalar.activation(probsT[:, j % 2, :, :], psP[:, :, :], ACT.Copy).then_inc(s["p_back"], 1)

            def steps(b, first):
                for j in range(PER_BODY):
                    exponential(b, j)
                    if not first or j >= STORED:
                        store(b, j - STORED)

            steps(0, True)
            with act.Fori(1, BODIES) as b:
                steps(b, False)
            for j in range(STORED):
                store(BODIES, j - STORED)

        @block.vector
        def _(dve):
            def take(b, j):
                n = at(b, j)[0]
                if not isinstance(n, int) or n >= 2:
                    dve.wait_ge(s["exp_done"], n - 1)
                for half in range(2):
                    dve.wait_ge(s["scored"], n * 2 + half + 1)
                    nc.vector.tensor_scalar(scores[:, j % 2, half * HALFW:(half + 1) * HALFW], psS[:, half, :], 0.0, -3.0e38,
                                            ALU.add, ALU.max, accum_out=row[:, j % 2, half:half + 1]).then_inc(s["s_taken"], 1)

            def round_half(b, j, half):
                n = at(b, j)[0]
                if half == 0:
                    dve.wait_ge(s["exp_done"], n + 1)
                    if not isinstance(n, int) or n >= 2:
                        dve.wait_ge(s["p_tr"], n - 1)
                part = slice(half * HALFW, (half + 1) * HALFW)
                last = nc.vector.tensor_scalar(probs[:, j % 2, part], exps[:, j % 2, part], ROUND, ROUND, ALU.add, ALU.subtract)
                if half:
                    last.then_inc(s["rounded"], 1)

            def steps(b, first):
                for j in range(PER_BODY):
                    n, pair, q, place, u, i = at(b, j)
                    r = row[:, j % 2, :]
                    take(b, j)
                    behind = not first or j >= ROUNDED
                    if behind:
                        round_half(b, j - ROUNDED, 0)
                    dve.wait_ge(s["s_taken"], n * 2 + 2)
                    nc.vector.tensor_tensor(r[:, 2:3], r[:, 0:1], r[:, 1:2], ALU.max).then_inc(s["bchain"], 1)
                    if behind:
                        round_half(b, j - ROUNDED, 1)
                    if place == 0:
                        dve.wait_ge(s["scale_ready"], pair + 1)
                    dve.wait_ge(s["bchain"], n + 1)
                    nc.vector.tensor_scalar(r[:, 3:4], r[:, 2:3], sq[:, q, 1, i, u:u + 1], LN255, ALU.mult, ALU.add).then_inc(s["bias_ready"], 1)
                    if place == SUMMED + 2 and (not first or j > PER_PAIR):
                        normalise(b, j - place - 1)

            def normalise(b, j):
                n, pair, q, place, u, i = at(b, j)
                dve.wait_ge(s["pv_done"], n + 1)
                nc.vector.reciprocal(sums[:, q, :], sums[:, q, :]).then_inc(s["inverted"], 1)
                dve.wait_ge(s["inverted"], pair + 1)
                heads = slice(pair * 2, pair * 2 + 2) if isinstance(pair, int) else bass.ds(pair * 2, 2)
                nc.vector.tensor_tensor(heads_out[:, :, heads, :].rearrange("p i u d -> p u i d"),
                                        psO[:, q, :, :].rearrange("p (u i) d -> p u i d", u=2),
                                        sums[:, q, :].rearrange("p (u i) -> p u i", u=2).unsqueeze(3).to_broadcast([P, 2, TILES, HD]),
                                        ALU.mult).then_inc(s["normalised"], 1)

            steps(0, True)
            with dve.Fori(1, BODIES) as b:
                steps(b, False)
            for j in range(ROUNDED):
                for half in range(2):
                    round_half(BODIES, j - ROUNDED, half)
            normalise(BODIES, -1)

    sc.close()
    sc = ctx.enter_context(ExitStack())
    oT = sb("c_oT", [P, 2, DIM])
    psT2 = sc.enter_context(nc.psum_tensor("c_psT2", [P, 2, BLK], F32))
    psO2 = sc.enter_context(nc.psum_tensor("c_psO2", [P, 2, BLK], F32))
    with nc.Block() as block:
        @block.tensor
        def _(pe):
            for i in range(TILES + 1):
                if i < TILES:
                    if i >= 2:
                        pe.wait_ge(s["o_back"], i - 1)
                    for c in range(CH):
                        last = nc.tensor.transpose(psT2[:, i % 2, c * P:(c + 1) * P], heads_out[:, i, c * HEADS // CH:(c + 1) * HEADS // CH, :].rearrange("p h d -> p (h d)"), ident[:, :])
                    last.then_inc(s["o_tr"], 1)
                if i:
                    j = i - 1
                    pe.wait_ge(s["o_back"], j + 1)
                    if j >= 2:
                        pe.wait_ge(s["added"], j - 1)
                    for c in range(CH):
                        last = nc.tensor.matmul(psO2[:, j % 2, 0:DIM], oT[:, j % 2, c * P:(c + 1) * P], wp[:, c, :],
                                                start=(c == 0), stop=(c == CH - 1))
                    last.then_inc(s["out_done"], 1)

        @block.scalar
        def _(act):
            for i in range(TILES):
                act.wait_ge(s["o_tr"], i + 1)
                if i >= 2:
                    act.wait_ge(s["out_done"], i - 1)
                nc.scalar.activation(oT[:, i % 2, :], psT2[:, i % 2, 0:DIM], ACT.Copy).then_inc(s["o_back"], 1)

        @block.vector
        def _(dve):
            dve.wait_ge(s["biased"], TILES)
            for i in range(TILES):
                dve.wait_ge(s["out_done"], i + 1)
                nc.vector.tensor_tensor(resid[:, i, :], psO2[:, i % 2, 0:DIM], resid[:, i, :], ALU.add).then_inc(s["added"], 1)
                if i:
                    dve.wait_ge(s["added"], i)
                    nc.vector.bn_stats(stats[:, i - 1, :], resid[:, i - 1, :])
            dve.wait_ge(s["added"], TILES)
            nc.vector.bn_stats(stats[:, TILES - 1, :], resid[:, TILES - 1, :])
    sc.close()


def stage_experts(nc, ctx, sem, sb, ps, g):
    resid, xnT, ident = g["resid"], g["xnT"], g["ident"]
    stats, mv, work = g["stats"], g["mv"], g["work"]
    LOG = MOE + 1
    PER_BANK = TILES // 2
    CHOICES = TILES * MOE_TOP
    HIDDEN = (P, UPCOLS - 2 * P)
    scattered_rows, expert_rows = g["sorted_x"], g["sorted_y"]
    expert_of = nc.dram_tensor("d_expert_of", (P, 1), U32, kind="Internal").ap()

    slot_u = sb("d_slot_u", [P, CHOICES], U32)
    top = sb("d_top", [P, TILES, 8])
    shared_gate = sb("d_shared_gate", [P, TILES])
    block_expert = sb("d_block_expert", [1, P], U32)
    xn_all = sb("d_xn_all", [P, TILES, ROWW])
    s = {n: sem("d_" + n) for n in (
        "var std normed transposed evacuated chain g_in consts pool_chain logged lready exp_done masked ranked "
        "slots_ready expert_ready expert_out expert_in scattered sw_in0 sw_in1 up_done silu h_ready down_done added "
        "rchain ranks_taken tagged passed x_tr x_back b_up b_silu b_h b_down b_y combined stored").split()}
    for x in range(SLOTS):
        s[f"in{x}"], s[f"out{x}"] = sem(f"d_in{x}"), sem(f"d_out{x}")

    gates = sb("d_gates", [P, CH, LOG])
    iota = sb("d_iota", [P, MOE])
    block_no = sb("d_block_no", [P, 1])
    before = sb("d_before", [P, P], BF16)
    ones = sb("d_ones", [P, P], BF16)
    logits = sb("d_logits", [P, TILES, LOG])
    pr = sb("d_probs", [P, TILES, LOG])
    small = sb("d_small", [P, 3, TILES])
    top_i = sb("d_top_i", [P, TILES, 8], U32)
    top_f = sb("d_top_f", [P, TILES, 8])
    chosen = sb("d_chosen", [P, TILES, MOE_TOP, MOE])
    mask = sb("d_mask", [P, TILES, MOE], BF16)
    earlier = sb("d_earlier", [P, TILES + 1, MOE], BF16)
    ones_f = sb("d_ones_f", [P, MOE])
    blocks_u = sb("d_blocks_u", [P, MOE], U32)
    blocks = sb("d_blocks", [P, 4, MOE])
    slot_of = sb("d_slot_of", [P, TILES, MOE])
    slot_f = sb("d_slot_f", [P, CHOICES])
    be = sb("d_be", [P, 2])
    be_u = sb("d_be_u", [P, 1], U32)

    sc = ctx.enter_context(ExitStack())
    psT = sc.enter_context(nc.psum_tensor("d_psT", [P, 2, BLK], F32))
    psL = sc.enter_context(nc.psum_tensor("d_psL", [P, 2, BLK], F32))
    with nc.Block() as block:
        @block.sync
        def _(sp):
            sp.dma_start(gates[:, :, :], g["gates_d"].rearrange("(c p) n -> p c n", p=P)).then_inc(s["g_in"], 16)

        @block.gpsimd
        def _(pool):
            nc.gpsimd.iota(iota[:, :], [[1, MOE]], base=0, channel_multiplier=0, allow_small_or_imprecise_dtypes=True)
            nc.gpsimd.iota(block_no[:, :], [[0, 1]], base=0, channel_multiplier=1, allow_small_or_imprecise_dtypes=True)
            nc.gpsimd.memset(ones[:, :], 1.0)
            nc.gpsimd.memset(ones_f[:, :], 1.0)
            nc.gpsimd.memset(earlier[:, 0, :], 0.0)
            nc.gpsimd.memset(before[:, :], 1.0).then_inc(s["pool_chain"], 1)
            pool.wait_ge(s["pool_chain"], 1)
            nc.gpsimd.affine_select(out=before[:, :], in_=before[:, :], compare_op=ALU.is_ge, fill=0.0,
                                    base=-1, pattern=[[1, P]], channel_multiplier=-1).then_inc(s["consts"], 1)

        @block.scalar
        def _(act):
            norm_std(nc, act, work, s["var"], s["std"])
            for i in range(TILES):
                act.wait_ge(s["transposed"], i + 1)
                nc.scalar.activation(xnT[:, :, i * P:(i + 1) * P],
                                     psT[:, i % 2, 0:DIM].rearrange("p (c t) -> p c t", c=CH),
                                     ACT.Copy).then_inc(s["evacuated"], 1)

        @block.vector
        def _(dve):
            link = counter(dve, s["chain"])
            norm_statistics(nc, dve, link, stats, mv, work, s["var"], s["std"])
            for i in range(TILES):
                nc.vector.tensor_scalar(xn_all[:, i, 0:DIM], resid[:, i, :], mv[:, i, 0:1], work[:, 2, i:i + 1],
                                        ALU.subtract, ALU.mult).then_inc(s["normed"], 1)
            dve.wait_ge(s["logged"], TILES)
            for b in range(2):
                last = nc.vector.tensor_copy(logits[:, b * PER_BANK:(b + 1) * PER_BANK, :],
                                             psL[:, b, 0:PER_BANK * LOG].rearrange("p (i e) -> p i e", e=LOG))

        @block.tensor
        def _(pe):
            pe.wait_ge(s["g_in"], 16)
            for i in range(TILES + 1):
                if i < TILES:
                    pe.wait_ge(s["normed"], i + 1)
                    if i >= 2:
                        pe.wait_ge(s["evacuated"], i - 1)
                    for c in range(CH):
                        last = nc.tensor.transpose(psT[:, i % 2, c * P:(c + 1) * P], xn_all[:, i, c * P:(c + 1) * P], ident[:, :])
                    last.then_inc(s["transposed"], 1)
                if i:
                    j = i - 1
                    pe.wait_ge(s["evacuated"], j + 1)
                    o = (j % PER_BANK) * LOG
                    for c in range(CH):
                        last = nc.tensor.matmul(psL[:, j // PER_BANK, o:o + LOG], xnT[:, c, j * P:(j + 1) * P], gates[:, c, :],
                                                start=(c == 0), stop=(c == CH - 1))
                    last.then_inc(s["logged"], 1)
    sc.close()

    wide = sb("d_wide", [P, SLOTS, WCOLS])
    rest = sb("d_rest", [REST, SLOTS, DIM])

    def w_up(x, c, first, width):
        return wide[:, x, c * UPCOLS + first:c * UPCOLS + first + width]

    gate = sb("d_gate", [P, 2, 2, BLK])
    hidden = sb("d_hidden", [P, 2, 2, BLK])
    sc = ctx.enter_context(ExitStack())
    psU = sc.enter_context(nc.psum_tensor("d_psU", [P, 2, 3, BLK], F32))
    psD = sc.enter_context(nc.psum_tensor("d_psD", [P, 2, BLK], F32))
    STEPS = SHARED * BLKS
    MASKED, RANKED = 3, 4
    loads = (s["sw_in0"], s["sw_in1"])
    ranks = psU[:, (RANKED + 1) % 2, 0:2, :]
    totals = psU[:, (RANKED + 1) % 2, 2, 0:MOE]
    with nc.Block() as block:
        @block.sync
        def _(sp):
            def load(e):
                x = e % 2
                if e >= 2:
                    sp.wait_ge(s["down_done"], 2 * BLKS * (e - 1))
                sp.dma_start(wide[:, x, :], g["swide_d"][e]).then_inc(loads[x], 16)
                sp.dma_start(rest[:, x, :], g["srest_d"][e]).then_inc(loads[x], 16)

            load(0)
            load(1)
            sp.wait_ge(s["expert_ready"], 1)
            sp.dma_start(expert_of, be_u[:, :]).then_inc(s["expert_out"], 16)
            sp.wait_ge(s["expert_out"], 16)
            sp.dma_start(block_expert[:, :], expert_of.rearrange("p a -> a p")).then_inc(s["expert_in"], 16)
            load(2)
            load(3)
            sp.wait_ge(s["expert_in"], 16)

        @block.gpsimd
        def _(pool):
            pool.wait_ge(s["slots_ready"], 1)
            pool.wait_ge(g["zeroed"], 32)
            tags = xn_all[:, :, TAG:ROWW].bitcast(U32)
            for k in range(MOE_TOP):
                if k:
                    pool.wait_ge(s["scattered"], 16 * TILES * k)
                nc.gpsimd.iota(tags, [[P, TILES], [0, ROWW - TAG]], base=k * TOKENS, channel_multiplier=1).then_inc(s["tagged"], 1)
                pool.wait_ge(s["tagged"], k + 1)
                for i in range(TILES):
                    c = i * MOE_TOP + k
                    nc.gpsimd.indirect_dma_start(out=scattered_rows, out_offset=bass.IndirectOffsetOnAxis(ap=slot_u[:, c:c + 1], axis=0),
                                                 in_=xn_all[:, i, :], in_offset=None).then_inc(s["scattered"], 16)
            pool.wait_ge(s["scattered"], 16 * CHOICES)

        @block.tensor
        def _(pe):
            for n in range(STEPS + 1):
                if n < STEPS:
                    e, b = n // BLKS, n % BLKS
                    x = e % 2
                    if b == 0:
                        pe.wait_ge(loads[x], (e // 2 + 1) * 32)
                    if n >= 2:
                        pe.wait_ge(s["h_ready"], n - 1)
                    if n == RANKED + 1:
                        pe.wait_ge(s["ranks_taken"], 1)
                    for k in range(3):
                        width = P if k < 2 else HIDDEN[1]
                        for c in range(CH):
                            last = nc.tensor.matmul(psU[0:width, n % 2, k, :], w_up(x, c, k * P, width),
                                                    xnT[:, c, b * BLK:(b + 1) * BLK], start=(c == 0), stop=(c == CH - 1))
                    last.then_inc(s["up_done"], 1)
                if n:
                    m = n - 1
                    e, b = m // BLKS, m % BLKS
                    x = e % 2
                    pe.wait_ge(s["h_ready"], m + 1)
                    for half in range(2):
                        if m:
                            pe.wait_ge(s["added"], (m - 1) * 2 + half + 1)
                        for j in range(2):
                            t0 = (2 * half + j) * P
                            out = psD[:, half, j * DIM:(j + 1) * DIM]
                            nc.tensor.matmul(out, hidden[:, m % 2, 0, t0:t0 + P], wide[:, x, DOWN0:WCOLS], start=True, stop=False)
                            last = nc.tensor.matmul(out, hidden[0:REST, m % 2, 1, t0:t0 + P], rest[:, x, :], start=False, stop=True)
                        last.then_inc(s["down_done"], 1)
                if n == RANKED:
                    pe.wait_ge(s["masked"], 1)
                    pe.wait_ge(s["consts"], 1)
                    pe.wait_ge(s["h_ready"], n)
                    nc.tensor.matmul(totals, ones[:, :], earlier[:, TILES, :], start=True, stop=True)
                    for i in range(TILES):
                        o = (i % PER_BANK) * MOE
                        dst = ranks[:, i // PER_BANK, o:o + MOE]
                        nc.tensor.matmul(dst, before[:, :], mask[:, i, :], start=True, stop=False)
                        last = nc.tensor.matmul(dst, ones[:, :], earlier[:, i, :], start=False, stop=True)
                    last.then_inc(s["ranked"], 1)

        @block.scalar
        def _(act):
            act.wait_ge(s["lready"], 1)
            nc.scalar.activation(pr[:, :, 0:MOE], logits[:, :, 0:MOE], ACT.Exp)
            nc.scalar.activation(pr[:, :, MOE], logits[:, :, MOE], ACT.Exp, scale=-1.0).then_inc(s["exp_done"], 1)
            for n in range(STEPS):
                act.wait_ge(s["up_done"], n + 1)
                if n >= 2:
                    act.wait_ge(s["h_ready"], n - 1)
                nc.scalar.activation(gate[:, n % 2, 0, :], psU[:, n % 2, 0, :], ACT.Silu)
                nc.scalar.activation(gate[0:REST, n % 2, 1, :], psU[0:REST, n % 2, 2, :], ACT.Silu).then_inc(s["silu"], 1)

        @block.vector
        def _(dve):
            link = counter(dve, s["rchain"])
            routed = logits[:, :, 0:MOE]
            wide_shape = [P, TILES, MOE]

            def one_hot(k):
                return nc.vector.tensor_tensor(chosen[:, :, k, :], top_f[:, :, k:k + 1].to_broadcast(wide_shape),
                                               iota[:, :].unsqueeze(1).to_broadcast(wide_shape), ALU.is_equal)

            def probabilities():
                dve.wait_ge(s["exp_done"], 1)
                nc.vector.tensor_scalar(small[:, 2, :], pr[:, :, MOE], 1.0, None, ALU.add)
                link(nc.vector.reduce_sum(small[:, 1, :], pr[:, :, 0:MOE], AX.X))
                nc.vector.reciprocal(shared_gate[:, :], small[:, 2, :])
                link(nc.vector.reciprocal(small[:, 1, :], small[:, 1, :]))
                link(nc.vector.tensor_tensor(pr[:, :, 0:MOE], pr[:, :, 0:MOE], small[:, 1, :].unsqueeze(2).to_broadcast(wide_shape), ALU.mult))
                for i in range(TILES):
                    last = nc.vector.max(top[:, i, :], pr[:, i, 0:MOE])
                link(last)

            def choices():
                for i in range(TILES):
                    last = nc.vector.max_index(top_i[:, i, :], top[:, i, :], pr[:, i, 0:MOE])
                link(last)
                link(nc.vector.tensor_copy(top_f[:, :, :], top_i[:, :, :]))
                dve.wait_ge(s["consts"], 1)
                for k in range(MOE_TOP - 1):
                    last = one_hot(k)
                link(last)

            def masks():
                link(one_hot(MOE_TOP - 1))
                for k in range(1, MOE_TOP):
                    link(nc.vector.tensor_tensor(mask[:, :, :], chosen[:, :, 0, :] if k == 1 else mask[:, :, :], chosen[:, :, k, :], ALU.add))

            def earlier_tiles():
                for i in range(TILES):
                    last = nc.vector.tensor_tensor(earlier[:, i + 1, :], earlier[:, i, :], mask[:, i, :], ALU.add)
                    if i < TILES - 1:
                        link(last)
                last.then_inc(s["masked"], 1)

            def blocks_of_experts():
                dve.wait_ge(s["ranked"], 1)
                nc.vector.tensor_scalar(blocks_u[:, :], totals, float(P - 1), None, ALU.add)
                link(nc.vector.tensor_copy(slot_of[:, :, :].rearrange("p (b i) e -> p b (i e)", b=2), ranks[:, :, 0:PER_BANK * MOE]))
                dve.sem_inc(s["ranks_taken"], 1)
                link(nc.vector.tensor_scalar(blocks_u[:, :], blocks_u[:, :], 7, None, ALU.logical_shift_right))
                link(nc.vector.tensor_copy(blocks[:, 0, :], blocks_u[:, :]))
                link(nc.vector.tensor_tensor_scan(blocks[:, 1, :], ones_f[:, :], blocks[:, 0, :], 0.0, ALU.mult, ALU.add))
                link(nc.vector.tensor_scalar(blocks[:, 3, :], blocks[:, 1, :], block_no[:, 0:1], None, ALU.is_le))
                link(nc.vector.reduce_sum(be[:, 0:1], blocks[:, 3, :], AX.X))
                nc.vector.tensor_scalar(be_u[:, :], be[:, 0:1], float(MOE - 1), None, ALU.min).then_inc(s["expert_ready"], 1)
                link(nc.vector.tensor_tensor(blocks[:, 2, :], blocks[:, 1, :], blocks[:, 0, :], ALU.subtract))
                link(nc.vector.tensor_scalar(blocks[:, 2, :], blocks[:, 2, :], float(P), None, ALU.mult))

            def rows_of_tokens():
                link(nc.vector.tensor_tensor(slot_of[:, :, :], slot_of[:, :, :],
                                             blocks[:, 2, :].unsqueeze(1).to_broadcast(wide_shape), ALU.add))
                for k in range(MOE_TOP):
                    last = nc.vector.tensor_tensor(chosen[:, :, k, :], chosen[:, :, k, :], slot_of[:, :, :], ALU.mult)
                link(last)

            def rows_of_choices():
                link(nc.vector.reduce_sum(slot_f[:, :].unsqueeze(2), chosen[:, :, :, :].rearrange("p i k e -> p (i k) e"), AX.X))
                nc.vector.tensor_copy(slot_u[:, :], slot_f[:, :]).then_inc(s["slots_ready"], 1)

            def step(n):
                if n < STEPS:
                    dve.wait_ge(s["silu"], n + 1)
                    if n >= 2:
                        dve.wait_ge(s["down_done"], 2 * (n - 1))
                    nc.vector.tensor_tensor(hidden[:, n % 2, 0, :], gate[:, n % 2, 0, :], psU[:, n % 2, 1, :], ALU.mult)
                    nc.vector.tensor_tensor(hidden[0:REST, n % 2, 1, :], gate[0:REST, n % 2, 1, :], psU[64:64 + REST, n % 2, 2, :],
                                            ALU.mult).then_inc(s["h_ready"], 1)
                if n:
                    m = n - 1
                    b = m % BLKS
                    for half in range(2):
                        dve.wait_ge(s["down_done"], 2 * m + half + 1)
                        for j in range(2):
                            i = b * BLK // P + 2 * half + j
                            last = nc.vector.scalar_tensor_tensor(resid[:, i, :], psD[:, half, j * DIM:(j + 1) * DIM],
                                                                  shared_gate[:, i:i + 1], resid[:, i, :], ALU.mult, ALU.add)
                        last.then_inc(s["added"], 1)

            link(nc.vector.tensor_reduce(small[:, 0, :], routed, AX.X, ALU.max))
            nc.vector.tensor_tensor(routed, routed, small[:, 0, :].unsqueeze(2).to_broadcast(wide_shape), ALU.subtract).then_inc(s["lready"], 1)
            step(0)
            probabilities()
            step(1)
            choices()
            step(2)
            masks()
            step(MASKED)
            earlier_tiles()
            step(RANKED)
            blocks_of_experts()
            step(RANKED + 1)
            rows_of_tokens()
            step(RANKED + 2)
            rows_of_choices()
            for n in range(RANKED + 3, STEPS + 1):
                step(n)
    sc.close()

    rows_in = sb("d_rows_in", [P, SLOTS, ROWW])
    colsT = sb("d_colsT", [P, 2, CH, P])
    b_gate = sb("d_b_gate", [P, 2, 2, P])
    b_hidden = sb("d_b_hidden", [P, 2, 2, P])
    rows_out = sb("d_rows_out", [P, SLOTS, DIM])
    sc = ctx.enter_context(ExitStack())
    psX = sc.enter_context(nc.psum_tensor("d_psX", [P, 2, BLK], F32))
    psH = sc.enter_context(nc.psum_tensor("d_psH", [P, 2, BLK], F32))
    psY = sc.enter_context(nc.psum_tensor("d_psY", [P, 2, BLK], F32))
    arrived = [s[f"in{x}"] for x in range(SLOTS)]
    left = [s[f"out{x}"] for x in range(SLOTS)]
    LAST = BLOCKS // SLOTS - 1
    IN = 3 * 16
    with nc.Block() as block:
        @block.sync
        def _(sp):
            def load(n, x):
                expert = sp.value_load(block_expert[0:1, n:n + 1] if isinstance(n, int) else block_expert[0:1, bass.ds(n, 1)],
                                       min_val=0, max_val=MOE - 1)
                r = slice(n * P, (n + 1) * P) if isinstance(n, int) else bass.ds(n * P, P)
                sp.dma_start(wide[:, x, :], g["wide_d"][bass.ds(expert, 1), :, :].rearrange("e p n -> p (e n)")).then_inc(arrived[x], 16)
                sp.dma_start(rest[:, x, :], g["rest_d"][bass.ds(expert, 1), :, :].rearrange("e i d -> i (e d)")).then_inc(arrived[x], 16)
                sp.dma_start(rows_in[:, x, :], scattered_rows[r, :]).then_inc(arrived[x], 16)

            for x in range(SLOTS):
                load(x, x)
            with sp.Fori(0, LAST) as it:
                for x in range(SLOTS):
                    sp.wait_ge(left[x], (it + 1) * 16)
                    load((it + 1) * SLOTS + x, x)

        @block.gpsimd
        def _(pool):
            def send(n, x):
                pool.wait_ge(s["b_y"], n + 1)
                pool.sem_inc(s["passed"], 1)
                nc.gpsimd.indirect_dma_start(out=expert_rows,
                                             out_offset=bass.IndirectOffsetOnAxis(ap=rows_in[:, x, TAG:TAG + 1].bitcast(U32), axis=0),
                                             in_=rows_out[:, x, :], in_offset=None).then_inc(left[x], 16)

            with pool.Fori(0, LAST + 1) as it:
                for x in range(SLOTS):
                    send(it * SLOTS + x, x)
            for x in range(SLOTS):
                pool.wait_ge(left[x], 16 * (LAST + 1))

        @block.tensor
        def _(pe):
            def turn(n, x, it):
                pe.wait_ge(arrived[x], (it + 1) * IN)
                if not isinstance(n, int) or n >= 2:
                    pe.wait_ge(s["x_back"], n - 1)
                for c in range(CH):
                    last = nc.tensor.transpose(psX[:, x % 2, c * P:(c + 1) * P], rows_in[:, x, c * P:(c + 1) * P], ident[:, :])
                last.then_inc(s["x_tr"], 1)

            def up(n, x):
                pe.wait_ge(s["x_back"], n + 1)
                if not isinstance(n, int) or n >= 2:
                    pe.wait_ge(s["b_h"], n - 1)
                for k in range(3):
                    width = P if k < 2 else HIDDEN[1]
                    for c in range(CH):
                        last = nc.tensor.matmul(psH[0:width, x % 2, k * P:(k + 1) * P], w_up(x, c, k * P, width),
                                                colsT[:, x % 2, c, :], start=(c == 0), stop=(c == CH - 1))
                last.then_inc(s["b_up"], 1)

            def down(n, x):
                pe.wait_ge(s["b_h"], n + 1)
                if not isinstance(n, int) or n >= 2:
                    pe.wait_ge(s["b_y"], n - 1)
                nc.tensor.matmul(psY[:, x % 2, 0:DIM], b_hidden[:, x % 2, 0, :], wide[:, x, DOWN0:WCOLS], start=True, stop=False)
                nc.tensor.matmul(psY[:, x % 2, 0:DIM], b_hidden[0:REST, x % 2, 1, :], rest[:, x, :],
                                 start=False, stop=True).then_inc(s["b_down"], 1)

            def steps(it, first, last):
                for x in range(SLOTS):
                    n = it * SLOTS + x
                    if not (last and x == SLOTS - 1):
                        turn(n + 1, (x + 1) % SLOTS, it + (x + 1) // SLOTS)
                    up(n, x)
                    if not (first and x == 0):
                        down(n - 1, (x - 1) % SLOTS)

            turn(0, 0, 0)
            steps(0, True, False)
            with pe.Fori(1, LAST) as it:
                steps(it, False, False)
            steps(LAST, False, True)
            down(LAST * SLOTS + SLOTS - 1, SLOTS - 1)

        @block.scalar
        def _(act):
            def columns(n, x):
                act.wait_ge(s["x_tr"], n + 1)
                if not isinstance(n, int) or n >= 2:
                    act.wait_ge(s["b_up"], n - 1)
                nc.scalar.activation(colsT[:, x % 2, :, :], psX[:, x % 2, 0:DIM].rearrange("p (c t) -> p c t", c=CH),
                                     ACT.Copy).then_inc(s["x_back"], 1)

            def silu(n, x):
                act.wait_ge(s["b_up"], n + 1)
                if not isinstance(n, int) or n >= 2:
                    act.wait_ge(s["b_h"], n - 1)
                nc.scalar.activation(b_gate[:, x % 2, 0, :], psH[:, x % 2, 0:P], ACT.Silu)
                nc.scalar.activation(b_gate[0:REST, x % 2, 1, :], psH[0:REST, x % 2, 2 * P:3 * P], ACT.Silu).then_inc(s["b_silu"], 1)

            def steps(it, last):
                for x in range(SLOTS):
                    n = it * SLOTS + x
                    if not (last and x == SLOTS - 1):
                        columns(n + 1, (x + 1) % SLOTS)
                    silu(n, x)

            columns(0, 0)
            steps(0, False)
            with act.Fori(1, LAST) as it:
                steps(it, False)
            steps(LAST, True)

        @block.vector
        def _(dve):
            def gated(n, x):
                dve.wait_ge(s["b_silu"], n + 1)
                if not isinstance(n, int) or n >= 2:
                    dve.wait_ge(s["b_down"], n - 1)
                nc.vector.tensor_tensor(b_hidden[:, x % 2, 0, :], b_gate[:, x % 2, 0, :], psH[:, x % 2, P:2 * P], ALU.mult)
                nc.vector.tensor_tensor(b_hidden[0:REST, x % 2, 1, :], b_gate[0:REST, x % 2, 1, :], psH[64:64 + REST, x % 2, 2 * P:3 * P],
                                        ALU.mult).then_inc(s["b_h"], 1)

            def result(n, x, it):
                dve.wait_ge(s["b_down"], n + 1)
                if not isinstance(it, int) or it >= 1:
                    dve.wait_ge(left[x], it * 16)
                nc.vector.tensor_copy(rows_out[:, x, :], psY[:, x % 2, 0:DIM]).then_inc(s["b_y"], 1)

            def steps(it, first):
                for x in range(SLOTS):
                    n = it * SLOTS + x
                    gated(n, x)
                    if not (first and x == 0):
                        result(n - 1, (x - 1) % SLOTS, it if x else it - 1)

            steps(0, True)
            with dve.Fori(1, LAST) as it:
                steps(it, False)
            steps(LAST, False)
            result(LAST * SLOTS + SLOTS - 1, SLOTS - 1, LAST)
    sc.close()

    RING = 4
    results = g["ctxT"][:, :, :].rearrange("p c t -> p (c t)").rearrange("p (r k d) -> p r k d", r=RING, k=MOE_TOP)
    ring = [sem(f"d_ring{r}") for r in range(RING)]
    with nc.Block() as block:
        @block.sync
        def _(sp):
            by_token = expert_rows[0:MOE_TOP * TOKENS, :].rearrange("(k i p) d -> i p k d", p=P, k=MOE_TOP)
            for i in range(TILES):
                if i >= RING:
                    sp.wait_ge(s["combined"], MOE_TOP * (i - RING + 1))
                sp.dma_start(results[:, i % RING, :, :], by_token[i]).then_inc(ring[i % RING], 16)

        @block.vector
        def _(dve):
            for i in range(TILES):
                dve.wait_ge(ring[i % RING], 16 * (i // RING + 1))
                for k in range(MOE_TOP):
                    if k:
                        dve.wait_ge(s["combined"], i * MOE_TOP + k)
                    nc.vector.scalar_tensor_tensor(resid[:, i, :], results[:, i % RING, k, :], top[:, i, k:k + 1], resid[:, i, :],
                                                   ALU.mult, ALU.add).then_inc(s["combined"], 1)

        @block.scalar
        def _(act):
            for i in range(TILES):
                act.wait_ge(s["combined"], MOE_TOP * (i + 1))
                act.dma_start(g["out"][i, :, :], resid[:, i, :]).then_inc(s["stored"], 16)
            act.wait_ge(s["stored"], 16 * TILES)


def build(nc, arrays, out):
    with ExitStack() as ctx:
        def sem(name):
            return ctx.enter_context(nc.semaphore(name))

        def sb(name, shape, dtype=F32):
            return ctx.enter_context(nc.sbuf_tensor(name, shape, dtype))

        def ps(name, shape, dtype=F32):
            return ctx.enter_context(nc.psum_tensor(name, shape, dtype))

        g = dict(arrays)
        g["out"] = out
        g["resid"] = sb("resid", [P, TILES, DIM])
        g["ctxT"] = sb("ctxT", [P, CH, TOKENS])
        g["xnT"] = sb("xnT", [P, CH, TOKENS])
        g["ident"] = sb("ident", [P, P])
        g["stats"] = sb("stats", [P, TILES, 6])
        g["mv"] = sb("mv", [P, TILES, 2])
        g["work"] = sb("work", [P, 4, TILES])
        g["xn"] = sb("xn", [P, 4, DIM])
        g["buffer"] = sb("buffer", [P, 2048])
        g["sorted_x"] = nc.dram_tensor("sorted_x", (BLOCKS * P, ROWW), F32, kind="Internal").ap()
        g["sorted_y"] = nc.dram_tensor("sorted_y", (MOE_TOP * TOKENS + BLOCKS * P, DIM), F32, kind="Internal").ap()
        g["values_d"] = nc.dram_tensor("values", (DIM, TOKENS), F32, kind="Internal").ap()
        g["zeros"] = sb("zeros", [P, DIM])
        g["pad_tags"] = sb("pad_tags", [P, BLOCKS, ROWW - TAG], U32)
        for name in ("ctx_in", "ident_ready", "zeros_ready", "zeroed"):
            g[name] = sem(name)
        for stage in (stage_recurrence, stage_product_keys, stage_attention, stage_experts):
            with ExitStack() as own:
                def own_sb(name, shape, dtype=F32):
                    return own.enter_context(nc.sbuf_tensor(name, shape, dtype))

                def own_ps(name, shape, dtype=F32):
                    return own.enter_context(nc.psum_tensor(name, shape, dtype))

                stage(nc, own, sem, own_sb, own_ps, g)


def layouts(inputs):
    import numpy as np

    a = {k: np.asarray(v) for k, v in inputs.items()}
    x = np.ascontiguousarray(a["x"].reshape(TOKENS, DIM))
    ctxT = np.ascontiguousarray(a["ctx_2048"].reshape(TOKENS, DIM).T)
    w13 = a["L1_ffn_w13"]
    se = a["L1_ffn_se_gate_up_w"]

    def up_layout(gate, up):
        out = np.zeros((len(gate), UPCOLS, DIM), np.float32)
        out[:, 0:P] = gate[:, 0:P]
        out[:, P:2 * P] = up[:, 0:P]
        out[:, 2 * P:2 * P + REST] = gate[:, P:]
        out[:, 2 * P + 64:] = up[:, P:]
        return np.ascontiguousarray(out.transpose(0, 2, 1))

    c = np.ascontiguousarray

    def expert_layout(gate, up, down):
        ups = up_layout(gate, up).reshape(len(gate), CH, P, UPCOLS).transpose(0, 2, 1, 3).reshape(len(gate), P, DOWN0)
        return c(np.concatenate([ups, down[:, 0:P]], axis=2)), c(down[:, P:])

    wide, rest = expert_layout(w13[:, :INTER], w13[:, INTER:], a["L1_ffn_w2"].transpose(0, 2, 1))
    swide, srest = expert_layout(se[:SH_INTER].reshape(SHARED, INTER, DIM), se[SH_INTER:].reshape(SHARED, INTER, DIM),
                                 a["L1_ffn_se_down_w"].T.reshape(SHARED, INTER, DIM))
    return {
        "x": x, "ctxT_d": ctxT, "td": np.ascontiguousarray(a["L0_xattn_time_decay"].reshape(CH, P).T),
        "tf": np.ascontiguousarray(a["L0_xattn_time_first"].reshape(CH, P).T),
        "pk_wqT_d": c(a["L0_ffn_Wq"].T),
        "pk_keysT_d": c(a["L0_ffn_keys"].transpose(0, 2, 3, 1).reshape(PK_HEADS * 2 * PK_DK, PK_KEYS)),
        "pk_downT_d": c(a["L0_ffn_e_down"].T), "pk_up_d": c(a["L0_ffn_e_up"]),
        "wq_d": c(a["L1_xattn_Wq"]), "bq_d": c(a["L1_xattn_bq"].reshape(1, -1)),
        "wkv_d": c(a["L1_xattn_Wkv"]), "bkv_d": c(a["L1_xattn_bkv"].reshape(1, -1)),
        "bv_d": c(a["L1_xattn_bkv"][DIM:].reshape(CH, P).T),
        "wp_d": c(a["L1_xattn_Wp"]), "bp_d": c(a["L1_xattn_bp"].reshape(1, -1)),
        "gates_d": c(np.concatenate([a["L1_ffn_gate_w"], a["L1_ffn_shared_gate_w"]]).T),
        "wide_d": wide, "rest_d": rest, "swide_d": swide, "srest_d": srest,
    }


def kernel(**inputs):
    import numpy as np
    import concourse.bacc as bacc
    from concourse.bass_utils import run_bass_kernel_spmd

    arrays = layouts(inputs)
    nc = bacc.Bacc("TRN2", target_bir_lowering=False, num_devices=1)
    aps = {n: nc.dram_tensor("in_" + n, a.shape, mybir.dt.from_np(a.dtype), kind="ExternalInput").ap() for n, a in arrays.items()}
    out = nc.dram_tensor("out", (BATCH, SEQ, DIM), F32, kind="ExternalOutput").ap()
    build(nc, aps, out)
    result = run_bass_kernel_spmd(nc, [{"in_" + n: a for n, a in arrays.items()}], core_ids=[0])
    return result.results[0]["out"]
```
